# Optimizing a Trainium2 kernel written in Bass

```python
import numpy as np
import jax
import jax.numpy as jnp

def _softmax(x, axis=-1):
    return jax.nn.softmax(x, axis=axis)

def _gelu(x):
    return jax.nn.gelu(x, approximate=True)

def _silu(x):
    return jax.nn.silu(x)

def _sigmoid(x):
    return jax.nn.sigmoid(x)

def _layernorm(x, axis=-1, eps=1e-05):
    m = jnp.mean(x, axis=axis, keepdims=True)
    v = jnp.var(x, axis=axis, keepdims=True)
    return (x - m) / jnp.sqrt(v + eps)

def _scatter_add(tgt, idx, src, axis=0):
    return tgt.at[idx].add(src)

def _segment_sum(src, seg, n):
    return jax.ops.segment_sum(src, seg, n)
kernel_name = 'mk_vit_tower_d1_tok_img512_r4_a4eec8'

def setup_inputs(seed: int=0):
    np.random.seed(seed)
    _w = jnp.asarray

    def _rec_inputs():
        import jax
        import jax.numpy as jnp
        _rk = jax.random.key(seed)
        x = 7.22013e-05 + 1.00017 * jax.random.normal(jax.random.fold_in(_rk, 1), (16, 512, 64, 2), jnp.float32)
        return x
    x = _rec_inputs()

    def _L0_tok_setup():
        import jax, jax.numpy as jnp
        import numpy as np
        B, L, C = (8, 512, 64)
        D = C // 8

        def _attn(q, k, v, scale):
            scores = jnp.einsum('bld,bmd->blm', q, k) / scale
            w = jax.nn.softmax(scores, axis=-1)
            return jnp.einsum('blm,bmd->bld', w, v)
        key = jax.random.key(seed)
        ks = jax.random.split(key, 16)
        he = lambda k, cin, cout: jax.random.normal(k, (cin, cout), jnp.float32) * np.sqrt(2.0 / cin)
        inp = {'x': jax.random.normal(ks[0], (B, L, C, 2), jnp.float32)}
        dims = [D, D, C, D, D, C, D, D, C, D, D, C]
        for i, dout in enumerate(dims):
            inp[f'w{i + 1}'] = he(ks[i + 1], C, dout)
        inp['alpha'] = jnp.zeros((1,), jnp.float32)
        inp['gamma'] = jnp.zeros((1,), jnp.float32)
        return inp
    _L0_tok_all = _L0_tok_setup()
    _L0_tok_in = {k: v for k, v in _L0_tok_all.items() if k in ('w1', 'w2', 'w3', 'w4', 'w5', 'w6', 'w7', 'w8', 'w9', 'w10', 'w11', 'w12', 'alpha', 'gamma')}
    del _L0_tok_all

    def _L0_attn_setup():
        import jax, jax.numpy as jnp
        import numpy as np
        B, N, D_IN = (8, 512, 128)
        H = 256
        D_EMB = 128
        D_ATTN = 64
        key = jax.random.key(seed)
        ks = jax.random.split(key, 9)
        s = lambda fi, fo: (2.0 / (fi + fo)) ** 0.5
        return {'x': jax.random.normal(ks[0], (B, N, D_IN), dtype=jnp.float32), 'We1': jax.random.normal(ks[1], (D_IN, H), dtype=jnp.float32) * s(D_IN, H), 'be1': jnp.zeros((H,), dtype=jnp.float32), 'We2': jax.random.normal(ks[2], (H, D_EMB), dtype=jnp.float32) * s(H, D_EMB), 'be2': jnp.zeros((D_EMB,), dtype=jnp.float32), 'Wk1': jax.random.normal(ks[3], (D_IN, H), dtype=jnp.float32) * s(D_IN, H), 'bk1': jnp.zeros((H,), dtype=jnp.float32), 'Wk2': jax.random.normal(ks[4], (H, 2 * D_ATTN), dtype=jnp.float32) * s(H, 2 * D_ATTN), 'bk2': jnp.zeros((2 * D_ATTN,), dtype=jnp.float32)}
    _L0_attn_all = _L0_attn_setup()
    _L0_attn_in = {k: v for k, v in _L0_attn_all.items() if k in ('We1', 'be1', 'We2', 'be2', 'Wk1', 'bk1', 'Wk2', 'bk2')}
    del _L0_attn_all

    def _L0_ffn_setup():
        import jax, jax.numpy as jnp
        import numpy as np
        B, T, D = (4, 2048, 128)
        E, F, CAP = (8, 512, 1024)
        key = jax.random.key(seed)
        ks = jax.random.split(key, 6)
        s = 0.02
        return {'x': jax.random.normal(ks[0], (B, T, D), dtype=jnp.float32), 'Wr': jax.random.normal(ks[1], (D, E), dtype=jnp.float32) * s, 'W1': jax.random.normal(ks[2], (E, D, F), dtype=jnp.float32) * s, 'b1': jax.random.normal(ks[3], (E, F), dtype=jnp.float32) * s, 'W2': jax.random.normal(ks[4], (E, F, D), dtype=jnp.float32) * s, 'b2': jax.random.normal(ks[5], (E, D), dtype=jnp.float32) * s}
    _L0_ffn_all = _L0_ffn_setup()
    _L0_ffn_in = {k: v for k, v in _L0_ffn_all.items() if k in ('Wr', 'W1', 'b1', 'W2', 'b2')}
    del _L0_ffn_all
    return {'x': x, 'L0_tok_w1': _L0_tok_in['w1'], 'L0_tok_w2': _L0_tok_in['w2'], 'L0_tok_w3': _L0_tok_in['w3'], 'L0_tok_w4': _L0_tok_in['w4'], 'L0_tok_w5': _L0_tok_in['w5'], 'L0_tok_w6': _L0_tok_in['w6'], 'L0_tok_w7': _L0_tok_in['w7'], 'L0_tok_w8': _L0_tok_in['w8'], 'L0_tok_w9': _L0_tok_in['w9'], 'L0_tok_w10': _L0_tok_in['w10'], 'L0_tok_w11': _L0_tok_in['w11'], 'L0_tok_w12': _L0_tok_in['w12'], 'L0_tok_alpha': _L0_tok_in['alpha'], 'L0_tok_gamma': _L0_tok_in['gamma'], 'L0_attn_We1': _L0_attn_in['We1'], 'L0_attn_be1': _L0_attn_in['be1'], 'L0_attn_We2': _L0_attn_in['We2'], 'L0_attn_be2': _L0_attn_in['be2'], 'L0_attn_Wk1': _L0_attn_in['Wk1'], 'L0_attn_bk1': _L0_attn_in['bk1'], 'L0_attn_Wk2': _L0_attn_in['Wk2'], 'L0_attn_bk2': _L0_attn_in['bk2'], 'L0_ffn_Wr': _L0_ffn_in['Wr'], 'L0_ffn_W1': _L0_ffn_in['W1'], 'L0_ffn_b1': _L0_ffn_in['b1'], 'L0_ffn_W2': _L0_ffn_in['W2'], 'L0_ffn_b2': _L0_ffn_in['b2']}

def reference(x, L0_tok_w1, L0_tok_w2, L0_tok_w3, L0_tok_w4, L0_tok_w5, L0_tok_w6, L0_tok_w7, L0_tok_w8, L0_tok_w9, L0_tok_w10, L0_tok_w11, L0_tok_w12, L0_tok_alpha, L0_tok_gamma, L0_attn_We1, L0_attn_be1, L0_attn_We2, L0_attn_be2, L0_attn_Wk1, L0_attn_bk1, L0_attn_Wk2, L0_attn_bk2, L0_ffn_Wr, L0_ffn_W1, L0_ffn_b1, L0_ffn_W2, L0_ffn_b2):
    import jax
    import jax.numpy as jnp

    def _L0_tok_ref(x, w1, w2, w3, w4, w5, w6, w7, w8, w9, w10, w11, w12, alpha, gamma):
        import jax, jax.numpy as jnp
        import numpy as np
        B, L, C = (8, 512, 64)
        D = C // 8

        def _attn(q, k, v, scale):
            scores = jnp.einsum('bld,bmd->blm', q, k) / scale
            w = jax.nn.softmax(scores, axis=-1)
            return jnp.einsum('blm,bmd->bld', w, v)
        ecg = x[:, :, :, 0]
        pcg = x[:, :, :, 1]
        proj = lambda f, w: jnp.einsum('blc,cd->bld', f, w)
        scale = jnp.sqrt(jnp.asarray(D, x.dtype))
        qkv_ecg_intra = _attn(proj(ecg, w1), proj(ecg, w2), proj(ecg, w3), scale)
        qkv_ecg_inter = _attn(proj(ecg, w4), proj(pcg, w5), proj(pcg, w6), scale)
        ecg_out = qkv_ecg_inter + alpha * qkv_ecg_intra
        qkv_pcg_intra = _attn(proj(pcg, w7), proj(pcg, w8), proj(pcg, w9), scale)
        qkv_pcg_inter = _attn(proj(pcg, w10), proj(ecg, w11), proj(ecg, w12), scale)
        pcg_out = qkv_pcg_inter + gamma * qkv_pcg_intra
        return jnp.concatenate([ecg_out, pcg_out], axis=-1)

    def _L0_attn_ref(x, We1, be1, We2, be2, Wk1, bk1, Wk2, bk2):
        import jax, jax.numpy as jnp
        import numpy as np
        B, N, D_IN = (8, 512, 128)
        H = 256
        D_EMB = 128
        D_ATTN = 64
        embs = jax.nn.relu(x @ We1 + be1) @ We2 + be2
        kq = jax.nn.relu(x @ Wk1 + bk1) @ Wk2 + bk2
        K, Q = (kq[..., :D_ATTN], kq[..., D_ATTN:])
        scores = jnp.einsum('bqd,bkd->bqk', Q, K)
        A = jax.nn.softmax(scores, axis=-1)
        return jnp.einsum('bqk,bkd->bqd', A, embs)

    def _L0_ffn_ref(x, Wr, W1, b1, W2, b2):
        import jax, jax.numpy as jnp
        import numpy as np
        B, T, D = (4, 2048, 128)
        E, F, CAP = (8, 512, 1024)
        Bb, Tt, Dd = x.shape
        N = Bb * Tt
        C = min(CAP, N)
        x_flat = x.reshape(N, Dd)
        logits = x_flat @ Wr
        probs = jax.nn.softmax(logits, axis=0)
        vals, idx = jax.lax.top_k(probs.T, C)
        selected = x_flat[idx]
        h = jax.nn.gelu(jnp.einsum('ecd,edf->ecf', selected, W1) + b1[:, None, :], approximate=False)
        out_e = jnp.einsum('ecf,efd->ecd', h, W2) + b2[:, None, :]
        weighted = vals[..., None] * out_e
        output = jnp.zeros_like(x_flat).at[idx.reshape(-1)].add(weighted.reshape(-1, Dd))
        return output.reshape(Bb, Tt, Dd)
    h = _L0_tok_ref(x, L0_tok_w1, L0_tok_w2, L0_tok_w3, L0_tok_w4, L0_tok_w5, L0_tok_w6, L0_tok_w7, L0_tok_w8, L0_tok_w9, L0_tok_w10, L0_tok_w11, L0_tok_w12, L0_tok_alpha, L0_tok_gamma)
    h = h + _L0_attn_ref(_layernorm(h, axis=-1), L0_attn_We1, L0_attn_be1, L0_attn_We2, L0_attn_be2, L0_attn_Wk1, L0_attn_bk1, L0_attn_Wk2, L0_attn_bk2)
    h = h + _L0_ffn_ref(_layernorm(h, axis=-1), L0_ffn_Wr, L0_ffn_W1, L0_ffn_b1, L0_ffn_W2, L0_ffn_b2)
    return h

_drawn_inputs = setup_inputs


def setup_inputs(seed=0):
    import zlib

    import numpy as np

    out = dict(_drawn_inputs(seed))
    spreads = {'L0_attn_be1': (0.0, 0.1),
     'L0_attn_be2': (0.0, 0.1),
     'L0_attn_bk1': (0.0, 0.1),
     'L0_attn_bk2': (0.0, 0.1)}
    factors = {'L0_ffn_Wr': 64.0,
     'L0_ffn_W1': 64.0,
     'L0_ffn_b1': 64.0,
     'L0_ffn_W2': 63.372,
     'L0_ffn_b2': 64.0}
    for name, (base, spread) in spreads.items():
        noise = np.random.default_rng([zlib.crc32(name.encode()), seed]).standard_normal(out[name].shape)
        drawn = base * np.exp(spread * noise) if base else spread * noise
        out[name] = jnp.asarray(drawn.astype(out[name].dtype))
    for name, factor in factors.items():
        out[name] = (out[name] * factor).astype(out[name].dtype)
    return out
```

```python
import numpy as np
import concourse.bass as bass
from concourse import mybir
from contextlib import ExitStack

F32 = mybir.dt.float32
BF16 = mybir.dt.bfloat16
I32 = mybir.dt.int32
U32 = mybir.dt.uint32
ALU = mybir.AluOpType
ACT = mybir.ActivationFunctionType
AX = mybir.AxisListType

B, L, C = 16, 512, 64
D = C // 8
P = 128
NC = L // P
DM = 2 * C
NA = 4
HID, DA = 256, 64
E, F, CAP = 8, 512, 1024
NF = F // P
TW = DM + E
EPS = 1e-5
SC_T = float(D) ** -0.5

SLOT_ROW = [0, 8, 16, 24, 40, 48]
Q_PART = [1, 1, 2, 1, 3, 2]
K_PART = [1, 2, 1, 3, 1, 2]
MAX_ROW = 32


def constants():
    c = {}
    c["ident"] = np.eye(P, dtype=np.float32)
    cf = np.zeros((P, 5), np.float32)
    for h in range(2):
        for s, r in enumerate(SLOT_ROW):
            rows = slice(64 * h + r, 64 * h + r + D)
            cf[rows, 0] = -1.0 * (Q_PART[s] > 1)
            cf[rows, 1] = -1.0 * (Q_PART[s] > 2)
            cf[rows, 2] = -1.0 * (K_PART[s] > 1)
            cf[rows, 3] = -1.0 * (K_PART[s] > 2)
        rows = slice(64 * h + MAX_ROW, 64 * h + MAX_ROW + 3)
        cf[rows, 2] = 1.0
        cf[rows, 4] = 1.0
    c["coef"] = cf
    p = np.arange(P)
    same = (p[:, None] % E == p[None, :] % E)
    c["group"] = same.astype(np.float32)
    c["before"] = (same & (p[:, None] < p[None, :])).astype(np.float32)
    c["expert"] = (p[:, None] % E == np.arange(E)[None, :]).astype(np.float32)
    c["iota"] = np.tile(np.arange(32, dtype=np.float32), (P, 1))
    tok = (np.arange(B)[None, None, :] * L + np.arange(NC)[None, :, None] * P + p[:, None, None])
    c["token"] = tok.astype(np.float32).reshape(P, NC * B)
    return c


def build(nc, A, out, upto=9):
    lg_d = nc.dram_tensor("logits_scratch", (B, E, NC, P), F32).ap()
    tab_d = nc.dram_tensor("table_scratch", (B * L, TW), F32).ap()
    idx_d = nc.dram_tensor("index_scratch", (E, CAP), I32).ap()

    ctx = ExitStack()
    with ctx:
        own = [ctx, ctx.enter_context(ExitStack())]

        def sb(name, shape, dt=F32, keep=False):
            return own[0 if keep else 1].enter_context(nc.sbuf_tensor(name, shape, dt))

        def pb(name, shape, dt=F32):
            return ctx.enter_context(nc.psum_tensor(name, shape, dt))

        def sem(name):
            return ctx.enter_context(nc.semaphore(name))

        ident = sb("ident_sb", [P, P], keep=True)
        nmx8 = sb("nmx8", [P, E], keep=True)
        rz8 = sb("rz8", [P, E], keep=True)
        identb = sb("identb", [P, P], BF16)
        coef = sb("coef_sb", [P, 5])
        w_stack = sb("w_stack", [P, 4, P])
        w_v = sb("w_v", [P, NA * C])
        mixw = sb("mixw", [P, 2])
        w_in = sb("w_in", [P, 2 * HID])
        b_in = sb("b_in", [P, 4])
        w_kq = sb("w_kq", [P, 2, 2 * DA])
        b_kq = sb("b_kq", [DA, 2])
        w_e2 = sb("w_e2", [P, 2, DM])
        b_e2 = sb("b_e2", [P, DM])
        w_r = sb("w_r", [P, E])
        half_m = sb("half_m", [P, NC])

        x_sb = sb("x_sb", [P, NC, DM])
        xT = sb("xT", [P, L])
        part1 = sb("part1", [P, 4, L], BF16)
        rest = sb("rest", [P, 4, L])
        part2 = sb("part2", [P, 4, L], BF16)
        q_st = sb("q_st", [P, NA, L], BF16)
        k_st = sb("k_st", [P, 2, L], BF16)
        v_sb = sb("v_sb", [P, NC, NA, C + 1])
        nmax = sb("nmax", [P, NC * NA])
        nrest = sb("nrest", [P, NC * NA])
        nm_st = sb("nm_st", [P, NC * NA, 64], BF16)
        pT = sb("pT", [P, NC, NA, L])
        rden = sb("rden", [P, NC, NA])
        o_n = sb("o_n", [P, 2, NA, C])
        h_sb = sb("h_sb", [P, NC, DM])

        stats = sb("stats", [P, NC, 6])
        mv = sb("mv", [P, NC, 2])
        var = sb("var", [P, NC])
        rstd = sb("rstd", [P, NC])
        xn = sb("xn", [P, NC, DM])
        xnT = sb("xnT", [P, L])
        hid = sb("hid", [P, 4, L])
        kT = sb("kT", [P, L])
        qT = sb("qT", [P, L])
        e_sb = sb("e_sb", [P, NC, DM + 1])
        nmax2 = sb("nmax2", [P, NC])
        p2T = sb("p2T", [P, NC, L])
        rden2 = sb("rden2", [P, NC])
        h2 = sb("h2", [P, NC, DM])
        stats2 = sb("stats2", [P, NC, 6])
        mv2 = sb("mv2", [P, NC, 2])
        var2 = sb("var2", [P, NC])
        rstd2 = sb("rstd2", [P, NC])
        row = sb("row", [P, NC, TW])
        rowT = sb("rowT", [P, L])
        lg = sb("lg", [P, NC * E])
        lgT = sb("lgT", [NC * E, P])

        s_ps = [pb(f"scores{i}", [P, 2, L]) for i in range(2)]
        t_ps = [pb(f"tmisc{i}", [P, L]) for i in range(2)]
        m_ps = [pb(f"mmisc{i}", [P, L]) for i in range(2)]

        const_in = sem("const_in")
        pool_const = sem("pool_const")
        act_const = sem("act_const")
        pool_waits = sem("pool_waits")
        dve_waits = sem("dve_waits")
        sp_waits = sem("sp_waits")
        x_in = sem("x_in")
        s_full = sem("s_full")
        s_free = [sem(f"s_free{i}") for i in range(2)]
        t_full = sem("t_full")
        m_full = sem("m_full")
        xT_ok = sem("xT_ok")
        part1_ok = sem("part1_ok")
        rest_ok = sem("rest_ok")
        part2_ok = sem("part2_ok")
        stack_ok = sem("stack_ok")
        v_ok = sem("v_ok")
        tmax_ok = sem("tmax_ok")
        nm_ok = sem("nm_ok")
        qmax_ok = sem("qmax_ok")
        p_ok = sem("p_ok")
        comb_st = sem("comb_st")
        h_ok = sem("h_ok")
        ln_st = sem("ln_st")
        var_ok = sem("var_ok")
        rstd_ok = sem("rstd_ok")
        xn_ok = sem("xn_ok")
        xnT_ok = sem("xnT_ok")
        hidk_ok = sem("hidk_ok")
        hide_ok = sem("hide_ok")
        kq_ok = sem("kq_ok")
        qz_ok = sem("qz_ok")
        e_ok = sem("e_ok")
        nmax2_ok = sem("nmax2_ok")
        q2max_ok = sem("q2max_ok")
        p2_ok = sem("p2_ok")
        out2_st = sem("out2_st")
        h2_ok = sem("h2_ok")
        ln2_st = sem("ln2_st")
        var2_ok = sem("var2_ok")
        rstd2_ok = sem("rstd2_ok")
        xn2_ok = sem("xn2_ok")
        rowT_ok = sem("rowT_ok")
        lg_ok = sem("lg_ok")
        rowlg_ok = sem("rowlg_ok")
        lgT_ok = sem("lgT_ok")
        h2_out = sem("h2_out")
        row_out = sem("row_out")
        lgT_out = sem("lgT_out")

        T_USES, M_USES, S_USES = 14, 22, 16

        def t_pos(kind, t, k):
            if isinstance(t, int):
                if kind == "A":
                    pos = k if t == 0 else T_USES * t - 4 + k
                elif kind == "PV":
                    pos = T_USES * t + 16 + k - (6 if t == B - 1 else 0)
                else:
                    pos = T_USES * t + {"V": 6, "AUG": 8}[kind] + k
                return pos // 2, pos, pos % 2
            off = {"A": -4, "PV": 16, "V": 6, "AUG": 8}[kind] + k
            return t * (T_USES // 2) + off // 2, t * T_USES + off, k % 2

        def m_pos(m, k):
            return m * (M_USES // 2) + k // 2, m * M_USES + k, k % 2

        def s_pos(t, k):
            return t * (S_USES // 2) + k // 2, t * S_USES + k, k % 2

        U_XNT, U_HID, U_KT, U_QT, U_E, U_S1, U_AUG, U_S2, U_PV, U_ROWT, U_LG, U_LGT = \
            0, 1, 5, 6, 7, 8, 12, 13, 17, 19, 20, 21

        T_ONLY0 = [("P1", 0), ("P1", 1), ("P1", 2), ("P1", 3), ("AUG", 0),
                   ("P2", 0), ("P2", 1), ("P2", 2), ("P2", 3)]
        ORDER = [("P1", 0), ("M_LN1", 0), ("P1", 1), ("M_XNT", 0), ("P1", 2), ("M_HIDK", 0),
                 ("P1", 3), ("M_HIDE", 0), ("M_KQ", 0), ("AUG", 0), ("P2", 0), ("M_E", 0),
                 ("M_S1", 0), ("M_S1", 1), ("P2", 1), ("M_S1", 2), ("M_S1", 3), ("P2", 2),
                 ("M_AUG", 0), ("P2", 3), ("A_X", 0), ("M_S2", 0), ("M_S2", 1), ("A_P", 0),
                 ("A_P", 1), ("M_S2", 2), ("M_S2", 3), ("A_P", 2), ("A_P", 3), ("M_PV", 0),
                 ("M_PV", 1), ("PV", 0), ("PV", 1), ("M_ROW", 0), ("PV", 2), ("M_LG", 0),
                 ("PV", 3), ("M_LGT", 0), ("V", 0)]
        FIRST_A = [("A_X", 0), ("A_P", 0), ("A_P", 1), ("A_P", 2), ("A_P", 3)]

        def run_steps(steps, order, t):
            for name, k in order:
                if name in steps:
                    if name.startswith("M_"):
                        steps[name](t - 1, k)
                    elif name in ("A_X", "A_P", "V"):
                        steps[name](t + 1, k)
                    else:
                        steps[name](t, k)

        def run_all(eng, steps):
            run_steps(steps, FIRST_A + [("V", 0)], -1)
            run_steps(steps, [s for s in ORDER if not s[0].startswith("M_")], 0)
            with eng.Fori(1, B - 1) as i:
                run_steps(steps, ORDER, i)
            run_steps(steps, [s for s in ORDER if s[0] not in ("A_X", "A_P", "V")], B - 1)
            run_steps(steps, [s for s in ORDER if s[0].startswith("M_")], B)

        first_block = ExitStack()
        block = first_block.enter_context(nc.Block())

        N_CONST = 16 * 13

        @block.sync
        def _(sp):
            for dst, src in (
                (ident[:, :], A["ident"]), (coef[:, :], A["coef"]),
                (w_stack[:, :, :], A["w_stack"].rearrange("j p n -> p j n")),
                (w_v[:, :], A["w_v"]),
                (mixw[:, 0:1], A["alpha"].rearrange("(a n) -> a n", a=1).to_broadcast([P, 1])),
                (mixw[:, 1:2], A["gamma"].rearrange("(a n) -> a n", a=1).to_broadcast([P, 1])),
                (w_in[:, :], A["w_in"]),
                (b_in[:, :], A["b_in"].rearrange("(j p) -> p j", p=P)),
                (w_kq[:, :, :], A["w_kq"].rearrange("(j p) n -> p j n", p=P)),
                (b_kq[:, :], A["b_kq"].rearrange("(j p) -> p j", p=DA)),
                (w_e2[:, :, :], A["w_e2"].rearrange("(j p) n -> p j n", p=P)),
                (b_e2[:, :], A["b_e2"].rearrange("(a n) -> a n", a=1).to_broadcast([P, DM])),
                (w_r[:, :], A["w_r"]),
            ):
                with nc.allow_non_contiguous_dma(reason="biases, once"):
                    sp.dma_start(dst, src).then_inc(const_in, 16)

            def a_x(t, k):
                if not (isinstance(t, int) and t == 0):
                    sp.wait_ge(t_full, t_pos("A", t - 1, 1)[1] + 1)
                src = A["x"][bass.ds(t, 1), :, :].rearrange("a (c p) n -> p (a c) n", p=P)
                sp.dma_start(x_sb[:, :, :], src).then_inc(x_in, 16)

            def m_pv(m, k):
                if k == 1:
                    sp.wait_ge(h2_ok, m * NC + NC)
                    dst = out[bass.ds(m, 1), :, :].rearrange("a (c p) n -> p (a c) n", p=P)
                    sp.dma_start(dst, h2[:, :, :]).then_inc(h2_out, 16)

            def m_lgt(m, k):
                sp.wait_ge(xn2_ok, m * NC + NC)
                sp.wait_ge(rowlg_ok, m + 1)
                dst = tab_d[bass.ds(m * L, L), :].rearrange("(c p) n -> p c n", p=P)
                sp.dma_start(dst, row[:, :, :]).then_inc(row_out, 16)
                sp.wait_ge(lgT_ok, m + 1)
                dst = lg_d[bass.ds(m, 1), :, :, :].rearrange("a e c t -> (a c) e t")
                for c in range(NC):
                    sp.dma_start(lg_d[bass.ds(m, 1), :, c, :].rearrange("a e t -> (a e) t"),
                                 lgT[c * E:(c + 1) * E, :]).then_inc(lgT_out, 16)

            run_all(sp, {"A_X": a_x, "M_PV": m_pv, "M_LGT": m_lgt})
            sp.wait_ge(h2_out, 16 * B)
            sp.wait_ge(row_out, 16 * B)
            sp.wait_ge(lgT_out, 64 * B)

        @block.gpsimd
        def _(pool):
            nc.gpsimd.memset(half_m[:, :], -0.5).then_inc(pool_const, 1)
            nc.gpsimd.memset(v_sb[:, :, :, C:C + 1], 1.0).then_inc(pool_const, 1)
            nc.gpsimd.memset(e_sb[:, :, DM:DM + 1], 1.0).then_inc(pool_const, 1)
            nc.gpsimd.memset(nm_st[:, :, :], 0.0).then_inc(pool_const, 1)
            nc.gpsimd.memset(q_st[:, :, :], 0.0).then_inc(pool_const, 1)
            pool.wait_ge(pool_const, 5)
            nc.gpsimd.memset(kT[DA:P, :], 0.0).then_inc(pool_const, 1)
            nc.gpsimd.memset(qT[DA:P, :], 0.0).then_inc(pool_const, 1)
            pool.wait_ge(pool_const, 7)
            nc.gpsimd.memset(kT[DA:DA + 1, :], 1.0).then_inc(pool_const, 1)

            def own_wait():
                pool.sem_inc(pool_waits, 1)

            def a_p(t, k):
                pool.wait_ge(rest_ok, t * 4 + k + 1)
                own_wait()
                nc.gpsimd.tensor_copy(part2[:, k, :], rest[:, k, :]).then_inc(part2_ok, 1)

            def rsqrt(v, r, v_ok, r_ok, m):
                pool.wait_ge(v_ok, m + 1)
                own_wait()
                nc.gpsimd.tensor_scalar(r[:, :], v[:, :], EPS, 1.0, ALU.add, ALU.mult)\
                    .then_inc(r_ok, 1)
                pool.wait_ge(r_ok, m * 2 + 1)
                nc.gpsimd.tensor_tensor(r[:, :], r[:, :], half_m[:, :], ALU.pow).then_inc(r_ok, 1)

            def m_ln1(m, k):
                rsqrt(var, rstd, var_ok, rstd_ok, m)

            def m_kq(m, k):
                pool.wait_ge(m_full, m_pos(m, U_QT)[1])
                own_wait()
                nc.gpsimd.memset(qT[DA:DA + 1, :], 0.0).then_inc(qz_ok, 1)

            def m_row(m, k):
                rsqrt(var2, rstd2, var2_ok, rstd2_ok, m)

            run_all(pool, {"A_P": a_p, "M_LN1": m_ln1, "M_KQ": m_kq, "M_ROW": m_row})

        @block.scalar
        def _(act):
            act.wait_ge(const_in, N_CONST)
            for j in range(2):
                w = w_v[:, (2 + j) * C:(3 + j) * C]
                nc.scalar.mul(w, w, mixw[:, j:j + 1]).then_inc(act_const, 1)
            nc.scalar.copy(identb[:, :], ident[:, :]).then_inc(act_const, 1)
            act.wait_ge(pool_const, 8)
            act.wait_ge(act_const, 3)

            def a_x(t, k):
                for k in range(2):
                    _, use, bank = t_pos("A", t, k)
                    act.wait_ge(t_full, use + 1)
                    nc.scalar.copy(xT[:, k * 256:(k + 1) * 256], t_ps[bank][:, 0:256])\
                        .then_inc(xT_ok, 1)

            def a_p(t, k):
                _, use, bank = t_pos("A", t, 2 + k)
                act.wait_ge(t_full, use + 1)
                if k < 2:
                    nc.scalar.copy(part1[:, k, :], t_ps[bank][:, :]).then_inc(part1_ok, 1)
                else:
                    nc.scalar.activation(part1[:, k, :], t_ps[bank][:, :], ACT.Identity,
                                         bias=coef[:, 4:5]).then_inc(part1_ok, 1)

            def v(t, k):
                for k in range(2):
                    _, use, bank = t_pos("V", t, k)
                    act.wait_ge(t_full, use + 1)
                    src = t_ps[bank][:, :].rearrange("p (c a n) -> p c a n", c=2, a=NA)
                    for c in range(2):
                        last = nc.scalar.copy(v_sb[:, 2 * k + c, :, 0:C], src[:, c])
                        if c == 0:
                            last.then_inc(v_ok, 1)
                        else:
                            last.then_inc(v_ok, 1)

            def aug(t, k):
                for pair in range(2):
                    _, use, bank = t_pos("AUG", t, pair)
                    act.wait_ge(t_full, use + 1)
                    for h in range(2):
                        r = slice(64 * h + MAX_ROW, 64 * h + MAX_ROW + 3)
                        nc.scalar.copy(q_st[r, 2 * pair + h, :], t_ps[bank][r, :])\
                            .then_inc(qmax_ok, 1)

            def p2(t, kc):
                for pair in range(2):
                    _, use, slot = s_pos(t, 8 + 2 * kc + pair)
                    act.wait_ge(s_full, use + 1)
                    nc.scalar.activation(pT[:, kc, 2 * pair:2 * pair + 2, :], s_ps[slot][:, :, :],
                                         ACT.Exp, scale=SC_T).then_inc(p_ok, 1)

            def m_xnt(m, k):
                _, use, bank = m_pos(m, U_XNT)
                act.wait_ge(m_full, use + 1)
                nc.scalar.copy(xnT[:, :], m_ps[bank][:, :]).then_inc(xnT_ok, 1)

            def m_hidk(m, k):
                for j in range(2):
                    _, use, bank = m_pos(m, U_HID + j)
                    act.wait_ge(m_full, use + 1)
                    nc.scalar.activation(hid[:, 2 + j, :], m_ps[bank][:, :], ACT.Relu,
                                         bias=b_in[:, 2 + j:3 + j]).then_inc(hidk_ok, 1)

            def m_aug(m, k):
                _, use, bank = m_pos(m, U_AUG)
                act.wait_ge(m_full, use + 1)
                nc.scalar.copy(qT[DA:DA + 1, :], m_ps[bank][DA:DA + 1, :]).then_inc(q2max_ok, 1)

            def m_s2(m, kc):
                _, use, bank = m_pos(m, U_S2 + kc)
                act.wait_ge(m_full, use + 1)
                nc.scalar.activation(p2T[:, kc, :], m_ps[bank][:, :], ACT.Exp).then_inc(p2_ok, 1)

            def m_row(m, k):
                _, use, bank = m_pos(m, U_ROWT)
                act.wait_ge(m_full, use + 1)
                nc.scalar.copy(rowT[:, :], m_ps[bank][:, :]).then_inc(rowT_ok, 1)

            def m_lg(m, k):
                _, use, bank = m_pos(m, U_LG)
                act.wait_ge(m_full, use + 1)
                nc.scalar.copy(lg[:, :], m_ps[bank][:, 0:NC * E]).then_inc(lg_ok, 1)

            def m_lgt(m, k):
                _, use, bank = m_pos(m, U_LGT)
                act.wait_ge(m_full, use + 1)
                act.wait_ge(lgT_out, m * 64)
                nc.scalar.copy(lgT[:, :], m_ps[bank][0:NC * E, 0:P]).then_inc(lgT_ok, 1)

            run_all(act, {"A_X": a_x, "A_P": a_p, "V": v, "AUG": aug, "P2": p2, "M_XNT": m_xnt,
                          "M_HIDK": m_hidk, "M_AUG": m_aug, "M_S2": m_s2, "M_ROW": m_row,
                          "M_LG": m_lg, "M_LGT": m_lgt})

        @block.vector
        def _(dve):
            dve.wait_ge(const_in, N_CONST)
            dve.wait_ge(pool_const, 8)
            dve.wait_ge(act_const, 3)

            def a_p(t, k):
                before, use, bank = t_pos("A", t, 2 + k)
                co = 0 if k < 2 else 2
                dve.wait_ge(part1_ok, t * 4 + k + 1)
                nc.vector.scalar_tensor_tensor(
                    out=rest[:, k, :], in0=part1[:, k, :], scalar=coef[:, co:co + 1],
                    in1=t_ps[bank][:, :], op0=ALU.mult, op1=ALU.add).then_inc(rest_ok, 1)

            def a_s(t, k):
                co = 0 if k < 2 else 2
                dve.wait_ge(part2_ok, t * 4 + k + 1)
                dve.wait_ge(s_full, t * S_USES)
                if k < 2:
                    for h in range(2):
                        r = slice(64 * h, 64 * h + 64)
                        nc.vector.scalar_tensor_tensor(
                            out=q_st[r, 2 * k + h, :], in0=part2[r, k, :],
                            scalar=coef[r, co + 1:co + 2], in1=rest[r, k, :], op0=ALU.mult,
                            op1=ALU.add).then_inc(stack_ok, 1)
                else:
                    nc.vector.scalar_tensor_tensor(
                        out=k_st[:, k - 2, :], in0=part2[:, k, :], scalar=coef[:, co + 1:co + 2],
                        in1=rest[:, k, :], op0=ALU.mult, op1=ALU.add).then_inc(stack_ok, 1)

            def a_p_all(t, k):
                a_p(t, k)
                if k > 0:
                    a_s(t, k - 1)
                if k == 3:
                    a_s(t, 3)

            def p1(t, qc):
                for pair in range(2):
                    _, use, slot = s_pos(t, 2 * qc + pair)
                    dve.wait_ge(s_full, use + 1)
                    at = NA * qc + 2 * pair
                    nc.vector.tensor_reduce(nmax[:, at:at + 2], s_ps[slot][:, :, :], AX.X, ALU.max,
                                            negate=True).then_inc(s_free[slot], 1)

            def aug(t, k):
                st = t * 3
                for s in range(2):
                    dve.wait_ge(s_free[s], t * 4 + 4)
                nc.vector.tensor_copy(nm_st[:, :, MAX_ROW], nmax[:, :]).then_inc(tmax_ok, 1)
                dve.wait_ge(tmax_ok, st + 1)
                nc.vector.tensor_tensor(nrest[:, :], nmax[:, :], nm_st[:, :, MAX_ROW],
                                        ALU.subtract).then_inc(tmax_ok, 1)
                dve.wait_ge(tmax_ok, st + 2)
                nc.vector.tensor_copy(nm_st[:, :, MAX_ROW + 1], nrest[:, :]).then_inc(tmax_ok, 1)
                dve.wait_ge(tmax_ok, st + 3)
                nc.vector.tensor_tensor(nm_st[:, :, MAX_ROW + 2], nrest[:, :],
                                        nm_st[:, :, MAX_ROW + 1], ALU.subtract).then_inc(nm_ok, 1)

            def pv(t, qc):
                _, use, bank = t_pos("PV", t, qc)
                dve.wait_ge(t_full, use + 1)
                o = t_ps[bank][:, 0:NA * (C + 1)].rearrange("p (a n) -> p a n", n=C + 1)
                st = t * 3 * NC + 3 * qc
                nc.vector.reciprocal(rden[:, qc, :], o[:, :, C]).then_inc(comb_st, 1)
                dve.wait_ge(comb_st, st + 1)
                nc.vector.tensor_tensor(
                    o_n[:, qc % 2, :, :], o[:, :, 0:C],
                    rden[:, qc, :].rearrange("p (a n) -> p a n", n=1).to_broadcast([P, NA, C]),
                    ALU.mult).then_inc(comb_st, 1)
                dve.wait_ge(comb_st, st + 2)
                on = o_n[:, qc % 2, :, :].rearrange("p a n -> p (a n)")
                nc.vector.tensor_tensor(h_sb[:, qc, :], on[:, 0:DM], on[:, DM:2 * DM],
                                        ALU.add).then_inc(comb_st, 1)

            def layernorm(m, src, st_t, mv_t, var_t, st, var_sem, rstd_t, rstd_sem, outs, out_sem):
                for c in range(NC):
                    nc.vector.bn_stats(st_t[:, c, :], src[:, c, :]).then_inc(st, 1)
                for c in range(NC):
                    dve.wait_ge(st, m * 2 * NC + c + 1)
                    dve.sem_inc(dve_waits, 1)
                    nc.vector.bn_aggr(mv_t[:, c, :], st_t[:, c, :]).then_inc(st, 1)
                dve.wait_ge(st, m * 2 * NC + 2 * NC)
                nc.vector.tensor_copy(var_t[:, :], mv_t[:, :, 1]).then_inc(var_sem, 1)
                dve.wait_ge(rstd_sem, m * 2 + 2)
                for c in range(NC):
                    nc.vector.tensor_scalar(outs[:, c, 0:DM], src[:, c, :], mv_t[:, c, 0:1],
                                            rstd_t[:, c:c + 1], ALU.subtract, ALU.mult)\
                        .then_inc(out_sem, 1)

            def m_ln1(m, k):
                dve.wait_ge(comb_st, (m + 1) * 3 * NC)
                layernorm(m, h_sb, stats, mv, var, ln_st, var_ok, rstd, rstd_ok, xn, xn_ok)

            def m_hide(m, k):
                for j in range(2):
                    _, use, bank = m_pos(m, U_HID + 2 + j)
                    dve.wait_ge(m_full, use + 1)
                    nc.vector.tensor_scalar(hid[:, j, :], m_ps[bank][:, :], b_in[:, j:j + 1], 0.0,
                                            ALU.add, ALU.max).then_inc(hide_ok, 1)

            def m_kq(m, k):
                for j, (dst, u) in enumerate(((kT, U_KT), (qT, U_QT))):
                    _, use, bank = m_pos(m, u)
                    dve.wait_ge(m_full, use + 1)
                    nc.vector.tensor_scalar(dst[0:DA, :], m_ps[bank][0:DA, :], b_kq[:, j:j + 1],
                                            None, ALU.add).then_inc(kq_ok, 1)

            def m_e(m, k):
                _, use, bank = m_pos(m, U_E)
                dve.wait_ge(m_full, use + 1)
                nc.vector.tensor_tensor(
                    e_sb[:, :, 0:DM], m_ps[bank][:, :].rearrange("p (c n) -> p c n", n=DM),
                    b_e2[:, :].rearrange("p (a n) -> p a n", a=1).to_broadcast([P, NC, DM]),
                    ALU.add).then_inc(e_ok, 1)

            def m_s1(m, qc):
                _, use, bank = m_pos(m, U_S1 + qc)
                dve.wait_ge(m_full, use + 1)
                nc.vector.tensor_reduce(nmax2[:, qc:qc + 1], m_ps[bank][:, :], AX.X, ALU.max,
                                        negate=True).then_inc(nmax2_ok, 1)

            def m_pv(m, k):
                _, use, bank = m_pos(m, U_PV + k)
                dve.wait_ge(m_full, use + 1)
                o = m_ps[bank][:, 0:2 * (DM + 1)].rearrange("p (c n) -> p c n", n=DM + 1)
                nc.vector.reciprocal(rden2[:, 2 * k:2 * k + 2], o[:, :, DM]).then_inc(out2_st, 1)
                dve.wait_ge(out2_st, m * 2 + k + 1)
                if k == 0:
                    dve.wait_ge(h2_out, m * 16)
                for c in range(2):
                    at = 2 * k + c
                    nc.vector.scalar_tensor_tensor(
                        out=h2[:, at, :], in0=o[:, c, 0:DM], scalar=rden2[:, at:at + 1],
                        in1=h_sb[:, at, :], op0=ALU.mult, op1=ALU.add).then_inc(h2_ok, 1)
                if k == 1:
                    dve.wait_ge(h2_ok, m * NC + NC)
                    dve.wait_ge(row_out, m * 16)
                    layernorm(m, h2, stats2, mv2, var2, ln2_st, var2_ok, rstd2, rstd2_ok, row,
                              xn2_ok)

            def m_lg(m, k):
                _, use, bank = m_pos(m, U_LG)
                dve.wait_ge(lg_ok, m + 1)
                nc.vector.tensor_copy(row[:, :, DM:TW],
                                      lg[:, :].rearrange("p (c e) -> p c e", e=E))\
                    .then_inc(rowlg_ok, 1)

            run_all(dve, {"A_P": a_p_all, "P1": p1, "AUG": aug, "PV": pv, "M_LN1": m_ln1,
                          "M_HIDE": m_hide, "M_KQ": m_kq, "M_E": m_e, "M_S1": m_s1, "M_PV": m_pv,
                          "M_LG": m_lg})

        @block.tensor
        def _(pe):
            pe.wait_ge(const_in, N_CONST)
            pe.wait_ge(pool_const, 8)
            pe.wait_ge(act_const, 3)

            def transposes(ps, parts, n=P):
                for j, src in enumerate(parts):
                    last = nc.tensor.transpose(ps[:, j * n:(j + 1) * n], src, ident[:, :])
                return last

            def t_slot(kind, t, k):
                first = isinstance(t, int) and t == 0
                last = isinstance(t, int) and t == B - 1
                if kind == "A" and k < 2:
                    if not first:
                        pe.wait_ge(qmax_ok, t * 4 - 2 + 2 * k)
                elif kind == "A" and k < 4:
                    pe.wait_ge(xT_ok, t * 2 + k - 1)
                elif kind == "A":
                    pe.wait_ge(rest_ok, t * 4 + k - 3)
                elif kind == "PV" and k < 2 and last:
                    pe.wait_ge(qmax_ok, t * 4 + 2 + 2 * k)
                elif kind == "PV" and k < 2:
                    pe.wait_ge(rest_ok, t * 4 + 7 + k)
                elif kind == "PV":
                    pe.wait_ge(comb_st, t * 3 * NC + 3 * (k - 2) + 2)
                elif kind == "V" and first:
                    pe.wait_ge(rest_ok, 3 + k)
                elif kind == "V":
                    pe.wait_ge(comb_st, t * 3 * NC + 3 * (k + 2 - NC) + 2)
                else:
                    pe.wait_ge(v_ok, t * 4 + 2 * k + 2)
                return t_ps[t_pos(kind, t, k)[2]]

            def s_slot(t, k):
                _, use, slot = s_pos(t, k)
                if k < 8:
                    if k >= 2:
                        pe.wait_ge(s_free[slot], t * 4 + k // 2)
                    else:
                        pe.wait_ge(p_ok, t * 8 - 1 + k) if not (isinstance(t, int) and t == 0) \
                            else None
                elif k < 10:
                    pe.wait_ge(s_free[slot], t * 4 + 4)
                else:
                    pe.wait_ge(p_ok, t * 8 + k - 9)
                return s_ps[slot]

            def a_x(t, k):
                pe.wait_ge(x_in, (t + 1) * 16)
                for k in range(2):
                    ps = t_slot("A", t, k)
                    last = transposes(ps, [x_sb[:, 2 * k + j, :] for j in range(2)])
                    last.then_inc(t_full, 1)

            def a_p(t, k):
                ps = t_slot("A", t, 2 + k)
                if k == 0:
                    pe.wait_ge(xT_ok, t * 2 + 2)
                nc.tensor.matmul(ps[:, :], w_stack[:, k, :], xT[:, :], start=True, stop=True)\
                    .then_inc(t_full, 1)

            def v(t, k):
                for k in range(2):
                    ps = t_slot("V", t, k)
                    for c in range(2):
                        at = (2 * k + c) * P
                        last = nc.tensor.matmul(ps[:, c * 256:(c + 1) * 256], xT[:, at:at + P],
                                                w_v[:, :], start=True, stop=True)
                    last.then_inc(t_full, 1)

            def p1(t, qc):
                if qc == 0:
                    pe.wait_ge(stack_ok, t * 6 + 6)
                for pair in range(2):
                    ps = s_slot(t, 2 * qc + pair)
                    for h in range(2):
                        last = nc.tensor.matmul(
                            ps[:, h, :], q_st[:, 2 * pair + h, qc * P:(qc + 1) * P],
                            k_st[:, pair, :], start=True, stop=True)
                    last.then_inc(s_full, 1)

            def aug(t, k):
                pe.wait_ge(nm_ok, t + 1)
                for pair in range(2):
                    ps = t_slot("AUG", t, pair)
                    for qc in range(NC):
                        at = NA * qc + 2 * pair
                        last = nc.tensor.matmul(
                            ps[:, qc * P:(qc + 1) * P],
                            nm_st[:, at:at + 2, :].rearrange("p a n -> p (a n)"), identb[:, :],
                            start=True, stop=True)
                    last.then_inc(t_full, 1)

            def p2(t, kc):
                if kc == 0:
                    pe.wait_ge(qmax_ok, t * 4 + 4)
                for pair in range(2):
                    ps = s_slot(t, 8 + 2 * kc + pair)
                    for h in range(2):
                        last = nc.tensor.matmul(
                            ps[:, h, :], k_st[:, pair, kc * P:(kc + 1) * P],
                            q_st[:, 2 * pair + h, :], start=True, stop=True)
                    last.then_inc(s_full, 1)

            def pv(t, qc):
                if qc == 0:
                    pe.wait_ge(p_ok, t * 8 + 8)
                    pe.wait_ge(v_ok, t * 4 + 4)
                ps = t_slot("PV", t, qc)
                for a in range(NA):
                    for kc in range(NC):
                        last = nc.tensor.matmul(
                            ps[:, a * (C + 1):(a + 1) * (C + 1)],
                            pT[:, kc, a, qc * P:(qc + 1) * P], v_sb[:, kc, a, :],
                            start=kc == 0, stop=kc == NC - 1)
                last.then_inc(t_full, 1)

            def m_slot(m, k):
                _, use, bank = m_pos(m, k)
                first = isinstance(m, int) and m == 0
                prev = (k - 2) % M_USES
                mm = m - 1 if k < 2 else m
                if k < 2 and first:
                    return m_ps[bank]
                if prev == U_XNT:
                    pe.wait_ge(xnT_ok, mm + 1)
                elif U_HID <= prev < U_HID + 2:
                    pe.wait_ge(hidk_ok, mm * 2 + prev - U_HID + 1)
                elif U_HID + 2 <= prev < U_HID + 4:
                    pe.wait_ge(hide_ok, mm * 2 + prev - U_HID - 1)
                elif prev in (U_KT, U_QT):
                    pe.wait_ge(kq_ok, mm * 2 + prev - U_KT + 1)
                elif prev == U_E:
                    pe.wait_ge(e_ok, mm + 1)
                elif U_S1 <= prev < U_S1 + NC:
                    pe.wait_ge(nmax2_ok, mm * NC + prev - U_S1 + 1)
                elif prev == U_AUG:
                    pe.wait_ge(q2max_ok, mm + 1)
                elif U_S2 <= prev < U_S2 + NC:
                    pe.wait_ge(p2_ok, mm * NC + prev - U_S2 + 1)
                elif U_PV <= prev < U_PV + 2:
                    pe.wait_ge(h2_ok, mm * NC + 2 * (prev - U_PV) + 2)
                elif prev == U_ROWT:
                    pe.wait_ge(rowT_ok, mm + 1)
                elif prev == U_LG:
                    pe.wait_ge(lg_ok, mm + 1)
                else:
                    pe.wait_ge(lgT_ok, mm + 1)
                return m_ps[bank]

            def m_xnt(m, k):
                pe.wait_ge(xn_ok, m * NC + NC)
                ps = m_slot(m, U_XNT)
                transposes(ps, [xn[:, c, :] for c in range(NC)]).then_inc(m_full, 1)

            def hidden(m, j, k):
                ps = m_slot(m, k)
                nc.tensor.matmul(ps[:, :], w_in[:, j * P:(j + 1) * P], xnT[:, :],
                                 start=True, stop=True).then_inc(m_full, 1)

            def m_hidk(m, k):
                pe.wait_ge(xnT_ok, m + 1)
                for j in range(2):
                    hidden(m, 2 + j, U_HID + j)

            def m_hide(m, k):
                for j in range(2):
                    hidden(m, j, U_HID + 2 + j)

            def m_kq(m, k):
                pe.wait_ge(hidk_ok, m * 2 + 2)
                for j, u in enumerate((U_KT, U_QT)):
                    ps = m_slot(m, u)
                    for i in range(2):
                        last = nc.tensor.matmul(ps[0:DA, :], w_kq[:, i, j * DA:(j + 1) * DA],
                                                hid[:, 2 + i, :], start=i == 0, stop=i == 1)
                    last.then_inc(m_full, 1)

            def m_e(m, k):
                pe.wait_ge(hide_ok, m * 2 + 2)
                ps = m_slot(m, U_E)
                for c in range(NC):
                    for i in range(2):
                        last = nc.tensor.matmul(ps[:, c * P:(c + 1) * P],
                                                hid[:, i, c * P:(c + 1) * P], w_e2[:, i, :],
                                                start=i == 0, stop=i == 1)
                last.then_inc(m_full, 1)

            def m_s1(m, qc):
                if qc == 0:
                    pe.wait_ge(kq_ok, m * 2 + 2)
                    pe.wait_ge(qz_ok, m + 1)
                ps = m_slot(m, U_S1 + qc)
                nc.tensor.matmul(ps[:, :], qT[:, qc * P:(qc + 1) * P], kT[:, :],
                                 start=True, stop=True).then_inc(m_full, 1)

            def m_aug(m, k):
                pe.wait_ge(nmax2_ok, m * NC + NC)
                ps = m_slot(m, U_AUG)
                for qc in range(NC):
                    last = nc.tensor.matmul(ps[DA:DA + 1, qc * P:(qc + 1) * P],
                                            nmax2[:, qc:qc + 1], ident[:, :],
                                            start=True, stop=True)
                last.then_inc(m_full, 1)

            def m_s2(m, kc):
                if kc == 0:
                    pe.wait_ge(q2max_ok, m + 1)
                ps = m_slot(m, U_S2 + kc)
                nc.tensor.matmul(ps[:, :], kT[:, kc * P:(kc + 1) * P], qT[:, :],
                                 start=True, stop=True).then_inc(m_full, 1)

            def m_pv(m, k):
                if k == 0:
                    pe.wait_ge(p2_ok, m * NC + NC)
                    pe.wait_ge(e_ok, m + 1)
                ps = m_slot(m, U_PV + k)
                for c in range(2):
                    qc = 2 * k + c
                    for kc in range(NC):
                        last = nc.tensor.matmul(ps[:, c * (DM + 1):(c + 1) * (DM + 1)],
                                                p2T[:, kc, qc * P:(qc + 1) * P], e_sb[:, kc, :],
                                                start=kc == 0, stop=kc == NC - 1)
                last.then_inc(m_full, 1)

            def m_row(m, k):
                pe.wait_ge(xn2_ok, m * NC + NC)
                ps = m_slot(m, U_ROWT)
                transposes(ps, [row[:, c, 0:DM] for c in range(NC)]).then_inc(m_full, 1)

            def m_lg(m, k):
                pe.wait_ge(rowT_ok, m + 1)
                ps = m_slot(m, U_LG)
                for c in range(NC):
                    last = nc.tensor.matmul(ps[:, c * E:(c + 1) * E], rowT[:, c * P:(c + 1) * P],
                                            w_r[:, :], start=True, stop=True)
                last.then_inc(m_full, 1)

            def m_lgt(m, k):
                pe.wait_ge(lg_ok, m + 1)
                ps = m_slot(m, U_LGT)
                nc.tensor.transpose(ps[0:NC * E, 0:P], lg[:, :], ident[:, :]).then_inc(m_full, 1)

            run_all(pe, {"A_X": a_x, "A_P": a_p, "V": v, "P1": p1, "AUG": aug, "P2": p2, "PV": pv,
                         "M_XNT": m_xnt, "M_HIDK": m_hidk, "M_HIDE": m_hide, "M_KQ": m_kq,
                         "M_E": m_e, "M_S1": m_s1, "M_AUG": m_aug, "M_S2": m_s2, "M_PV": m_pv,
                         "M_ROW": m_row, "M_LG": m_lg, "M_LGT": m_lgt})
        first_block.close()

        group, before, expert, iota, token = (
            sb(n + "_sb", list(A[n].shape)) for n in ("group", "before", "expert", "iota", "token"))
        ones = sb("ones", [P, L])
        lgs = sb("lgs", [P, L])
        prob = sb("prob", [P, L])
        rmax = sb("rmax", [P, 1])
        gmax = sb("gmax", [1, E])
        nrow = sb("nrow", [1, P])
        nmx = sb("nmx", [P, 1])
        zpart = sb("zpart", [P, 1])
        zrow = sb("zrow", [P, E])
        cur = sb("cur", [P, 1], I32)
        bit = sb("bit", [P, 1], I32)
        cand = sb("cand", [P, 1], I32)
        count = sb("count", [P, 1])
        keep = sb("keep", [P, 1], U32)
        need = sb("need", [P, 1])
        above = sb("above", [P, L])
        ties = sb("ties", [P, L])
        scan = sb("scan", [P, L])
        chosen = sb("chosen", [P, L])
        place_i = sb("place_i", [P, L], I32)
        hi_i = sb("hi_i", [P, L], I32)
        lo_i = sb("lo_i", [P, L], I32)
        hi_f = sb("hi_f", [P, L])
        lo_f = sb("lo_f", [P, L])
        hiT = sb("hiT", [P, L])
        loT = sb("loT", [P, L])
        oh_hi = [pT[:, 2 * j:2 * j + 2, :, :].rearrange("p a b (c n) -> p (a b c) n", n=32)
                 for j in range(2)]
        oh_lo = [sb(f"oh_lo{j}", [P, P, 32]) for j in range(2)]
        idx_sb = sb("idx_sb", [P, 2, 32], I32)

        sel_in = sem("sel_in")
        sel_st = sem("sel_st")
        sel_pe = sem("sel_pe")
        sel_act = sem("sel_act")
        bis_st = sem("bis_st")
        bis_sum = sem("bis_sum")
        ones_ok = sem("ones_ok")
        dig_ok = sem("dig_ok")
        digT_ps = sem("digT_ps")
        hiT_ok = sem("hiT_ok")
        hot_hi = sem("hot_hi")
        hot_st = sem("hot_st")
        hot_lo = sem("hot_lo")
        hot_used = sem("hot_used")
        idx_ok = sem("idx_ok")
        idx_out = sem("idx_out")
        BITS = 30
        N_DVE1 = 5

        second_block = ExitStack()
        block = second_block.enter_context(nc.Block())

        @block.sync
        def _(sp):
            sp.dma_start(lgs[:, :], lg_d.rearrange("b e c t -> (b e) (c t)")).then_inc(sel_in, 16)
            for dst, n in ((group, "group"), (before, "before"), (expert, "expert"),
                           (iota, "iota"), (token, "token")):
                sp.dma_start(dst[:, :], A[n]).then_inc(sel_in, 16)
            sp.wait_ge(idx_ok, 8)
            for g in range(2):
                sp.dma_start(idx_d[4 * g:4 * g + 4, :].rearrange("e (h l) -> (e h) l", l=32),
                             idx_sb[:, g, :]).then_inc(idx_out, 16)
            sp.wait_ge(idx_out, 32)

        @block.gpsimd
        def _(pool):
            nc.gpsimd.memset(ones[:, :], 1.0).then_inc(ones_ok, 1)
            nc.gpsimd.memset(cur[:, :], 0).then_inc(ones_ok, 1)
            nc.gpsimd.memset(bit[:, :], 1 << (BITS - 1)).then_inc(ones_ok, 1)
            pool.wait_ge(sel_in, 16 * 6)
            for c in range(NC):
                pool.wait_ge(hot_st, c + 1)
                flat = oh_lo[c % 2][:, :, :].rearrange("p (b e) n -> p b (e n)", e=E)
                nc.gpsimd.tensor_tensor(
                    flat, flat,
                    token[:, c * B:(c + 1) * B].rearrange("p (b a) -> p b a", a=1)
                    .to_broadcast([P, B, E * 32]), ALU.mult).then_inc(hot_lo, 1)

        @block.scalar
        def _(act):
            act.wait_ge(sel_st, 5)
            nc.scalar.activation(prob[:, :], lgs[:, :], ACT.Exp, bias=nmx[:, :],
                                 accum_out=zpart[:, :]).then_inc(sel_act, 1)
            act.wait_ge(digT_ps, 1)
            nc.scalar.copy(hiT[:, :], s_ps[0][:, 0, :]).then_inc(hiT_ok, 1)

        @block.vector
        def _(dve):
            steps = [0]

            def step(instruction):
                instruction.then_inc(sel_st, 1)
                steps[0] += 1
                dve.wait_ge(sel_st, steps[0])

            dve.wait_ge(sel_in, 16 * 6)
            step(nc.vector.tensor_reduce(rmax[:, :], lgs[:, :], AX.X, ALU.max))
            dve.wait_ge(sel_pe, 1)
            step(nc.vector.tensor_reduce(
                gmax[:, :], m_ps[0][0:1, 0:P].rearrange("p (b e) -> p e b", e=E), AX.X, ALU.max))
            step(nc.vector.tensor_scalar(
                nrow[:, :].rearrange("p (b e) -> p b e", e=E),
                gmax[:, :].rearrange("p (a e) -> p a e", a=1).to_broadcast([1, B, E]), -1.0, None,
                ALU.mult))
            dve.wait_ge(sel_pe, 2)
            nc.vector.tensor_copy(nmx8[:, :], m_ps[1][:, 8:8 + E]).then_inc(sel_st, 1)
            steps[0] += 1
            step(nc.vector.tensor_copy(nmx[:, :], m_ps[1][:, 0:1]))
            dve.wait_ge(sel_act, 1)
            step(nc.vector.tensor_scalar(zrow[:, :], expert[:, :], zpart[:, 0:1], None, ALU.mult))
            dve.wait_ge(sel_pe, 3)
            step(nc.vector.reciprocal(rz8[:, :], m_ps[0][:, 16:16 + E]))

            dve.wait_ge(ones_ok, 3)
            with dve.Fori(0, BITS) as i:
                nc.vector.tensor_tensor(cand[:, :], cur[:, :], bit[:, :], ALU.bitwise_or)\
                    .then_inc(bis_st, 1)
                dve.wait_ge(bis_st, i * 5 + 1)
                nc.vector.tensor_scalar(above[:, :], prob[:, :], cand[:, :].bitcast(F32), None,
                                        ALU.is_ge, ALU.add, accum_out=count[:, :])\
                    .then_inc(bis_st, 1)
                dve.wait_ge(bis_sum, i + 1)
                nc.vector.tensor_scalar(keep[:, :], m_ps[0][:, 0:1], float(CAP), None, ALU.is_ge)\
                    .then_inc(bis_st, 1)
                dve.wait_ge(bis_st, i * 5 + 3)
                dve.sem_inc(dve_waits, 1)
                nc.vector.copy_predicated(cur[:, :], keep[:, :], cand[:, :]).then_inc(bis_st, 1)
                nc.vector.tensor_scalar(bit[:, :], bit[:, :], 1, None, ALU.logical_shift_right)\
                    .then_inc(bis_st, 1)
                dve.wait_ge(bis_st, i * 5 + 5)
                dve.sem_inc(dve_waits, 1)
            thr = cur[:, :].bitcast(F32)
            nc.vector.tensor_scalar(ties[:, :], prob[:, :], thr, None, ALU.is_equal)\
                .then_inc(sel_st, 1)
            steps[0] += 1
            step(nc.vector.tensor_scalar(above[:, :], prob[:, :], thr, None, ALU.is_gt, ALU.add,
                                         accum_out=count[:, :]))
            step(nc.vector.tensor_tensor_scan(scan[:, :], ones[:, :], ties[:, :], 0.0, ALU.mult,
                                              ALU.add))
            dve.wait_ge(sel_pe, 4)
            step(nc.vector.tensor_scalar(need[:, :], m_ps[1][:, 32:33], -1.0, float(CAP), ALU.mult,
                                         ALU.add))
            step(nc.vector.tensor_tensor(need[:, :], need[:, :], m_ps[1][:, 33:34], ALU.subtract))
            step(nc.vector.scalar_tensor_tensor(out=chosen[:, :], in0=scan[:, :],
                                                scalar=need[:, :], in1=ties[:, :], op0=ALU.is_le,
                                                op1=ALU.mult))
            step(nc.vector.tensor_tensor(chosen[:, :], chosen[:, :], above[:, :], ALU.add))
            step(nc.vector.tensor_tensor_scan(scan[:, :], ones[:, :], chosen[:, :], 0.0, ALU.mult,
                                              ALU.add))
            dve.wait_ge(sel_pe, 5)
            step(nc.vector.tensor_copy(need[:, :], m_ps[0][:, 34:35]))
            step(nc.vector.scalar_tensor_tensor(out=scan[:, :], in0=scan[:, :], scalar=need[:, :],
                                                in1=chosen[:, :], op0=ALU.add, op1=ALU.mult))
            step(nc.vector.tensor_scalar(place_i[:, :], scan[:, :], -1.0, None, ALU.add))
            step(nc.vector.tensor_scalar(hi_i[:, :], place_i[:, :], 5, None,
                                         ALU.arith_shift_right))
            step(nc.vector.tensor_scalar(lo_i[:, :], place_i[:, :], 31, None, ALU.bitwise_and))
            nc.vector.tensor_copy(hi_f[:, :], hi_i[:, :]).then_inc(dig_ok, 1)
            nc.vector.tensor_copy(lo_f[:, :], lo_i[:, :]).then_inc(dig_ok, 1)
            dve.wait_ge(digT_ps, 2)
            step(nc.vector.tensor_copy(loT[:, :], s_ps[0][:, 1, :]))
            dve.wait_ge(hiT_ok, 1)
            for c in range(NC):
                if c >= 2:
                    dve.wait_ge(hot_used, c - 1)
                for dig, hot, done in ((loT, oh_lo[c % 2][:, :, :], hot_st),
                                       (hiT, oh_hi[c % 2], hot_hi)):
                    nc.vector.tensor_tensor(
                        hot, dig[:, c * P:(c + 1) * P].rearrange("p (n a) -> p n a", a=1)
                        .to_broadcast([P, P, 32]),
                        iota[:, :].rearrange("p (a n) -> p a n", a=1).to_broadcast([P, P, 32]),
                        ALU.is_equal).then_inc(done, 1)
            dve.wait_ge(hot_used, NC)
            for g in range(2):
                for e in range(4):
                    r = slice(32 * e, 32 * e + 32)
                    nc.vector.tensor_copy(idx_sb[r, g, :], t_ps[g][r, 32 * e:32 * e + 32])\
                        .then_inc(idx_ok, 1)

        @block.tensor
        def _(pe):
            pe.wait_ge(sel_in, 16 * 6)
            pe.wait_ge(ones_ok, 3)
            pe.wait_ge(sel_st, 1)
            nc.tensor.matmul(m_ps[0][0:1, 0:P], rmax[:, :], ident[:, :], start=True, stop=True)\
                .then_inc(sel_pe, 1)
            pe.wait_ge(sel_st, 3)
            nc.tensor.matmul(m_ps[1][:, 0:1], nrow[:, :], ones[0:1, 0:1], start=True, stop=True)
            nc.tensor.matmul(m_ps[1][:, 8:8 + E], ones[0:1, 0:P], nrow[:, 0:E],
                             start=True, stop=True).then_inc(sel_pe, 1)
            pe.wait_ge(sel_st, 6)
            nc.tensor.matmul(m_ps[0][:, 16:16 + E], ones[:, 0:P], zrow[:, :],
                             start=True, stop=True).then_inc(sel_pe, 1)
            pe.wait_ge(sel_st, 7)
            with pe.Fori(0, BITS) as i:
                pe.wait_ge(bis_st, i * 5 + 2)
                nc.tensor.matmul(m_ps[0][:, 0:1], group[:, :], count[:, :], start=True, stop=True)\
                    .then_inc(bis_sum, 1)
            pe.wait_ge(sel_st, 10)
            nc.tensor.matmul(m_ps[1][:, 32:33], group[:, :], count[:, :], start=True, stop=True)
            nc.tensor.matmul(m_ps[1][:, 33:34], before[:, :], scan[:, L - 1:L],
                             start=True, stop=True).then_inc(sel_pe, 1)
            pe.wait_ge(sel_st, 15)
            nc.tensor.matmul(m_ps[0][:, 34:35], before[:, :], scan[:, L - 1:L],
                             start=True, stop=True).then_inc(sel_pe, 1)
            for j, src in enumerate((hi_f, lo_f)):
                pe.wait_ge(dig_ok, j + 1)
                for c in range(NC):
                    last = nc.tensor.transpose(s_ps[0][:, j, c * P:(c + 1) * P],
                                               src[:, c * P:(c + 1) * P], ident[:, :])
                last.then_inc(digT_ps, 1)
            for c in range(NC):
                pe.wait_ge(hot_hi, c + 1)
                pe.wait_ge(hot_lo, c + 1)
                for b in range(B):
                    for g in range(2):
                        at = slice(b * E + 4 * g, b * E + 4 * g + 4)
                        last = nc.tensor.matmul(
                            t_ps[g][:, 0:P],
                            oh_hi[c % 2][:, at, :].rearrange("p e n -> p (e n)"),
                            oh_lo[c % 2][:, at, :].rearrange("p e n -> p (e n)"),
                            start=c == 0 and b == 0, stop=c == NC - 1 and b == B - 1)
                last.then_inc(hot_used, 1)

        second_block.close()

        own.pop().close()
        own.append(ctx)
        NT = CAP // L
        idx = [sb(f"idx{s}", [P, CAP // P], I32) for s in range(2)]
        w1 = [sb(f"w1_{s}", [P, F]) for s in range(2)]
        w2 = [sb(f"w2_{s}", [P, NF, DM]) for s in range(2)]
        b1 = [sb(f"b1_{s}", [P, NF]) for s in range(2)]
        b2 = [sb(f"b2_{s}", [P, DM]) for s in range(2)]
        g_sb = [sb(f"g_sb{u}", [P, NC, TW]) for u in range(NT)]
        gT = [sb(f"gT{u}", [P, L]) for u in range(NT)]
        hT = [sb(f"hT{u}", [P, NF, L]) for u in range(NT)]
        wt = [sb(f"wt{u}", [P, NC]) for u in range(NT)]
        y = [sb(f"y{u}", [P, NC, DM]) for u in range(NT)]

        w_in_s = [sem(f"w_in{s}") for s in range(2)]
        g_in = [sem(f"g_in{u}") for u in range(NT)]
        gT_ps = sem("gT_ps")
        gT_ok = sem("gT_ok")
        f_full = sem("f_full")
        hT_ok = sem("hT_ok")
        o_full = sem("o_full")
        wl_ok = sem("wl_ok")
        we_ok = sem("we_ok")
        y_st = sem("y_st")
        y_ok = sem("y_ok")
        y_out = [sem(f"y_out{u}") for u in range(NT)]

        third_block = ExitStack()
        block = third_block.enter_context(nc.Block())

        out_rows = out.rearrange("b l n -> (b l) n")

        @block.sync
        def _(sp):
            def load(e, s, before_it):
                if before_it:
                    for u in range(NT):
                        sp.wait_ge(y_out[u], (e - 1) * NC * 16)
                        sp.sem_inc(sp_waits, 1)
                    sp.wait_ge(o_full, (e - 1) * NT)
                    sp.sem_inc(sp_waits, 1)
                with nc.allow_non_contiguous_dma(reason="small"):
                    for dst, src in (
                        (idx[s][:, :], idx_d[bass.ds(e, 1), :]
                         .rearrange("a (p j) -> p (a j)", p=P)),
                        (w1[s][:, :], A["w1"][bass.ds(e, 1), :, :].rearrange("a d f -> (a d) f")),
                        (w2[s][:, :, :], A["w2"][bass.ds(e, 1), :, :]
                         .rearrange("a (f p) d -> p (a f) d", p=P)),
                        (b1[s][:, :], A["b1"][bass.ds(e, 1), :]
                         .rearrange("a (f p) -> p (a f)", p=P)),
                        (b2[s][:, :], A["b2"][bass.ds(e, 1), :].to_broadcast([P, DM])),
                    ):
                        sp.dma_start(dst, src).then_inc(w_in_s[s], 16)

            load(0, 0, False)
            load(1, 1, False)
            with sp.Fori(1, E // 2) as i:
                load(i * 2, 0, True)
                load(i * 2 + 1, 1, True)
            for u in range(NT):
                sp.wait_ge(y_out[u], E * NC * 16)

        @block.gpsimd
        def _(pool):
            def gather(e, s, u, n_loads):
                if u == 0:
                    pool.wait_ge(w_in_s[s], n_loads)
                    pool.sem_inc(pool_waits, 1)
                for j in range(NC):
                    nc.gpsimd.indirect_dma_start(
                        out=g_sb[u][:, j, :], out_offset=None, in_=tab_d[:, :],
                        in_offset=bass.IndirectOffsetOnAxis(
                            ap=idx[s][:, u * NC + j:u * NC + j + 1], axis=0))\
                        .then_inc(g_in[u], 16)

            def scatter(e, s, u):
                pool.wait_ge(y_ok, e * NT + u + 1)
                if u == 0:
                    for v in range(NT):
                        pool.wait_ge(y_out[v], e * NC * 16)
                pool.sem_inc(pool_waits, 1)
                for j in range(NC):
                    nc.gpsimd.indirect_dma_start(
                        out=out_rows, out_offset=bass.IndirectOffsetOnAxis(
                            ap=idx[s][:, u * NC + j:u * NC + j + 1], axis=0),
                        in_=y[u][:, j, :], in_offset=None, compute_op=ALU.add)\
                        .then_inc(y_out[u], 16)

            for u in range(NT):
                gather(0, 0, u, 5 * 16)
            with pool.Fori(0, E // 2 - 1) as i:
                for s in range(2):
                    for u in range(NT):
                        scatter(i * 2 + s, s, u)
                        gather(i * 2 + s + 1, 1 - s, u, (i + 1 + s) * 5 * 16)
            for u in range(NT):
                scatter(E - 2, 0, u)
                gather(E - 1, 1, u, E // 2 * 5 * 16)
            for u in range(NT):
                scatter(E - 1, 1, u)

        @block.scalar
        def _(act):
            with act.Fori(0, E // 2) as i:
                for s in range(2):
                    e = i * 2 + s
                    for u in range(NT):
                        act.wait_ge(wl_ok, e * NT + u + 1)
                        nc.scalar.activation(wt[u][:, :], wt[u][:, :], ACT.Exp).then_inc(we_ok, 1)
                    act.wait_ge(w_in_s[s], (i + 1) * 5 * 16)
                    for u in range(NT):
                        for f in range(NF):
                            act.wait_ge(f_full, (e * NT + u) * NF + f + 1)
                            nc.scalar.activation(hT[u][:, f, :], s_ps[f // 2][:, f % 2, :],
                                                 ACT.Gelu, bias=b1[s][:, f:f + 1])\
                                .then_inc(hT_ok, 1)

        @block.vector
        def _(dve):
            def prepare(e, s, u):
                dve.wait_ge(g_in[u], (e + 1) * NC * 16)
                nc.vector.tensor_scalar(wt[u][:, :], g_sb[u][:, :, bass.ds(e + DM, 1)]
                                        .rearrange("p c a -> p (c a)"),
                                        nmx8[:, bass.ds(e, 1)], None, ALU.add).then_inc(wl_ok, 1)
                dve.wait_ge(gT_ps, e * NT + u + 1)
                nc.vector.tensor_copy(gT[u][:, :], m_ps[u][:, :]).then_inc(gT_ok, 1)

            with dve.Fori(0, E // 2) as i:
                for s in range(2):
                    e = i * 2 + s
                    for u in range(NT):
                        prepare(e, s, u)
                    for u in range(NT):
                        st = (e * NT + u) * 3
                        dve.wait_ge(w_in_s[s], (i + 1) * 5 * 16)
                        dve.wait_ge(y_out[u], e * NC * 16)
                        dve.wait_ge(we_ok, e * NT + u + 1)
                        nc.vector.tensor_scalar(wt[u][:, :], wt[u][:, :], rz8[:, bass.ds(e, 1)],
                                                None, ALU.mult).then_inc(y_st, 1)
                        dve.wait_ge(o_full, e * NT + u + 1)
                        nc.vector.tensor_tensor(
                            y[u][:, :, :],
                            t_ps[u][:, :].rearrange("p (c n) -> p c n", n=DM),
                            b2[s][:, :].rearrange("p (a n) -> p a n", a=1)
                            .to_broadcast([P, NC, DM]), ALU.add).then_inc(y_st, 1)
                        dve.wait_ge(y_st, (e * NT + u) * 2 + 2)
                        nc.vector.tensor_tensor(
                            y[u][:, :, :], y[u][:, :, :],
                            wt[u][:, :].rearrange("p (c a) -> p c a", a=1)
                            .to_broadcast([P, NC, DM]), ALU.mult).then_inc(y_ok, 1)

        @block.tensor
        def _(pe):
            with pe.Fori(0, E // 2) as i:
                for s in range(2):
                    e = i * 2 + s
                    for u in range(NT):
                        pe.wait_ge(g_in[u], (e + 1) * NC * 16)
                        for j in range(NC):
                            last = nc.tensor.transpose(m_ps[u][:, j * P:(j + 1) * P],
                                                       g_sb[u][:, j, 0:DM], ident[:, :])
                        last.then_inc(gT_ps, 1)
                    pe.wait_ge(w_in_s[s], (i + 1) * 5 * 16)
                    for u in range(NT):
                        pe.wait_ge(gT_ok, e * NT + u + 1)
                        for f in range(NF):
                            if u > 0:
                                pe.wait_ge(hT_ok, e * NT * NF + f + 1)
                            nc.tensor.matmul(s_ps[f // 2][:, f % 2, :],
                                             w1[s][:, f * P:(f + 1) * P], gT[u][:, :],
                                             start=True, stop=True).then_inc(f_full, 1)
                    for u in range(NT):
                        pe.wait_ge(hT_ok, (e * NT + u) * NF + NF)
                        pe.wait_ge(y_st, e * NT * 2)
                        for j in range(NC):
                            for f in range(NF):
                                last = nc.tensor.matmul(
                                    t_ps[u][:, j * P:(j + 1) * P],
                                    hT[u][:, f, j * P:(j + 1) * P], w2[s][:, f, :],
                                    start=f == 0, stop=f == NF - 1)
                        last.then_inc(o_full, 1)

        third_block.close()


def layout(i):
    g = {k: np.ascontiguousarray(np.asarray(v)) for k, v in i.items()}
    w = {n: g[f"L0_tok_w{n}"] for n in range(1, 13)}
    ecg, pcg = 0, 1
    q = [(4, ecg), (10, pcg), (1, ecg), (7, pcg)]
    k = [(5, pcg), (11, ecg), (2, ecg), (8, pcg)]
    v = [(6, pcg), (12, ecg), (3, ecg), (9, pcg)]
    w_stack = np.zeros((4, DM, P), np.float32)
    w_v = np.zeros((DM, NA * C), np.float32)
    for a in range(NA):
        for r in SLOT_ROW:
            at = 64 * (a % 2) + r
            w_stack[a // 2, q[a][1]::2, at:at + D] = w[q[a][0]]
            w_stack[2 + a // 2, k[a][1]::2, at:at + D] = w[k[a][0]]
        w_v[v[a][1]::2, a * C:(a + 1) * C] = w[v[a][0]]
    d = {"x": g["x"].reshape(B, L, DM), "w_stack": w_stack, "w_v": w_v,
         "alpha": g["L0_tok_alpha"], "gamma": g["L0_tok_gamma"],
         "w_in": np.concatenate([g["L0_attn_We1"], g["L0_attn_Wk1"]], 1),
         "b_in": np.concatenate([g["L0_attn_be1"], g["L0_attn_bk1"]]),
         "w_kq": g["L0_attn_Wk2"], "b_kq": g["L0_attn_bk2"],
         "w_e2": g["L0_attn_We2"], "b_e2": g["L0_attn_be2"], "w_r": g["L0_ffn_Wr"],
         "w1": g["L0_ffn_W1"], "b1": g["L0_ffn_b1"], "w2": g["L0_ffn_W2"], "b2": g["L0_ffn_b2"]}
    d.update(constants())
    return {n: np.ascontiguousarray(a) for n, a in d.items()}


def kernel(**inputs):
    import concourse.bacc as bacc
    from concourse.bass_utils import run_bass_kernel_spmd

    arrays = layout(inputs)
    nc = bacc.Bacc("TRN2", target_bir_lowering=False, num_devices=1)
    aps = {n: nc.dram_tensor("in_" + n, a.shape, mybir.dt.from_np(a.dtype), kind="ExternalInput").ap()
           for n, a in arrays.items()}
    out = nc.dram_tensor("out", (B, L, DM), F32, kind="ExternalOutput").ap()
    build(nc, aps, out)
    r = run_bass_kernel_spmd(nc, [{"in_" + n: a for n, a in arrays.items()}], core_ids=[0])
    return r.results[0]["out"]
```

```python
import numpy as np
import concourse.bass as bass
from concourse import mybir
from contextlib import ExitStack

F32 = mybir.dt.float32
BF16 = mybir.dt.bfloat16
I32 = mybir.dt.int32
U32 = mybir.dt.uint32
ALU = mybir.AluOpType
ACT = mybir.ActivationFunctionType
AX = mybir.AxisListType

B, L, C = 16, 512, 64
D = C // 8
P = 128
NC = L // P
DM = 2 * C
NA = 4
HID, DA = 256, 64
E, F, CAP = 8, 512, 1024
NF = F // P
TW = DM + E
EPS = 1e-5
SC_T = float(D) ** -0.5

SLOT_ROW = [0, 8, 16, 24, 40, 48]
Q_PART = [1, 1, 2, 1, 3, 2]
K_PART = [1, 2, 1, 3, 1, 2]
MAX_ROW = 32


def constants():
    c = {}
    c["ident"] = np.eye(P, dtype=np.float32)
    cf = np.zeros((P, 5), np.float32)
    for h in range(2):
        for s, r in enumerate(SLOT_ROW):
            rows = slice(64 * h + r, 64 * h + r + D)
            cf[rows, 0] = -1.0 * (Q_PART[s] > 1)
            cf[rows, 1] = -1.0 * (Q_PART[s] > 2)
            cf[rows, 2] = -1.0 * (K_PART[s] > 1)
            cf[rows, 3] = -1.0 * (K_PART[s] > 2)
        rows = slice(64 * h + MAX_ROW, 64 * h + MAX_ROW + 3)
        cf[rows, 2] = 1.0
        cf[rows, 4] = 1.0
    c["coef"] = cf
    p = np.arange(P)
    same = (p[:, None] % E == p[None, :] % E)
    c["group"] = same.astype(np.float32)
    c["before"] = (same & (p[:, None] < p[None, :])).astype(np.float32)
    c["expert"] = (p[:, None] % E == np.arange(E)[None, :]).astype(np.float32)
    c["iota"] = np.tile(np.arange(32, dtype=np.float32), (P, 1))
    tok = (np.arange(B)[None, None, :] * L + np.arange(NC)[None, :, None] * P + p[:, None, None])
    c["token"] = tok.astype(np.float32).reshape(P, NC * B)
    return c


def build(nc, A, out, upto=9):
    lg_d = nc.dram_tensor("logits_scratch", (B, E, L), F32).ap()
    tab_d = nc.dram_tensor("table_scratch", (B * L, TW), F32).ap()
    idx_d = nc.dram_tensor("index_scratch", (E, CAP), I32).ap()

    ctx = ExitStack()
    with ctx:
        own = [ctx, ctx.enter_context(ExitStack())]

        def sb(name, shape, dt=F32, keep=False):
            return own[0 if keep else 1].enter_context(nc.sbuf_tensor(name, shape, dt))

        def pb(name, shape, dt=F32):
            return ctx.enter_context(nc.psum_tensor(name, shape, dt))

        def sem(name):
            return ctx.enter_context(nc.semaphore(name))

        ident = sb("ident_sb", [P, P], keep=True)
        nmx8 = sb("nmx8", [P, E], keep=True)
        rz8 = sb("rz8", [P, E], keep=True)
        w1 = [sb(f"w1_{s}", [P, F], keep=True) for s in range(2)]
        w2 = [sb(f"w2_{s}", [P, NF, DM], keep=True) for s in range(2)]
        b1 = [sb(f"b1_{s}", [P, NF], keep=True) for s in range(2)]
        b2 = [sb(f"b2_{s}", [P, DM], keep=True) for s in range(2)]
        identb = sb("identb", [P, P], BF16)
        coef = sb("coef_sb", [P, 5])
        w_stack = sb("w_stack", [P, 4, P])
        w_v = sb("w_v", [P, NA * C])
        mixw = sb("mixw", [P, 2])
        w_in = sb("w_in", [P, 2 * HID])
        b_in = sb("b_in", [P, 4])
        w_kq = sb("w_kq", [P, 2, 2 * DA])
        b_kq = sb("b_kq", [P, 1])
        w_e2 = sb("w_e2", [P, 2, DM])
        b_e2 = sb("b_e2", [P, DM])
        w_r = sb("w_r", [P, E])
        half_m = sb("half_m", [P, NC])

        x_sb = sb("x_sb", [P, NC, DM])
        xT = sb("xT", [P, L])
        part1 = sb("part1", [P, 4, L], BF16)
        rest = sb("rest", [P, 4, L])
        part2 = sb("part2", [P, 4, L], BF16)
        q_st = sb("q_st", [P, NA, L], BF16)
        k_st = sb("k_st", [P, 2, L], BF16)
        v_sb = sb("v_sb", [P, NC, NA, P])
        nmax = sb("nmax", [P, NC * NA])
        nrest = sb("nrest", [P, NC * NA])
        nm_st = sb("nm_st", [P, NC * NA, 64], BF16)
        pT = sb("pT", [P, NC, NA, L])
        rden = sb("rden", [P, NC, NA])
        o_n = sb("o_n", [P, 2, NA, C])
        h_sb = sb("h_sb", [P, NC, DM])

        stats = sb("stats", [P, NC, 6])
        mv = sb("mv", [P, NC, 2])
        var = sb("var", [P, NC])
        rstd = sb("rstd", [P, NC])
        xn = sb("xn", [P, NC, DM])
        xnT = sb("xnT", [P, L])
        hid = sb("hid", [P, 4, L])
        kT = sb("kT", [P, L])
        qT = sb("qT", [P, L])
        e_sb = sb("e_sb", [P, NC, DM + 1])
        nmax2 = sb("nmax2", [P, NC])
        p2T = sb("p2T", [P, NC, L])
        rden2 = sb("rden2", [P, NC])
        h2 = sb("h2", [P, NC, DM])
        stats2 = sb("stats2", [P, NC, 6])
        mv2 = sb("mv2", [P, NC, 2])
        var2 = sb("var2", [P, NC])
        rstd2 = sb("rstd2", [P, NC])
        row = sb("row", [P, NC, TW])
        rowT = sb("rowT", [P, L])
        lgT = sb("lgT", [E, L])

        s_ps = [pb(f"scores{i}", [P, 2, L]) for i in range(2)]
        t_ps = [pb(f"tmisc{i}", [P, L]) for i in range(2)]
        m_ps = [pb(f"mmisc{i}", [P, L]) for i in range(2)]

        const_in = sem("const_in")
        pool_const = sem("pool_const")
        act_const = sem("act_const")
        pool_waits = sem("pool_waits")
        dve_waits = sem("dve_waits")
        sp_waits = sem("sp_waits")
        pe_waits = sem("pe_waits")
        x_in = sem("x_in")
        s_full = sem("s_full")
        s_free = [sem(f"s_free{i}") for i in range(2)]
        t_full = sem("t_full")
        m_full = sem("m_full")
        xT_ok = sem("xT_ok")
        part1_ok = sem("part1_ok")
        rest_ok = sem("rest_ok")
        part2_ok = sem("part2_ok")
        stack_ok = sem("stack_ok")
        v_ok = sem("v_ok")
        tmax_ok = sem("tmax_ok")
        nm_ok = sem("nm_ok")
        qmax_ok = sem("qmax_ok")
        p_ok = sem("p_ok")
        comb_st = sem("comb_st")
        h_ok = sem("h_ok")
        ln_st = sem("ln_st")
        var_ok = sem("var_ok")
        rstd_ok = sem("rstd_ok")
        xn_ok = sem("xn_ok")
        xnT_ok = sem("xnT_ok")
        hidk_ok = sem("hidk_ok")
        hide_ok = sem("hide_ok")
        kq_ok = sem("kq_ok")
        qz_ok = sem("qz_ok")
        e_ok = sem("e_ok")
        nmax2_ok = sem("nmax2_ok")
        q2max_ok = sem("q2max_ok")
        p2_ok = sem("p2_ok")
        out2_st = sem("out2_st")
        h2_ok = sem("h2_ok")
        ln2_st = sem("ln2_st")
        var2_ok = sem("var2_ok")
        rstd2_ok = sem("rstd2_ok")
        xn2_ok = sem("xn2_ok")
        rowT_ok = sem("rowT_ok")
        rowlg_ok = sem("rowlg_ok")
        lgT_ok = sem("lgT_ok")
        h2_out = sem("h2_out")
        row_out = sem("row_out")
        lgT_out = sem("lgT_out")

        H2_OUT, ROW_OUT, LGT_OUT, LG_OK = 16, 16, 16, 1

        T_USES, M_USES, S_USES = 14, 22, 16

        def t_pos(kind, t, k):
            if isinstance(t, int):
                if kind == "A":
                    pos = k if t == 0 else T_USES * t - 4 + k
                elif kind == "PV":
                    pos = T_USES * t + 16 + k - (6 if t == B - 1 else 0)
                else:
                    pos = T_USES * t + {"V": 6, "AUG": 8}[kind] + k
                return pos // 2, pos, pos % 2
            off = {"A": -4, "PV": 16, "V": 6, "AUG": 8}[kind] + k
            return t * (T_USES // 2) + off // 2, t * T_USES + off, k % 2

        def m_pos(m, k):
            return m * (M_USES // 2) + k // 2, m * M_USES + k, k % 2

        def s_pos(t, k):
            return t * (S_USES // 2) + k // 2, t * S_USES + k, k % 2

        U_XNT, U_HID, U_KQ, U_E, U_S1, U_AUG, U_S2, U_PV, U_ROWT, U_LG, U_LGT = \
            0, 1, 5, 6, 8, 12, 13, 17, 19, 20, 21

        T_ONLY0 = [("P1", 0), ("P1", 1), ("P1", 2), ("P1", 3), ("AUG", 0),
                   ("P2", 0), ("P2", 1), ("P2", 2), ("P2", 3)]
        ORDER = [("P1", 0), ("M_LN1", 0), ("P1", 1), ("M_XNT", 0), ("P1", 2), ("M_HIDK", 0),
                 ("P1", 3), ("M_HIDE", 0), ("M_KQ", 0), ("AUG", 0), ("P2", 0), ("M_E", 0),
                 ("M_S1", 0), ("M_S1", 1), ("P2", 1), ("M_S1", 2), ("M_S1", 3), ("P2", 2),
                 ("M_AUG", 0), ("P2", 3), ("A_X", 0), ("M_S2", 0), ("M_S2", 1), ("A_P", 0),
                 ("A_P", 1), ("M_S2", 2), ("M_S2", 3), ("A_P", 2), ("A_P", 3), ("M_PV", 0),
                 ("M_PV", 1), ("PV", 0), ("PV", 1), ("M_ROW", 0), ("PV", 2), ("M_LG", 0),
                 ("PV", 3), ("M_LGT", 0), ("V", 0)]
        FIRST_A = [("A_X", 0), ("A_P", 0), ("A_P", 1), ("A_P", 2), ("A_P", 3)]

        def run_steps(steps, order, t):
            for name, k in order:
                if name in steps:
                    if name.startswith("M_"):
                        steps[name](t - 1, k)
                    elif name in ("A_X", "A_P", "V"):
                        steps[name](t + 1, k)
                    else:
                        steps[name](t, k)

        def run_all(eng, steps):
            run_steps(steps, FIRST_A + [("V", 0)], -1)
            run_steps(steps, [s for s in ORDER if not s[0].startswith("M_")], 0)
            with eng.Fori(1, B - 1) as i:
                run_steps(steps, ORDER, i)
            run_steps(steps, [s for s in ORDER if s[0] not in ("A_X", "A_P", "V")], B - 1)
            run_steps(steps, [s for s in ORDER if s[0].startswith("M_")], B)

        first_block = ExitStack()
        block = first_block.enter_context(nc.Block())

        N_CONST = 16 * 13

        @block.sync
        def _(sp):
            for dst, src in (
                (ident[:, :], A["ident"]), (coef[:, :], A["coef"]),
                (w_stack[:, :, :], A["w_stack"].rearrange("j p n -> p j n")),
                (w_v[:, :], A["w_v"]),
                (mixw[:, 0:1], A["alpha"].rearrange("(a n) -> a n", a=1).to_broadcast([P, 1])),
                (mixw[:, 1:2], A["gamma"].rearrange("(a n) -> a n", a=1).to_broadcast([P, 1])),
                (w_in[:, :], A["w_in"]),
                (b_in[:, :], A["b_in"].rearrange("(j p) -> p j", p=P)),
                (w_kq[:, :, :], A["w_kq"].rearrange("(j p) n -> p j n", p=P)),
                (b_kq[:, :], A["b_kq"].rearrange("(p a) -> p a", a=1)),
                (w_e2[:, :, :], A["w_e2"].rearrange("(j p) n -> p j n", p=P)),
                (b_e2[:, :], A["b_e2"].rearrange("(a n) -> a n", a=1).to_broadcast([P, DM])),
                (w_r[:, :], A["w_r"]),
            ):
                with nc.allow_non_contiguous_dma(reason="biases, once"):
                    sp.dma_start(dst, src).then_inc(const_in, 16)

            sp.sem_inc(h2_out, H2_OUT)
            sp.sem_inc(row_out, ROW_OUT)
            sp.sem_inc(lgT_out, LGT_OUT)

            def a_x(t, k):
                if not (isinstance(t, int) and t == 0):
                    sp.wait_ge(t_full, t_pos("A", t - 1, 1)[1] + 1)
                src = A["x"][bass.ds(t, 1), :, :].rearrange("a (c p) n -> p (a c) n", p=P)
                sp.dma_start(x_sb[:, :, :], src).then_inc(x_in, 16)

            def m_pv(m, k):
                if k == 1:
                    sp.wait_ge(h2_ok, m * NC + NC)
                    dst = out[bass.ds(m, 1), :, :].rearrange("a (c p) n -> p (a c) n", p=P)
                    sp.dma_start(dst, h2[:, :, :]).then_inc(h2_out, 16)

            def m_lgt(m, k):
                sp.wait_ge(xn2_ok, m * NC + NC)
                sp.wait_ge(rowlg_ok, m + 1 + LG_OK)
                dst = tab_d[bass.ds(m * L, L), :].rearrange("(c p) n -> p c n", p=P)
                sp.dma_start(dst, row[:, :, :]).then_inc(row_out, 16)
                sp.wait_ge(lgT_ok, m + 1 + LG_OK)
                sp.dma_start(lg_d[bass.ds(m, 1), :, :].rearrange("a e t -> (a e) t"), lgT[:, :])\
                    .then_inc(lgT_out, 16)

            run_all(sp, {"A_X": a_x, "M_PV": m_pv, "M_LGT": m_lgt})
            sp.wait_ge(h2_out, 16 * B + H2_OUT)
            sp.wait_ge(row_out, 16 * B + ROW_OUT)
            sp.wait_ge(lgT_out, 16 * B + LGT_OUT)

        @block.gpsimd
        def _(pool):
            nc.gpsimd.memset(half_m[:, :], -0.5).then_inc(pool_const, 1)
            nc.gpsimd.memset(v_sb[:, :, :, C:C + 1], 1.0).then_inc(pool_const, 1)
            nc.gpsimd.memset(v_sb[:, :, :, C + 1:P], 0.0).then_inc(pool_const, 1)
            nc.gpsimd.memset(e_sb[:, :, DM:DM + 1], 1.0).then_inc(pool_const, 1)
            nc.gpsimd.memset(nm_st[:, :, :], 0.0).then_inc(pool_const, 1)
            nc.gpsimd.memset(q_st[:, :, :], 0.0).then_inc(pool_const, 1)
            pool.wait_ge(pool_const, 6)
            nc.gpsimd.memset(kT[DA:P, :], 0.0).then_inc(pool_const, 1)
            nc.gpsimd.memset(qT[DA:P, :], 0.0).then_inc(pool_const, 1)
            pool.wait_ge(pool_const, 8)
            nc.gpsimd.memset(kT[DA:DA + 1, :], 1.0).then_inc(pool_const, 1)

            def own_wait():
                pool.sem_inc(pool_waits, 1)

            def rsqrt(v, r, v_ok, r_ok, m):
                pool.wait_ge(v_ok, m + 1)
                own_wait()
                nc.gpsimd.tensor_scalar(r[:, :], v[:, :], EPS, 1.0, ALU.add, ALU.mult)\
                    .then_inc(r_ok, 1)
                pool.wait_ge(r_ok, m * 2 + 1)
                nc.gpsimd.tensor_tensor(r[:, :], r[:, :], half_m[:, :], ALU.pow).then_inc(r_ok, 1)

            def m_ln1(m, k):
                rsqrt(var, rstd, var_ok, rstd_ok, m)

            def m_kq(m, k):
                pool.wait_ge(m_full, m_pos(m, U_KQ)[1])
                own_wait()
                nc.gpsimd.memset(qT[DA:DA + 1, :], 0.0).then_inc(qz_ok, 1)

            def m_row(m, k):
                rsqrt(var2, rstd2, var2_ok, rstd2_ok, m)

            run_all(pool, {"M_LN1": m_ln1, "M_KQ": m_kq, "M_ROW": m_row})

        @block.scalar
        def _(act):
            act.sem_inc(lgT_ok, LG_OK)
            act.wait_ge(const_in, N_CONST)
            for j in range(2):
                w = w_v[:, (2 + j) * C:(3 + j) * C]
                nc.scalar.mul(w, w, mixw[:, j:j + 1]).then_inc(act_const, 1)
            nc.scalar.copy(identb[:, :], ident[:, :]).then_inc(act_const, 1)
            act.wait_ge(pool_const, 9)
            act.wait_ge(act_const, 3)

            def a_x(t, k):
                for k in range(2):
                    _, use, bank = t_pos("A", t, k)
                    act.wait_ge(t_full, use + 1)
                    nc.scalar.copy(xT[:, k * 256:(k + 1) * 256], t_ps[bank][:, 0:256])\
                        .then_inc(xT_ok, 1)

            def a_p(t, k):
                _, use, bank = t_pos("A", t, 2 + k)
                act.wait_ge(t_full, use + 1)
                if k < 2:
                    nc.scalar.copy(part1[:, k, :], t_ps[bank][:, :]).then_inc(part1_ok, 1)
                else:
                    nc.scalar.activation(part1[:, k, :], t_ps[bank][:, :], ACT.Identity,
                                         bias=coef[:, 4:5]).then_inc(part1_ok, 1)

            def a_r(t, k):
                act.wait_ge(rest_ok, t * 4 + k + 1)
                nc.scalar.copy(part2[:, k, :], rest[:, k, :]).then_inc(part2_ok, 1)

            def a_all(t, k):
                a_p(t, k)
                if k > 0:
                    a_r(t, k - 1)
                if k == 3:
                    a_r(t, 3)

            def v(t, k):
                for k in range(2):
                    _, use, bank = t_pos("V", t, k)
                    act.wait_ge(t_full, use + 1)
                    src = t_ps[bank][:, :].rearrange("p (c a n) -> p c a n", c=2, a=NA)
                    for c in range(2):
                        last = nc.scalar.copy(v_sb[:, 2 * k + c, :, 0:C], src[:, c])
                        if c == 0:
                            last.then_inc(v_ok, 1)
                        else:
                            last.then_inc(v_ok, 1)

            def aug(t, k):
                for pair in range(2):
                    _, use, bank = t_pos("AUG", t, pair)
                    act.wait_ge(t_full, use + 1)
                    for h in range(2):
                        r = slice(64 * h + MAX_ROW, 64 * h + MAX_ROW + 3)
                        nc.scalar.copy(q_st[r, 2 * pair + h, :], t_ps[bank][r, :])\
                            .then_inc(qmax_ok, 1)

            def p2(t, kc):
                for pair in range(2):
                    _, use, slot = s_pos(t, 8 + 2 * kc + pair)
                    act.wait_ge(s_full, use + 1)
                    nc.scalar.activation(pT[:, kc, 2 * pair:2 * pair + 2, :], s_ps[slot][:, :, :],
                                         ACT.Exp, scale=SC_T).then_inc(p_ok, 1)

            def m_xnt(m, k):
                _, use, bank = m_pos(m, U_XNT)
                act.wait_ge(m_full, use + 1)
                nc.scalar.copy(xnT[:, :], m_ps[bank][:, :]).then_inc(xnT_ok, 1)

            def m_hidk(m, k):
                for j in range(2):
                    _, use, bank = m_pos(m, U_HID + j)
                    act.wait_ge(m_full, use + 1)
                    nc.scalar.activation(hid[:, 2 + j, :], m_ps[bank][:, :], ACT.Relu,
                                         bias=b_in[:, 2 + j:3 + j]).then_inc(hidk_ok, 1)

            def m_aug(m, k):
                _, use, bank = m_pos(m, U_AUG)
                act.wait_ge(m_full, use + 1)
                nc.scalar.copy(qT[DA:DA + 1, :], m_ps[bank][DA:DA + 1, :]).then_inc(q2max_ok, 1)

            def m_s2(m, kc):
                _, use, bank = m_pos(m, U_S2 + kc)
                act.wait_ge(m_full, use + 1)
                nc.scalar.activation(p2T[:, kc, :], m_ps[bank][:, :], ACT.Exp).then_inc(p2_ok, 1)

            def m_row(m, k):
                _, use, bank = m_pos(m, U_ROWT)
                act.wait_ge(m_full, use + 1)
                nc.scalar.copy(rowT[:, :], m_ps[bank][:, :]).then_inc(rowT_ok, 1)

            def m_lg(m, k):
                _, use, bank = m_pos(m, U_LG)
                act.wait_ge(m_full, use + 1)
                act.wait_ge(lgT_out, m * 16 + LGT_OUT)
                nc.scalar.copy(lgT[:, :], m_ps[bank][0:E, :]).then_inc(lgT_ok, 1)

            run_all(act, {"A_X": a_x, "A_P": a_all, "V": v, "AUG": aug, "P2": p2, "M_XNT": m_xnt,
                          "M_HIDK": m_hidk, "M_AUG": m_aug, "M_S2": m_s2, "M_ROW": m_row,
                          "M_LG": m_lg})

        @block.vector
        def _(dve):
            dve.sem_inc(rowlg_ok, LG_OK)
            dve.wait_ge(const_in, N_CONST)
            dve.wait_ge(pool_const, 9)
            dve.wait_ge(act_const, 3)

            def a_p(t, k):
                before, use, bank = t_pos("A", t, 2 + k)
                co = 0 if k < 2 else 2
                dve.wait_ge(part1_ok, t * 4 + k + 1)
                nc.vector.scalar_tensor_tensor(
                    out=rest[:, k, :], in0=part1[:, k, :], scalar=coef[:, co:co + 1],
                    in1=t_ps[bank][:, :], op0=ALU.mult, op1=ALU.add).then_inc(rest_ok, 1)

            def a_s(t, k):
                co = 0 if k < 2 else 2
                dve.wait_ge(part2_ok, t * 4 + k + 1)
                dve.wait_ge(s_full, t * S_USES)
                if k < 2:
                    for h in range(2):
                        r = slice(64 * h, 64 * h + 64)
                        nc.vector.scalar_tensor_tensor(
                            out=q_st[r, 2 * k + h, :], in0=part2[r, k, :],
                            scalar=coef[r, co + 1:co + 2], in1=rest[r, k, :], op0=ALU.mult,
                            op1=ALU.add).then_inc(stack_ok, 1)
                else:
                    nc.vector.scalar_tensor_tensor(
                        out=k_st[:, k - 2, :], in0=part2[:, k, :], scalar=coef[:, co + 1:co + 2],
                        in1=rest[:, k, :], op0=ALU.mult, op1=ALU.add).then_inc(stack_ok, 1)

            def a_p_all(t, k):
                a_p(t, k)
                if k > 0:
                    a_s(t, k - 1)
                if k == 3:
                    a_s(t, 3)

            def p1(t, qc):
                for pair in range(2):
                    _, use, slot = s_pos(t, 2 * qc + pair)
                    dve.wait_ge(s_full, use + 1)
                    at = NA * qc + 2 * pair
                    nc.vector.tensor_reduce(nmax[:, at:at + 2], s_ps[slot][:, :, :], AX.X, ALU.max,
                                            negate=True).then_inc(s_free[slot], 1)

            def aug(t, k):
                st = t * 3
                for s in range(2):
                    dve.wait_ge(s_free[s], t * 4 + 4)
                nc.vector.tensor_copy(nm_st[:, :, MAX_ROW], nmax[:, :]).then_inc(tmax_ok, 1)
                dve.wait_ge(tmax_ok, st + 1)
                nc.vector.tensor_tensor(nrest[:, :], nmax[:, :], nm_st[:, :, MAX_ROW],
                                        ALU.subtract).then_inc(tmax_ok, 1)
                dve.wait_ge(tmax_ok, st + 2)
                nc.vector.tensor_copy(nm_st[:, :, MAX_ROW + 1], nrest[:, :]).then_inc(tmax_ok, 1)
                dve.wait_ge(tmax_ok, st + 3)
                nc.vector.tensor_tensor(nm_st[:, :, MAX_ROW + 2], nrest[:, :],
                                        nm_st[:, :, MAX_ROW + 1], ALU.subtract).then_inc(nm_ok, 1)

            def pv(t, qc):
                _, use, bank = t_pos("PV", t, qc)
                dve.wait_ge(t_full, use + 1)
                o = t_ps[bank][:, :].rearrange("p (a n) -> p a n", a=NA)
                st = t * 3 * NC + 3 * qc
                nc.vector.reciprocal(rden[:, qc, :], o[:, :, C]).then_inc(comb_st, 1)
                dve.wait_ge(comb_st, st + 1)
                nc.vector.tensor_tensor(
                    o_n[:, qc % 2, :, :], o[:, :, 0:C],
                    rden[:, qc, :].rearrange("p (a n) -> p a n", n=1).to_broadcast([P, NA, C]),
                    ALU.mult).then_inc(comb_st, 1)
                dve.wait_ge(comb_st, st + 2)
                on = o_n[:, qc % 2, :, :].rearrange("p a n -> p (a n)")
                nc.vector.tensor_tensor(h_sb[:, qc, :], on[:, 0:DM], on[:, DM:2 * DM],
                                        ALU.add).then_inc(comb_st, 1)

            def layernorm(m, src, st_t, mv_t, var_t, st, var_sem, rstd_t, rstd_sem, outs, out_sem):
                for c in range(NC):
                    nc.vector.bn_stats(st_t[:, c, :], src[:, c, :]).then_inc(st, 1)
                for c in range(NC):
                    dve.wait_ge(st, m * 2 * NC + c + 1)
                    dve.sem_inc(dve_waits, 1)
                    nc.vector.bn_aggr(mv_t[:, c, :], st_t[:, c, :]).then_inc(st, 1)
                dve.wait_ge(st, m * 2 * NC + 2 * NC)
                nc.vector.tensor_copy(var_t[:, :], mv_t[:, :, 1]).then_inc(var_sem, 1)
                dve.wait_ge(rstd_sem, m * 2 + 2)
                for c in range(NC):
                    nc.vector.tensor_scalar(outs[:, c, 0:DM], src[:, c, :], mv_t[:, c, 0:1],
                                            rstd_t[:, c:c + 1], ALU.subtract, ALU.mult)\
                        .then_inc(out_sem, 1)

            def m_ln1(m, k):
                dve.wait_ge(comb_st, (m + 1) * 3 * NC)
                layernorm(m, h_sb, stats, mv, var, ln_st, var_ok, rstd, rstd_ok, xn, xn_ok)

            def m_hide(m, k):
                for j in range(2):
                    _, use, bank = m_pos(m, U_HID + 2 + j)
                    dve.wait_ge(m_full, use + 1)
                    nc.vector.tensor_scalar(hid[:, j, :], m_ps[bank][:, :], b_in[:, j:j + 1], 0.0,
                                            ALU.add, ALU.max).then_inc(hide_ok, 1)

            def m_kq(m, k):
                _, use, bank = m_pos(m, U_KQ)
                dve.wait_ge(m_full, use + 1)
                for dst, r in ((kT, slice(0, DA)), (qT, slice(DA, 2 * DA))):
                    nc.vector.tensor_scalar(dst[0:DA, :], m_ps[bank][r, :], b_kq[r, :], None,
                                            ALU.add).then_inc(kq_ok, 1)

            def m_e(m, k):
                for k in range(2):
                    _, use, bank = m_pos(m, U_E + k)
                    dve.wait_ge(m_full, use + 1)
                    nc.vector.tensor_tensor(
                        e_sb[:, 2 * k:2 * k + 2, 0:DM],
                        m_ps[bank][:, 0:2 * DM].rearrange("p (c n) -> p c n", n=DM),
                        b_e2[:, :].rearrange("p (a n) -> p a n", a=1).to_broadcast([P, 2, DM]),
                        ALU.add).then_inc(e_ok, 1)

            def m_s1(m, qc):
                _, use, bank = m_pos(m, U_S1 + qc)
                dve.wait_ge(m_full, use + 1)
                nc.vector.tensor_reduce(nmax2[:, qc:qc + 1], m_ps[bank][:, :], AX.X, ALU.max,
                                        negate=True).then_inc(nmax2_ok, 1)

            def m_pv(m, k):
                _, use, bank = m_pos(m, U_PV + k)
                dve.wait_ge(m_full, use + 1)
                o = m_ps[bank][:, 0:2 * (DM + 1)].rearrange("p (c n) -> p c n", n=DM + 1)
                nc.vector.reciprocal(rden2[:, 2 * k:2 * k + 2], o[:, :, DM]).then_inc(out2_st, 1)
                dve.wait_ge(out2_st, m * 2 + k + 1)
                if k == 0:
                    dve.wait_ge(h2_out, m * 16 + H2_OUT)
                for c in range(2):
                    at = 2 * k + c
                    nc.vector.scalar_tensor_tensor(
                        out=h2[:, at, :], in0=o[:, c, 0:DM], scalar=rden2[:, at:at + 1],
                        in1=h_sb[:, at, :], op0=ALU.mult, op1=ALU.add).then_inc(h2_ok, 1)
                if k == 1:
                    dve.wait_ge(h2_ok, m * NC + NC)
                    dve.wait_ge(row_out, m * 16 + ROW_OUT)
                    layernorm(m, h2, stats2, mv2, var2, ln2_st, var2_ok, rstd2, rstd2_ok, row,
                              xn2_ok)

            def m_lgt(m, k):
                _, use, bank = m_pos(m, U_LGT)
                dve.wait_ge(m_full, use + 1)
                nc.vector.tensor_copy(row[:, :, DM:TW], m_ps[bank][:, 0:NC * E]
                                      .rearrange("p (c e) -> p c e", e=E)).then_inc(rowlg_ok, 1)

            run_all(dve, {"A_P": a_p_all, "P1": p1, "AUG": aug, "PV": pv, "M_LN1": m_ln1,
                          "M_HIDE": m_hide, "M_KQ": m_kq, "M_E": m_e, "M_S1": m_s1, "M_PV": m_pv,
                          "M_LGT": m_lgt})

        @block.tensor
        def _(pe):
            pe.wait_ge(const_in, N_CONST)
            pe.wait_ge(pool_const, 9)
            pe.wait_ge(act_const, 3)

            def transposes(ps, parts, n=P):
                for j, src in enumerate(parts):
                    last = nc.tensor.transpose(ps[:, j * n:(j + 1) * n], src, ident[:, :])
                return last

            def t_slot(kind, t, k):
                first = isinstance(t, int) and t == 0
                last = isinstance(t, int) and t == B - 1
                if kind == "A" and k < 2:
                    if not first:
                        pe.wait_ge(qmax_ok, t * 4 - 2 + 2 * k)
                elif kind == "A" and k < 4:
                    pe.wait_ge(xT_ok, t * 2 + k - 1)
                elif kind == "A":
                    pe.wait_ge(rest_ok, t * 4 + k - 3)
                elif kind == "PV" and k < 2 and last:
                    pe.wait_ge(qmax_ok, t * 4 + 2 + 2 * k)
                elif kind == "PV" and k < 2:
                    pe.wait_ge(rest_ok, t * 4 + 7 + k)
                elif kind == "PV":
                    pe.wait_ge(comb_st, t * 3 * NC + 3 * (k - 2) + 2)
                elif kind == "V" and first:
                    pe.wait_ge(rest_ok, 3 + k)
                elif kind == "V":
                    pe.wait_ge(comb_st, t * 3 * NC + 3 * (k + 2 - NC) + 2)
                else:
                    pe.wait_ge(v_ok, t * 4 + 2 * k + 2)
                return t_ps[t_pos(kind, t, k)[2]]

            def s_slot(t, k):
                _, use, slot = s_pos(t, k)
                if k < 8:
                    if k >= 2:
                        pe.wait_ge(s_free[slot], t * 4 + k // 2)
                    else:
                        pe.wait_ge(p_ok, t * 8 - 1 + k) if not (isinstance(t, int) and t == 0) \
                            else None
                elif k < 10:
                    pe.wait_ge(s_free[slot], t * 4 + 4)
                else:
                    pe.wait_ge(p_ok, t * 8 + k - 9)
                return s_ps[slot]

            def a_x(t, k):
                pe.wait_ge(x_in, (t + 1) * 16)
                for k in range(2):
                    ps = t_slot("A", t, k)
                    last = transposes(ps, [x_sb[:, 2 * k + j, :] for j in range(2)])
                    last.then_inc(t_full, 1)

            def a_p(t, k):
                ps = t_slot("A", t, 2 + k)
                if k == 0:
                    pe.wait_ge(xT_ok, t * 2 + 2)
                nc.tensor.matmul(ps[:, :], w_stack[:, k, :], xT[:, :], start=True, stop=True)\
                    .then_inc(t_full, 1)

            def v(t, k):
                for k in range(2):
                    ps = t_slot("V", t, k)
                    for c in range(2):
                        at = (2 * k + c) * P
                        last = nc.tensor.matmul(ps[:, c * 256:(c + 1) * 256], xT[:, at:at + P],
                                                w_v[:, :], start=True, stop=True)
                    last.then_inc(t_full, 1)

            def p1(t, qc):
                if qc == 0:
                    pe.wait_ge(stack_ok, t * 6 + 6)
                for pair in range(2):
                    ps = s_slot(t, 2 * qc + pair)
                    for h in range(2):
                        last = nc.tensor.matmul(
                            ps[:, h, :], q_st[:, 2 * pair + h, qc * P:(qc + 1) * P],
                            k_st[:, pair, :], start=True, stop=True)
                    last.then_inc(s_full, 1)

            def aug(t, k):
                pe.wait_ge(nm_ok, t + 1)
                for pair in range(2):
                    ps = t_slot("AUG", t, pair)
                    for qc in range(NC):
                        at = NA * qc + 2 * pair
                        last = nc.tensor.matmul(
                            ps[:, qc * P:(qc + 1) * P],
                            nm_st[:, at:at + 2, :].rearrange("p a n -> p (a n)"), identb[:, :],
                            start=True, stop=True)
                    last.then_inc(t_full, 1)

            def p2(t, kc):
                if kc == 0:
                    pe.wait_ge(qmax_ok, t * 4 + 4)
                for pair in range(2):
                    ps = s_slot(t, 8 + 2 * kc + pair)
                    for h in range(2):
                        last = nc.tensor.matmul(
                            ps[:, h, :], k_st[:, pair, kc * P:(kc + 1) * P],
                            q_st[:, 2 * pair + h, :], start=True, stop=True)
                    last.then_inc(s_full, 1)

            def pv(t, qc):
                if qc == 0:
                    pe.wait_ge(p_ok, t * 8 + 8)
                    pe.wait_ge(v_ok, t * 4 + 4)
                ps = t_slot("PV", t, qc)
                for a in range(NA):
                    for kc in range(NC):
                        last = nc.tensor.matmul(
                            ps[:, a * P:(a + 1) * P],
                            pT[:, kc, a, qc * P:(qc + 1) * P], v_sb[:, kc, a, :],
                            start=kc == 0, stop=kc == NC - 1)
                last.then_inc(t_full, 1)

            def m_slot(m, k):
                _, use, bank = m_pos(m, k)
                first = isinstance(m, int) and m == 0
                prev = (k - 2) % M_USES
                mm = m - 1 if k < 2 else m
                if k < 2 and first:
                    return m_ps[bank]
                if prev == U_XNT:
                    pe.wait_ge(xnT_ok, mm + 1)
                elif U_HID <= prev < U_HID + 2:
                    pe.wait_ge(hidk_ok, mm * 2 + prev - U_HID + 1)
                elif U_HID + 2 <= prev < U_HID + 4:
                    pe.wait_ge(hide_ok, mm * 2 + prev - U_HID - 1)
                elif prev == U_KQ:
                    pe.wait_ge(kq_ok, mm * 2 + 2)
                elif U_E <= prev < U_E + 2:
                    pe.wait_ge(e_ok, mm * 2 + prev - U_E + 1)
                elif U_S1 <= prev < U_S1 + NC:
                    pe.wait_ge(nmax2_ok, mm * NC + prev - U_S1 + 1)
                elif prev == U_AUG:
                    pe.wait_ge(q2max_ok, mm + 1)
                elif U_S2 <= prev < U_S2 + NC:
                    pe.wait_ge(p2_ok, mm * NC + prev - U_S2 + 1)
                elif U_PV <= prev < U_PV + 2:
                    pe.wait_ge(h2_ok, mm * NC + 2 * (prev - U_PV) + 2)
                elif prev == U_ROWT:
                    pe.wait_ge(rowT_ok, mm + 1)
                elif prev == U_LG:
                    pe.wait_ge(lgT_ok, mm + 1 + LG_OK)
                else:
                    pe.wait_ge(rowlg_ok, mm + 1 + LG_OK)
                return m_ps[bank]

            def m_xnt(m, k):
                pe.wait_ge(xn_ok, m * NC + NC)
                ps = m_slot(m, U_XNT)
                transposes(ps, [xn[:, c, :] for c in range(NC)]).then_inc(m_full, 1)

            def hidden(m, j, k):
                ps = m_slot(m, k)
                nc.tensor.matmul(ps[:, :], w_in[:, j * P:(j + 1) * P], xnT[:, :],
                                 start=True, stop=True).then_inc(m_full, 1)

            def m_hidk(m, k):
                pe.wait_ge(xnT_ok, m + 1)
                for j in range(2):
                    hidden(m, 2 + j, U_HID + j)

            def m_hide(m, k):
                for j in range(2):
                    hidden(m, j, U_HID + 2 + j)

            def m_kq(m, k):
                pe.wait_ge(hidk_ok, m * 2 + 2)
                ps = m_slot(m, U_KQ)
                for i in range(2):
                    last = nc.tensor.matmul(ps[:, :], w_kq[:, i, :], hid[:, 2 + i, :],
                                            start=i == 0, stop=i == 1)
                last.then_inc(m_full, 1)

            def m_e(m, k):
                pe.wait_ge(hide_ok, m * 2 + 2)
                for k in range(2):
                    ps = m_slot(m, U_E + k)
                    for j in range(2):
                        c = 2 * k + j
                        for i in range(2):
                            last = nc.tensor.matmul(ps[:, j * P:(j + 1) * P],
                                                    hid[:, i, c * P:(c + 1) * P], w_e2[:, i, :],
                                                    start=i == 0, stop=i == 1)
                    last.then_inc(m_full, 1)

            def m_s1(m, qc):
                if qc == 0:
                    pe.wait_ge(kq_ok, m * 2 + 2)
                    pe.wait_ge(qz_ok, m + 1)
                ps = m_slot(m, U_S1 + qc)
                nc.tensor.matmul(ps[:, :], qT[:, qc * P:(qc + 1) * P], kT[:, :],
                                 start=True, stop=True).then_inc(m_full, 1)

            def m_aug(m, k):
                pe.wait_ge(nmax2_ok, m * NC + NC)
                ps = m_slot(m, U_AUG)
                for qc in range(NC):
                    last = nc.tensor.matmul(ps[DA:DA + 1, qc * P:(qc + 1) * P],
                                            nmax2[:, qc:qc + 1], ident[:, :],
                                            start=True, stop=True)
                last.then_inc(m_full, 1)

            def m_s2(m, kc):
                if kc == 0:
                    pe.wait_ge(q2max_ok, m + 1)
                ps = m_slot(m, U_S2 + kc)
                nc.tensor.matmul(ps[:, :], kT[:, kc * P:(kc + 1) * P], qT[:, :],
                                 start=True, stop=True).then_inc(m_full, 1)

            def m_pv(m, k):
                if k == 0:
                    pe.wait_ge(p2_ok, m * NC + NC)
                    pe.wait_ge(e_ok, m * 2 + 2)
                ps = m_slot(m, U_PV + k)
                for c in range(2):
                    qc = 2 * k + c
                    for kc in range(NC):
                        last = nc.tensor.matmul(ps[:, c * (DM + 1):(c + 1) * (DM + 1)],
                                                p2T[:, kc, qc * P:(qc + 1) * P], e_sb[:, kc, :],
                                                start=kc == 0, stop=kc == NC - 1)
                last.then_inc(m_full, 1)

            def m_row(m, k):
                pe.wait_ge(xn2_ok, m * NC + NC)
                ps = m_slot(m, U_ROWT)
                transposes(ps, [row[:, c, 0:DM] for c in range(NC)]).then_inc(m_full, 1)

            def m_lg(m, k):
                pe.wait_ge(rowT_ok, m + 1)
                ps = m_slot(m, U_LG)
                nc.tensor.matmul(ps[0:E, :], w_r[:, :], rowT[:, :], start=True, stop=True)\
                    .then_inc(m_full, 1)

            def m_lgt(m, k):
                pe.wait_ge(lgT_ok, m + 1 + LG_OK)
                ps = m_slot(m, U_LGT)
                pe.sem_inc(pe_waits, 1)
                for c in range(NC):
                    last = nc.tensor.transpose(ps[:, c * E:(c + 1) * E],
                                               lgT[:, c * P:(c + 1) * P], ident[0:E, 0:E])
                last.then_inc(m_full, 1)

            run_all(pe, {"A_X": a_x, "A_P": a_p, "V": v, "P1": p1, "AUG": aug, "P2": p2, "PV": pv,
                         "M_XNT": m_xnt, "M_HIDK": m_hidk, "M_HIDE": m_hide, "M_KQ": m_kq,
                         "M_E": m_e, "M_S1": m_s1, "M_AUG": m_aug, "M_S2": m_s2, "M_PV": m_pv,
                         "M_ROW": m_row, "M_LG": m_lg, "M_LGT": m_lgt})
        first_block.close()

        group, before, expert, iota, token = (
            sb(n + "_sb", list(A[n].shape)) for n in ("group", "before", "expert", "iota", "token"))
        ones = sb("ones", [P, L])
        lgs = sb("lgs", [P, L])
        prob = sb("prob", [P, L])
        rmax = sb("rmax", [P, 1])
        gmax = sb("gmax", [1, E])
        nrow = sb("nrow", [1, P])
        nmx = sb("nmx", [P, 1])
        zpart = sb("zpart", [P, 1])
        zrow = sb("zrow", [P, E])
        cur = sb("cur", [P, 1], I32)
        bit = sb("bit", [P, 1], I32)
        cand = sb("cand", [P, 1], I32)
        count = sb("count", [P, 1])
        keep = sb("keep", [P, 1], U32)
        need = sb("need", [P, 1])
        above = sb("above", [P, L])
        ties = sb("ties", [P, L])
        scan = sb("scan", [P, L])
        chosen = sb("chosen", [P, L])
        place_i = sb("place_i", [P, L], I32)
        hi_i = sb("hi_i", [P, L], I32)
        lo_i = sb("lo_i", [P, L], I32)
        hi_f = sb("hi_f", [P, L])
        lo_f = sb("lo_f", [P, L])
        hiT = sb("hiT", [P, L])
        loT = sb("loT", [P, L])
        oh_hi = [pT[:, 2 * j:2 * j + 2, :, :].rearrange("p a b (c n) -> p (a b c) n", n=32)
                 for j in range(2)]
        oh_lo = [sb(f"oh_lo{j}", [P, P, 32]) for j in range(2)]
        idx_sb = sb("idx_sb", [P, 2, 32], I32)

        sel_in = sem("sel_in")
        sel_st = sem("sel_st")
        sel_pe = sem("sel_pe")
        sel_act = sem("sel_act")
        bis_st = sem("bis_st")
        bis_sum = sem("bis_sum")
        ones_ok = sem("ones_ok")
        dig_ok = sem("dig_ok")
        digT_ps = sem("digT_ps")
        hiT_ok = sem("hiT_ok")
        hot_hi = sem("hot_hi")
        hot_st = sem("hot_st")
        hot_lo = sem("hot_lo")
        hot_used = sem("hot_used")
        idx_ok = sem("idx_ok")
        idx_out = sem("idx_out")
        BITS = 30
        N_DVE1 = 5

        w_in_s = [sem(f"w_in{s}") for s in range(2)]

        def load_expert(sp, e, s):
            with nc.allow_non_contiguous_dma(reason="biases"):
                for dst, src in (
                    (w1[s][:, :], A["w1"][bass.ds(e, 1), :, :].rearrange("a d f -> (a d) f")),
                    (w2[s][:, :, :], A["w2"][bass.ds(e, 1), :, :]
                     .rearrange("a (f p) d -> p (a f) d", p=P)),
                    (b1[s][:, :], A["b1"][bass.ds(e, 1), :].rearrange("a (f p) -> p (a f)", p=P)),
                    (b2[s][:, :], A["b2"][bass.ds(e, 1), :].to_broadcast([P, DM])),
                ):
                    sp.dma_start(dst, src).then_inc(w_in_s[s], 16)

        second_block = ExitStack()
        block = second_block.enter_context(nc.Block())

        @block.sync
        def _(sp):
            sp.dma_start(lgs[:, :], lg_d.rearrange("b e t -> (b e) t")).then_inc(sel_in, 16)
            for dst, n in ((group, "group"), (before, "before"), (expert, "expert"),
                           (iota, "iota"), (token, "token")):
                sp.dma_start(dst[:, :], A[n]).then_inc(sel_in, 16)
            for e in range(2):
                load_expert(sp, e, e)
            sp.wait_ge(idx_ok, 8)
            for g in range(2):
                sp.dma_start(idx_d[4 * g:4 * g + 4, :].rearrange("e (h l) -> (e h) l", l=32),
                             idx_sb[:, g, :]).then_inc(idx_out, 16)
            sp.wait_ge(idx_out, 32)

        @block.gpsimd
        def _(pool):
            nc.gpsimd.memset(ones[:, :], 1.0).then_inc(ones_ok, 1)
            nc.gpsimd.memset(cur[:, :], 0).then_inc(ones_ok, 1)
            nc.gpsimd.memset(bit[:, :], 1 << (BITS - 1)).then_inc(ones_ok, 1)
            pool.wait_ge(sel_in, 16 * 6)
            for c in range(NC):
                pool.wait_ge(hot_st, c + 1)
                flat = oh_lo[c % 2][:, :, :].rearrange("p (b e) n -> p b (e n)", e=E)
                nc.gpsimd.tensor_tensor(
                    flat, flat,
                    token[:, c * B:(c + 1) * B].rearrange("p (b a) -> p b a", a=1)
                    .to_broadcast([P, B, E * 32]), ALU.mult).then_inc(hot_lo, 1)

        @block.scalar
        def _(act):
            act.wait_ge(sel_st, 5)
            nc.scalar.activation(prob[:, :], lgs[:, :], ACT.Exp, bias=nmx[:, :],
                                 accum_out=zpart[:, :]).then_inc(sel_act, 1)
            act.wait_ge(digT_ps, 1)
            nc.scalar.copy(hiT[:, :], s_ps[0][:, 0, :]).then_inc(hiT_ok, 1)

        @block.vector
        def _(dve):
            steps = [0]

            def step(instruction):
                instruction.then_inc(sel_st, 1)
                steps[0] += 1
                dve.wait_ge(sel_st, steps[0])

            dve.wait_ge(sel_in, 16 * 6)
            step(nc.vector.tensor_reduce(rmax[:, :], lgs[:, :], AX.X, ALU.max))
            dve.wait_ge(sel_pe, 1)
            step(nc.vector.tensor_reduce(
                gmax[:, :], m_ps[0][0:1, 0:P].rearrange("p (b e) -> p e b", e=E), AX.X, ALU.max))
            step(nc.vector.tensor_scalar(
                nrow[:, :].rearrange("p (b e) -> p b e", e=E),
                gmax[:, :].rearrange("p (a e) -> p a e", a=1).to_broadcast([1, B, E]), -1.0, None,
                ALU.mult))
            dve.wait_ge(sel_pe, 2)
            nc.vector.tensor_copy(nmx8[:, :], m_ps[1][:, 8:8 + E]).then_inc(sel_st, 1)
            steps[0] += 1
            step(nc.vector.tensor_copy(nmx[:, :], m_ps[1][:, 0:1]))
            dve.wait_ge(sel_act, 1)
            step(nc.vector.tensor_scalar(zrow[:, :], expert[:, :], zpart[:, 0:1], None, ALU.mult))
            dve.wait_ge(sel_pe, 3)
            step(nc.vector.reciprocal(rz8[:, :], m_ps[0][:, 16:16 + E]))

            dve.wait_ge(ones_ok, 3)
            with dve.Fori(0, BITS) as i:
                nc.vector.tensor_tensor(cand[:, :], cur[:, :], bit[:, :], ALU.bitwise_or)\
                    .then_inc(bis_st, 1)
                dve.wait_ge(bis_st, i * 5 + 1)
                nc.vector.tensor_scalar(above[:, :], prob[:, :], cand[:, :].bitcast(F32), None,
                                        ALU.is_ge, ALU.add, accum_out=count[:, :])\
                    .then_inc(bis_st, 1)
                dve.wait_ge(bis_sum, i + 1)
                nc.vector.tensor_scalar(keep[:, :], m_ps[0][:, 0:1], float(CAP), None, ALU.is_ge)\
                    .then_inc(bis_st, 1)
                dve.wait_ge(bis_st, i * 5 + 3)
                dve.sem_inc(dve_waits, 1)
                nc.vector.copy_predicated(cur[:, :], keep[:, :], cand[:, :]).then_inc(bis_st, 1)
                nc.vector.tensor_scalar(bit[:, :], bit[:, :], 1, None, ALU.logical_shift_right)\
                    .then_inc(bis_st, 1)
                dve.wait_ge(bis_st, i * 5 + 5)
                dve.sem_inc(dve_waits, 1)
            thr = cur[:, :].bitcast(F32)
            nc.vector.tensor_scalar(ties[:, :], prob[:, :], thr, None, ALU.is_equal)\
                .then_inc(sel_st, 1)
            steps[0] += 1
            step(nc.vector.tensor_scalar(above[:, :], prob[:, :], thr, None, ALU.is_gt, ALU.add,
                                         accum_out=count[:, :]))
            step(nc.vector.tensor_tensor_scan(scan[:, :], ones[:, :], ties[:, :], 0.0, ALU.mult,
                                              ALU.add))
            dve.wait_ge(sel_pe, 4)
            step(nc.vector.tensor_scalar(need[:, :], m_ps[1][:, 32:33], -1.0, float(CAP), ALU.mult,
                                         ALU.add))
            step(nc.vector.tensor_tensor(need[:, :], need[:, :], m_ps[1][:, 33:34], ALU.subtract))
            step(nc.vector.scalar_tensor_tensor(out=chosen[:, :], in0=scan[:, :],
                                                scalar=need[:, :], in1=ties[:, :], op0=ALU.is_le,
                                                op1=ALU.mult))
            step(nc.vector.tensor_tensor(chosen[:, :], chosen[:, :], above[:, :], ALU.add))
            step(nc.vector.tensor_tensor_scan(scan[:, :], ones[:, :], chosen[:, :], 0.0, ALU.mult,
                                              ALU.add))
            dve.wait_ge(sel_pe, 5)
            step(nc.vector.tensor_copy(need[:, :], m_ps[0][:, 34:35]))
            step(nc.vector.scalar_tensor_tensor(out=scan[:, :], in0=scan[:, :], scalar=need[:, :],
                                                in1=chosen[:, :], op0=ALU.add, op1=ALU.mult))
            step(nc.vector.tensor_scalar(place_i[:, :], scan[:, :], -1.0, None, ALU.add))
            step(nc.vector.tensor_scalar(hi_i[:, :], place_i[:, :], 5, None,
                                         ALU.arith_shift_right))
            step(nc.vector.tensor_scalar(lo_i[:, :], place_i[:, :], 31, None, ALU.bitwise_and))
            nc.vector.tensor_copy(hi_f[:, :], hi_i[:, :]).then_inc(dig_ok, 1)
            nc.vector.tensor_copy(lo_f[:, :], lo_i[:, :]).then_inc(dig_ok, 1)
            dve.wait_ge(digT_ps, 2)
            step(nc.vector.tensor_copy(loT[:, :], s_ps[0][:, 1, :]))
            dve.wait_ge(hiT_ok, 1)
            for c in range(NC):
                if c >= 2:
                    dve.wait_ge(hot_used, c - 1)
                for dig, hot, done in ((loT, oh_lo[c % 2][:, :, :], hot_st),
                                       (hiT, oh_hi[c % 2], hot_hi)):
                    nc.vector.tensor_tensor(
                        hot, dig[:, c * P:(c + 1) * P].rearrange("p (n a) -> p n a", a=1)
                        .to_broadcast([P, P, 32]),
                        iota[:, :].rearrange("p (a n) -> p a n", a=1).to_broadcast([P, P, 32]),
                        ALU.is_equal).then_inc(done, 1)
            dve.wait_ge(hot_used, NC)
            for g in range(2):
                for e in range(4):
                    r = slice(32 * e, 32 * e + 32)
                    nc.vector.tensor_copy(idx_sb[r, g, :], t_ps[g][r, 32 * e:32 * e + 32])\
                        .then_inc(idx_ok, 1)

        @block.tensor
        def _(pe):
            pe.wait_ge(sel_in, 16 * 6)
            pe.wait_ge(ones_ok, 3)
            pe.wait_ge(sel_st, 1)
            nc.tensor.matmul(m_ps[0][0:1, 0:P], rmax[:, :], ident[:, :], start=True, stop=True)\
                .then_inc(sel_pe, 1)
            pe.wait_ge(sel_st, 3)
            nc.tensor.matmul(m_ps[1][:, 0:1], nrow[:, :], ones[0:1, 0:1], start=True, stop=True)
            nc.tensor.matmul(m_ps[1][:, 8:8 + E], ones[0:1, 0:P], nrow[:, 0:E],
                             start=True, stop=True).then_inc(sel_pe, 1)
            pe.wait_ge(sel_st, 6)
            nc.tensor.matmul(m_ps[0][:, 16:16 + E], ones[:, 0:P], zrow[:, :],
                             start=True, stop=True).then_inc(sel_pe, 1)
            pe.wait_ge(sel_st, 7)
            with pe.Fori(0, BITS) as i:
                pe.wait_ge(bis_st, i * 5 + 2)
                nc.tensor.matmul(m_ps[0][:, 0:1], group[:, :], count[:, :], start=True, stop=True)\
                    .then_inc(bis_sum, 1)
            pe.wait_ge(sel_st, 10)
            nc.tensor.matmul(m_ps[1][:, 32:33], group[:, :], count[:, :], start=True, stop=True)
            nc.tensor.matmul(m_ps[1][:, 33:34], before[:, :], scan[:, L - 1:L],
                             start=True, stop=True).then_inc(sel_pe, 1)
            pe.wait_ge(sel_st, 15)
            nc.tensor.matmul(m_ps[0][:, 34:35], before[:, :], scan[:, L - 1:L],
                             start=True, stop=True).then_inc(sel_pe, 1)
            for j, src in enumerate((hi_f, lo_f)):
                pe.wait_ge(dig_ok, j + 1)
                for c in range(NC):
                    last = nc.tensor.transpose(s_ps[0][:, j, c * P:(c + 1) * P],
                                               src[:, c * P:(c + 1) * P], ident[:, :])
                last.then_inc(digT_ps, 1)
            for c in range(NC):
                pe.wait_ge(hot_hi, c + 1)
                pe.wait_ge(hot_lo, c + 1)
                for b in range(B):
                    for g in range(2):
                        at = slice(b * E + 4 * g, b * E + 4 * g + 4)
                        last = nc.tensor.matmul(
                            t_ps[g][:, 0:P],
                            oh_hi[c % 2][:, at, :].rearrange("p e n -> p (e n)"),
                            oh_lo[c % 2][:, at, :].rearrange("p e n -> p (e n)"),
                            start=c == 0 and b == 0, stop=c == NC - 1 and b == B - 1)
                last.then_inc(hot_used, 1)

        second_block.close()

        own.pop().close()
        own.append(ctx)
        NT = CAP // L
        TILES = E * NT
        idx = sb("idx", [P, E, NT, NC], I32)
        g_idx = sb("g_idx", [P, NT, NC], I32)
        s_idx = [sb(f"s_idx{u}", [P, NC], I32) for u in range(NT)]
        g_sb = sb("g_sb", [P, NT, NC, TW])
        gT = [sb(f"gT{u}", [P, L]) for u in range(NT)]
        hT = [sb(f"hT{u}", [P, NF, L]) for u in range(NT)]
        wt = [sb(f"wt{s}", [P, NT, NC]) for s in range(2)]
        y = [sb(f"y{u}", [P, NC, DM]) for u in range(NT)]

        idx_in = sem("idx_in")
        g_idx_ok = sem("g_idx_ok")
        s_idx_ok = sem("s_idx_ok")
        g_in = [sem(f"g_in{u}") for u in range(NT)]
        gT_ps = sem("gT_ps")
        gT_ok = sem("gT_ok")
        f_full = sem("f_full")
        hT_ok = sem("hT_ok")
        o_full = sem("o_full")
        we_ok = sem("we_ok")
        wz_ok = sem("wz_ok")
        y_st = sem("y_st")
        y_ok = sem("y_ok")
        y_out = [sem(f"y_out{u}") for u in range(NT)]
        y_done = sem("y_done")
        Y_ST, Y_DONE = 1, 1

        third_block = ExitStack()
        block = third_block.enter_context(nc.Block())

        out_rows = out.rearrange("b l n -> (b l) n")

        def run_experts(eng, body):
            body(0, 0)
            with eng.Fori(0, E // 2 - 2) as i:
                body(i * 2 + 1, 1)
                body(i * 2 + 2, 0)
            body(E - 3, 1)
            body(E - 2, 0)
            body(E - 1, 1)

        @block.sync
        def _(sp):
            sp.dma_start(idx[:, :, :, :], idx_d.rearrange("e (p u j) -> p e u j", p=P, u=NT))\
                .then_inc(idx_in, 16)

            def load(e, s):
                sp.wait_ge(y_st, (e - 1) * NT + Y_ST)
                sp.sem_inc(sp_waits, 1)
                load_expert(sp, e, s)

            with sp.Fori(1, E // 2) as i:
                load(i * 2, 0)
                load(i * 2 + 1, 1)
            for u in range(NT):
                sp.wait_ge(y_out[u], E * NC * 16)

        @block.gpsimd
        def _(pool):
            pool.sem_inc(y_done, Y_DONE)

            def gather(u):
                for j in range(NC):
                    nc.gpsimd.indirect_dma_start(
                        out=g_sb[:, u, j, :], out_offset=None, in_=tab_d[:, :],
                        in_offset=bass.IndirectOffsetOnAxis(
                            ap=g_idx[:, u, j:j + 1], axis=0)).then_inc(g_in[u], 16)

            def scatter(u):
                for j in range(NC):
                    nc.gpsimd.indirect_dma_start(
                        out=out_rows, out_offset=bass.IndirectOffsetOnAxis(
                            ap=s_idx[u][:, j:j + 1], axis=0),
                        in_=y[u][:, j, :], in_offset=None, compute_op=ALU.add)\
                        .then_inc(y_out[u], 16)

            def own_wait():
                pool.sem_inc(pool_waits, 1)

            def body(e, s):
                first = isinstance(e, int) and e == 0
                last = isinstance(e, int) and e == E - 1
                if not last:
                    pool.wait_ge(gT_ps, (e + 1) * NT)
                    pool.wait_ge(we_ok, e + 1)
                    own_wait()
                    gather(1)
                if not first:
                    pool.wait_ge(y_ok, e * NT)
                    pool.wait_ge(s_idx_ok, e * NT)
                    own_wait()
                    scatter(1)
                if not (last or isinstance(e, int) and e == E - 2):
                    pool.wait_ge(gT_ps, (e + 1) * NT + 1)
                    pool.wait_ge(we_ok, e + 2)
                    pool.wait_ge(g_idx_ok, e + 3)
                    own_wait()
                    gather(0)
                if not first:
                    for u in range(NT):
                        pool.wait_ge(y_out[u], e * NC * 16)
                    pool.sem_inc(y_done, 1)
                pool.wait_ge(y_ok, e * NT + 1)
                pool.wait_ge(s_idx_ok, e * NT + 1)
                own_wait()
                scatter(0)

            pool.wait_ge(g_idx_ok, 1)
            gather(0)
            gather(1)
            pool.wait_ge(gT_ps, 1)
            pool.wait_ge(we_ok, 1)
            pool.wait_ge(g_idx_ok, 2)
            gather(0)
            run_experts(pool, body)
            pool.wait_ge(y_ok, TILES)
            pool.wait_ge(s_idx_ok, TILES)
            scatter(1)

        @block.scalar
        def _(act):
            def weights(e, s):
                if not (isinstance(e, int) and e < 2):
                    act.wait_ge(y_ok, (e - 1) * NT)
                for u in range(NT):
                    act.wait_ge(g_in[u], (e + 1) * NC * 16)
                nc.scalar.activation(
                    wt[s][:, :, :], g_sb[:, :, :, bass.ds(e + DM, 1)]
                    .rearrange("p u c a -> p u (c a)"), ACT.Exp, bias=nmx8[:, bass.ds(e, 1)])\
                    .then_inc(we_ok, 1)

            def indices(e):
                if isinstance(e, int) and e == 0:
                    act.wait_ge(idx_in, 16)
                nc.scalar.copy(g_idx[:, :, :], idx[:, bass.ds(e, 1), :, :]
                               .rearrange("p e u j -> p (e u) j")).then_inc(g_idx_ok, 1)

            def body(e, s):
                for u in range(NT):
                    for f in range(NF):
                        act.wait_ge(f_full, (e * NT + u) * NF + f + 1)
                        nc.scalar.activation(hT[u][:, f, :], s_ps[f // 2][:, f % 2, :],
                                             ACT.Gelu, bias=b1[s][:, f:f + 1])\
                            .then_inc(hT_ok, 1)
                if not (isinstance(e, int) and e == E - 1):
                    weights(e + 1, 1 - s)
                if not (isinstance(e, int) and e >= E - 2):
                    indices(e + 2)

            indices(0)
            weights(0, 0)
            indices(1)
            run_experts(act, body)

        @block.vector
        def _(dve):
            dve.sem_inc(y_st, Y_ST)

            def copy_gT(n, u):
                dve.wait_ge(gT_ps, n + 1)
                nc.vector.tensor_copy(gT[u][:, :], m_ps[u][:, :]).then_inc(gT_ok, 1)

            def result(n, e, u, s):
                if isinstance(e, int) and e == 0 and u == 0:
                    dve.wait_ge(idx_in, 16)
                nc.vector.tensor_copy(s_idx[u][:, :], idx[:, bass.ds(e, 1), u, :]
                                      .rearrange("p e j -> p (e j)")).then_inc(s_idx_ok, 1)
                dve.wait_ge(o_full, n + 1)
                nc.vector.tensor_tensor(
                    y[u][:, :, :],
                    t_ps[u][:, :].rearrange("p (c n) -> p c n", n=DM),
                    b2[s][:, :].rearrange("p (a n) -> p a n", a=1)
                    .to_broadcast([P, NC, DM]), ALU.add).then_inc(y_st, 1)
                dve.wait_ge(y_st, n + 1 + Y_ST)
                nc.vector.tensor_tensor(
                    y[u][:, :, :], y[u][:, :, :],
                    wt[s][:, u, :].rearrange("p (c a) -> p c a", a=1)
                    .to_broadcast([P, NC, DM]), ALU.mult).then_inc(y_ok, 1)

            def body(e, s):
                first = isinstance(e, int) and e == 0
                last = isinstance(e, int) and e == E - 1
                copy_gT(e * NT + 1, 1)
                if not first:
                    dve.wait_ge(y_done, e - 1 + Y_DONE)
                    result(e * NT - 1, e - 1, 1, 1 - s)
                dve.wait_ge(we_ok, e + 1)
                nc.vector.tensor_scalar(wt[s][:, :, :], wt[s][:, :, :], rz8[:, bass.ds(e, 1)],
                                        None, ALU.mult).then_inc(wz_ok, 1)
                if not last:
                    copy_gT(e * NT + 2, 0)
                if not first:
                    dve.wait_ge(y_out[0], e * NC * 16)
                dve.wait_ge(wz_ok, e + 1)
                result(e * NT, e, 0, s)

            copy_gT(0, 0)
            run_experts(dve, body)
            dve.wait_ge(y_out[1], (E - 1) * NC * 16)
            result(TILES - 1, E - 1, 1, 1)

        @block.tensor
        def _(pe):
            def turn(e, u):
                pe.wait_ge(g_in[u], (e + 1) * NC * 16)
                for j in range(NC):
                    last = nc.tensor.transpose(m_ps[u][:, j * P:(j + 1) * P],
                                               g_sb[:, u, j, 0:DM], ident[:, :])
                last.then_inc(gT_ps, 1)

            def hidden(e, s, u):
                n = e * NT + u
                pe.wait_ge(gT_ok, n + 1)
                for f in range(NF):
                    if not (isinstance(n, int) and n == 0):
                        pe.wait_ge(hT_ok, (n - 1) * NF + f + 1)
                    nc.tensor.matmul(s_ps[f // 2][:, f % 2, :], w1[s][:, f * P:(f + 1) * P],
                                     gT[u][:, :], start=True, stop=True).then_inc(f_full, 1)

            def output(n, s, u):
                pe.wait_ge(hT_ok, n * NF + NF)
                if not (isinstance(n, int) and n < 2):
                    pe.wait_ge(y_st, n - 1 + Y_ST)
                for j in range(NC):
                    for f in range(NF):
                        last = nc.tensor.matmul(
                            t_ps[u][:, j * P:(j + 1) * P],
                            hT[u][:, f, j * P:(j + 1) * P], w2[s][:, f, :],
                            start=f == 0, stop=f == NF - 1)
                last.then_inc(o_full, 1)

            def body(e, s):
                first = isinstance(e, int) and e == 0
                last = isinstance(e, int) and e == E - 1
                if isinstance(e, int):
                    pe.wait_ge(w_in_s[s], (e // 2 + 1) * 4 * 16)
                else:
                    pe.wait_ge(w_in_s[s], (e - s + 2) * 2 * 16)
                hidden(e, s, 0)
                turn(e, 1)
                if not first:
                    output(e * NT - 1, 1 - s, 1)
                hidden(e, s, 1)
                if not last:
                    turn(e + 1, 0)
                output(e * NT, s, 0)

            turn(0, 0)
            run_experts(pe, body)
            output(TILES - 1, 1, 1)

        third_block.close()


def layout(i):
    g = {k: np.ascontiguousarray(np.asarray(v)) for k, v in i.items()}
    w = {n: g[f"L0_tok_w{n}"] for n in range(1, 13)}
    ecg, pcg = 0, 1
    q = [(4, ecg), (10, pcg), (1, ecg), (7, pcg)]
    k = [(5, pcg), (11, ecg), (2, ecg), (8, pcg)]
    v = [(6, pcg), (12, ecg), (3, ecg), (9, pcg)]
    w_stack = np.zeros((4, DM, P), np.float32)
    w_v = np.zeros((DM, NA * C), np.float32)
    for a in range(NA):
        for r in SLOT_ROW:
            at = 64 * (a % 2) + r
            w_stack[a // 2, q[a][1]::2, at:at + D] = w[q[a][0]]
            w_stack[2 + a // 2, k[a][1]::2, at:at + D] = w[k[a][0]]
        w_v[v[a][1]::2, a * C:(a + 1) * C] = w[v[a][0]]
    d = {"x": g["x"].reshape(B, L, DM), "w_stack": w_stack, "w_v": w_v,
         "alpha": g["L0_tok_alpha"], "gamma": g["L0_tok_gamma"],
         "w_in": np.concatenate([g["L0_attn_We1"], g["L0_attn_Wk1"]], 1),
         "b_in": np.concatenate([g["L0_attn_be1"], g["L0_attn_bk1"]]),
         "w_kq": g["L0_attn_Wk2"], "b_kq": g["L0_attn_bk2"],
         "w_e2": g["L0_attn_We2"], "b_e2": g["L0_attn_be2"], "w_r": g["L0_ffn_Wr"],
         "w1": g["L0_ffn_W1"], "b1": g["L0_ffn_b1"], "w2": g["L0_ffn_W2"], "b2": g["L0_ffn_b2"]}
    d.update(constants())
    return {n: np.ascontiguousarray(a) for n, a in d.items()}


def kernel(**inputs):
    import concourse.bacc as bacc
    from concourse.bass_utils import run_bass_kernel_spmd

    arrays = layout(inputs)
    nc = bacc.Bacc("TRN2", target_bir_lowering=False, num_devices=1)
    aps = {n: nc.dram_tensor("in_" + n, a.shape, mybir.dt.from_np(a.dtype), kind="ExternalInput").ap()
           for n, a in arrays.items()}
    out = nc.dram_tensor("out", (B, L, DM), F32, kind="ExternalOutput").ap()
    build(nc, aps, out)
    r = run_bass_kernel_spmd(nc, [{"in_" + n: a for n, a in arrays.items()}], core_ids=[0])
    return r.results[0]["out"]
```

```python
import numpy as np
import concourse.bass as bass
from concourse import mybir
from contextlib import ExitStack

F32 = mybir.dt.float32
BF16 = mybir.dt.bfloat16
I32 = mybir.dt.int32
ALU = mybir.AluOpType
ACT = mybir.ActivationFunctionType
AX = mybir.AxisListType

B, L, C = 16, 512, 64
D = C // 8
P = 128
NC = L // P
DM = 2 * C
NA = 4
HID, DA = 256, 64
E, F, CAP = 8, 512, 1024
NF = F // P
ROWS = P // NC
TW = DM + E
SEARCH_BITS = 30
LO, HI = 16, CAP // 16
EPS = 1e-5
SC_T = float(D) ** -0.5

SLOT_ROW = [0, 8, 16, 24, 40, 48]
Q_PART = [1, 1, 2, 1, 3, 2]
K_PART = [1, 2, 1, 3, 1, 2]
MAX_ROW = 32


ORDER_TEXT = {
    "pe": """
P1.7@1 M_HIDK.0 M_LGT.0@-2 A_P.0@2 M_HIDK.1 M_HIDE.0 AUG.0@1 M_KQ.0 AUG.1@1 M_HIDE.1 P2.0@1
A_P.1@2 P2.1@1 P2.2@1 M_S1.0 P2.3@1 A_P.2@2 P2.4@1 P2.5@1 M_E.0 P2.6@1 P2.7@1 A_P.3@2 M_S1.1
M_E.1 PV.0@1 P1.0@2 P1.1@2 PV.1@1 P1.2@2 M_ROW.0@-1 M_TR.0 P1.3@2 M_TR.1 OT.0@1 M_S1.2 M_S1.3
OT.1@1 V.0@2 M_TR.2 P1.4@2 P1.5@2 M_LG.0@-1 M_TR.3 V.1@2 M_PV.0 M_XNT.0@1 P1.6@2
""",
    "act": """
M_HIDK.0 EX.6@1 M_HIDK.1 A_P.0@2 EX.7@1 AUG.0@1 AUG.1@1 P2.0@1 A_P.1@2 P2.1@1 P2.2@1 P2.3@1
A_P.2@2 P2.4@1 P2.5@1 A_R.0@2 M_EX.0 P2.6@1 P2.7@1 A_P.3@2 A_R.1@2 A_R.2@2 A_R.3@2 M_EX.1 PV.0@1
EX.0@2 EX.1@2 PV.1@1 M_ROW.0@-1 M_TR.0 EX.2@2 M_TR.1 EX.3@2 M_EX.2 V.0@2 M_EX.3 M_TR.2 M_LG.0@-1
M_TR.3 EX.4@2 EX.5@2 M_XNT.0@1 V.1@2
""",
    "dve": """
M_LGT.0@-2 MAX.0@1 A_P.0@2 M_HIDE.0 RD.0@1 M_LN2.0@-1 M_KQ.0 M_HIDE.1 A_P.1@2 M_S1.0 M_XN2.0@-1
A_P.2@2 M_E.0 A_R.0@2 M_S1.1 A_P.3@2 A_R.1@2 A_R.2@2 A_R.3@2 M_E.1 PV.0@1 P1.0@2 P1.1@2 PV.1@1
P1.2@2 M_TR.0 P1.3@2 M_TR.1 OT.0@1 M_S1.2 M_S1.3 OT.1@1 M_TR.2 M_LN.0@1 P1.4@2 M_TR.3 P1.5@2
M_XN.0@1 M_PV.0 P1.6@2 P1.7@2
""",
    "pool": """
M_LN2.0@-1 M_HR.0 M_LN.0@1
""",
    "sp": """
M_LGT.0@-2 A_X.0@3 M_PV.0
""",
}


def read_order(text):
    steps = []
    for word in text.split():
        step, _, off = word.partition("@")
        name, k = step.split(".")
        steps.append((name, int(k), int(off or 0)))
    return steps


ORDERS = {engine: read_order(text) for engine, text in ORDER_TEXT.items()}


def constants():
    c = {}
    c["ident"] = np.eye(P, dtype=np.float32)
    cf = np.zeros((P, 5), np.float32)
    for h in range(2):
        for s, r in enumerate(SLOT_ROW):
            rows = slice(64 * h + r, 64 * h + r + D)
            cf[rows, 0] = -1.0 * (Q_PART[s] > 1)
            cf[rows, 1] = -1.0 * (Q_PART[s] > 2)
            cf[rows, 2] = -1.0 * (K_PART[s] > 1)
            cf[rows, 3] = -1.0 * (K_PART[s] > 2)
        rows = slice(64 * h + MAX_ROW, 64 * h + MAX_ROW + 3)
        cf[rows, 2] = 1.0
        cf[rows, 4] = 1.0
    c["coef"] = cf
    p = np.arange(P)
    same = (p[:, None] % E == p[None, :] % E)
    c["group"] = same.astype(np.float32)
    c["before"] = (same & (p[:, None] < p[None, :])).astype(np.float32)
    c["expert"] = (p[:, None] % E == np.arange(E)[None, :]).astype(np.float32)
    col = np.arange(NC)[None, :, None] + NC * np.arange(B)[None, None, :] + np.zeros((E, 1, 1))
    c["tok_col"] = np.tile(col.astype(np.float32).reshape(1, -1), (P, 1))
    c["tok_row"] = p.astype(np.float32)[:, None]
    steps = np.array([[k << (SEARCH_BITS - 2 * i - 2) for k in (1, 2, 3)]
                      for i in range(SEARCH_BITS // 2)], np.int32)
    c["two_bits"] = np.tile(steps.reshape(1, -1), (P, 1))
    return c


def build(nc, A, out):
    lg_d = nc.dram_tensor("logits_scratch", (B, E, L), F32).ap()
    tab_d = nc.dram_tensor("table_scratch", (B * L, TW), F32).ap()

    ctx = ExitStack()
    with ctx:
        own = [ctx, ctx.enter_context(ExitStack())]

        def sb(name, shape, dt=F32, keep=False):
            return own[0 if keep else 1].enter_context(nc.sbuf_tensor(name, shape, dt))

        def pb(name, shape, dt=F32):
            return ctx.enter_context(nc.psum_tensor(name, shape, dt))

        def sem(name):
            return ctx.enter_context(nc.semaphore(name))

        ident = sb("ident_sb", [P, P], keep=True)
        nmx8 = sb("nmx8", [P, E], keep=True)
        rz8 = sb("rz8", [P, E], keep=True)
        w1 = [sb(f"w1_{s}", [P, F], keep=True) for s in range(2)]
        w2 = [sb(f"w2_{s}", [P, NF, DM], keep=True) for s in range(2)]
        b1 = [sb(f"b1_{s}", [P, NF], keep=True) for s in range(2)]
        b2 = [sb(f"b2_{s}", [P, DM], keep=True) for s in range(2)]
        NT = CAP // L
        idx = sb("idx", [P, E, NT, NC], I32, keep=True)
        group, before, expert, tok_col, tok_row = (
            sb(n + "_sb", list(A[n].shape), keep=True)
            for n in ("group", "before", "expert", "tok_col", "tok_row"))
        two_bits = sb("two_bits_sb", list(A["two_bits"].shape), I32, keep=True)
        lgs = sb("lgs", [P, L], keep=True)
        identb = sb("identb", [P, P], BF16)
        coef = sb("coef_sb", [P, 5])
        w_stack = sb("w_stack", [P, 4, P])
        w_v = sb("w_v", [P, NA * C])
        mixw = sb("mixw", [P, 2])
        w_in = sb("w_in", [P, 2 * HID])
        b_in = sb("b_in", [P, 4])
        w_kq = sb("w_kq", [P, 2, 2 * DA])
        b_kq = sb("b_kq", [P, 1])
        w_e2 = sb("w_e2", [P, 2, DM])
        b_e2 = sb("b_e2", [P, DM])
        w_r = sb("w_r", [P, ROWS])
        half_m = sb("half_m", [P, NC])

        xT = sb("xT", [P, L])
        part1 = sb("part1", [P, 4, L], BF16)
        rest = sb("rest", [P, 4, L])
        part2 = sb("part2", [P, 4, L], BF16)
        q_st = sb("q_st", [P, NA, L], BF16)
        k_st = sb("k_st", [P, 2, L], BF16)
        v_sb = sb("v_sb", [P, NC, NA, C])
        nmax = sb("nmax", [P, NC * NA])
        nrest = sb("nrest", [P, NC * NA])
        nbias = sb("nbias", [P, NC * NA])
        exps = sb("exps", [P, 4, L])
        den = sb("den", [P, NC, NA])
        nm_st = sb("nm_st", [P, NC * NA, 64], BF16)
        pT = sb("pT", [P, NC, NA, L])
        rden = sb("rden", [P, NC, NA])
        oT = sb("oT", [P, 2, L])
        o_n = sb("o_n", [P, 2, 2, NA, C])
        h_sb = sb("h_sb", [P, NC, DM])
        h_res = sb("h_res", [P, NC, DM])

        stats = sb("stats", [P, NC, 6])
        mv = sb("mv", [P, NC, 2])
        var = sb("var", [P, NC])
        rstd = sb("rstd", [P, NC])
        xn = sb("xn", [P, NC, DM])
        xnT = sb("xnT", [P, L])
        hid = sb("hid", [P, 4, L])
        kT = sb("kT", [P, L])
        qT = sb("qT", [P, L])
        e_sb = sb("e_sb", [P, NC, DM])
        nmax2 = sb("nmax2", [P, NC])
        probs2 = sb("probs2", [P, NC, L])
        p2T = sb("p2T", [P, NC, L])
        den2 = sb("den2", [P, NC])
        rden2 = sb("rden2", [P, NC])
        h2 = sb("h2", [P, NC, DM])
        stats2 = sb("stats2", [P, NC, 6])
        mv2 = sb("mv2", [P, NC, 2])
        var2 = sb("var2", [P, NC])
        rstd2 = sb("rstd2", [P, NC])
        row = sb("row", [P, NC, TW])
        rowT = sb("rowT", [P, L])
        lgT = sb("lgT", [P, P])

        s_ps = [pb(f"scores{i}", [P, 2, L]) for i in range(2)]
        t_ps = [pb(f"tmisc{i}", [P, L]) for i in range(2)]
        m_ps = [pb(f"mmisc{i}", [P, L]) for i in range(2)]

        const_in = sem("const_in")
        mlp_in = sem("mlp_in")
        pool_const = sem("pool_const")
        act_const = sem("act_const")
        pool_waits = sem("pool_waits")
        dve_waits = sem("dve_waits")
        sp_waits = sem("sp_waits")
        x_in = sem("x_in")
        s_full = sem("s_full")
        t_full = sem("t_full")
        m_full = sem("m_full")
        part1_ok = sem("part1_ok")
        rest_ok = sem("rest_ok")
        part2_ok = sem("part2_ok")
        stack_ok = sem("stack_ok")
        v_ok = sem("v_ok")
        max_st = sem("max_st")
        bias_ok = sem("bias_ok")
        sum_ok = sem("sum_ok")
        rden_ok = sem("rden_ok")
        oT_act = sem("oT_act")
        oT_dve = sem("oT_dve")
        tmax_ok = sem("tmax_ok")
        nm_ok = sem("nm_ok")
        qmax_ok = sem("qmax_ok")
        p_ok = sem("p_ok")
        comb_st = sem("comb_st")
        hres_ok = sem("hres_ok")
        ln_st = sem("ln_st")
        var_ok = sem("var_ok")
        rstd_ok = sem("rstd_ok")
        xn_ok = sem("xn_ok")
        xnT_ok = sem("xnT_ok")
        hidk_ok = sem("hidk_ok")
        hide_ok = sem("hide_ok")
        kq_ok = sem("kq_ok")
        e_ok = sem("e_ok")
        nmax2_ok = sem("nmax2_ok")
        p2_ok = sem("p2_ok")
        p2T_act = sem("p2T_act")
        p2T_dve = sem("p2T_dve")
        out2_st = sem("out2_st")
        h2_ok = sem("h2_ok")
        ln2_st = sem("ln2_st")
        var2_ok = sem("var2_ok")
        rstd2_ok = sem("rstd2_ok")
        xn2_ok = sem("xn2_ok")
        rowT_ok = sem("rowT_ok")
        rowlg_ok = sem("rowlg_ok")
        lgT_ok = sem("lgT_ok")
        h2_out = sem("h2_out")
        row_out = sem("row_out")
        lgT_out = sem("lgT_out")

        sel_in = sem("sel_in")
        N_SEL = 16 * 6

        order = ORDERS

        ring = {"A_P": "T", "V": "T", "AUG": "T", "PV": "T", "OT": "T", "P1": "S", "P2": "S"}
        for name in ("M_XNT", "M_HIDK", "M_HIDE", "M_KQ", "M_E", "M_S1", "M_TR", "M_PV",
                     "M_ROW", "M_LG", "M_LGT"):
            ring[name] = "M"
        offsets = {(name, k): off for name, k, off in order["pe"]}
        all_offsets = [off for steps in order.values() for _, _, off in steps]
        OFF_MAX, OFF_MIN = max(all_offsets), min(all_offsets)
        LOOP_FIRST, LOOP_END = 1 - OFF_MIN, B - OFF_MAX
        bank_of, uses, ring_place, earlier = {}, {"T": 0, "S": 0, "M": 0}, {}, {}
        for name, k, _ in order["pe"]:
            if name in ring:
                bank_of[name, k] = uses[ring[name]] % 2
                uses[ring[name]] += 1
        count_of, last_in = {"T": 0, "S": 0, "M": 0}, {}
        for turn in range(-OFF_MAX, B - OFF_MIN):
            for name, k, off in order["pe"]:
                t = turn + off
                if name in ring and 0 <= t < B:
                    r = ring[name]
                    ring_place[name, k, t] = count_of[r]
                    count_of[r] += 1
                    earlier[name, k, t] = last_in.get((r, bank_of[name, k]))
                    last_in[r, bank_of[name, k]] = (name, k, t)

        def filled(name, t, k):
            if isinstance(t, int):
                return ring_place[name, k, t] + 1
            ref = LOOP_FIRST + offsets[name, k]
            n = uses[ring[name]]
            return t * n + (ring_place[name, k, ref] + 1 - n * ref)

        def use_before(name, t, k):
            if isinstance(t, int):
                return earlier[name, k, t]
            ref = LOOP_FIRST + offsets[name, k]
            other, k2, t2 = earlier[name, k, ref]
            return other, k2, t + (t2 - ref)

        def run_all(eng, which, steps):
            def turn(i):
                for name, k, off in order[which]:
                    t = i + off
                    if name in steps and not (isinstance(t, int) and not 0 <= t < B):
                        steps[name](t, k)
            for i in range(-OFF_MAX, LOOP_FIRST):
                turn(i)
            with eng.Fori(LOOP_FIRST, LOOP_END) as i:
                turn(i)
            for i in range(LOOP_END, B - OFF_MIN):
                turn(i)

        w_in_s = [sem(f"w_in{s}") for s in range(2)]

        def load_expert(sp, e, s):
            with nc.allow_non_contiguous_dma(reason="biases"):
                for dst, src in (
                    (w1[s][:, :], A["w1"][bass.ds(e, 1), :, :].rearrange("a d f -> (a d) f")),
                    (w2[s][:, :, :], A["w2"][bass.ds(e, 1), :, :]
                     .rearrange("a (f p) d -> p (a f) d", p=P)),
                    (b1[s][:, :], A["b1"][bass.ds(e, 1), :].rearrange("a (f p) -> p (a f)", p=P)),
                    (b2[s][:, :], A["b2"][bass.ds(e, 1), :].to_broadcast([P, DM])),
                ):
                    sp.dma_start(dst, src).then_inc(w_in_s[s], 16)

        first_block = ExitStack()
        block = first_block.enter_context(nc.Block())

        N_EARLY, N_CONST, N_MLP = 16 * 2, 16 * 6, 16 * 7

        @block.sync
        def _(sp):
            def load(sem_in, pairs):
                for dst, src in pairs:
                    with nc.allow_non_contiguous_dma(reason="biases, once"):
                        sp.dma_start(dst, src).then_inc(sem_in, 16)

            load(const_in, (
                (ident[:, :], A["ident"]),
                (w_stack[:, :, :], A["w_stack"].rearrange("j p n -> p j n"))))

            def load_rest():
                load(const_in, (
                    (coef[:, :], A["coef"]), (w_v[:, :], A["w_v"]),
                    (mixw[:, 0:1],
                     A["alpha"].rearrange("(a n) -> a n", a=1).to_broadcast([P, 1])),
                    (mixw[:, 1:2],
                     A["gamma"].rearrange("(a n) -> a n", a=1).to_broadcast([P, 1]))))
                load(mlp_in, (
                    (w_in[:, :], A["w_in"]),
                    (b_in[:, :], A["b_in"].rearrange("(j p) -> p j", p=P)),
                    (w_kq[:, :, :], A["w_kq"].rearrange("(j p) n -> p j n", p=P)),
                    (b_kq[:, :], A["b_kq"].rearrange("(p a) -> p a", a=1)),
                    (w_e2[:, :, :], A["w_e2"].rearrange("(j p) n -> p j n", p=P)),
                    (b_e2[:, :], A["b_e2"].rearrange("(a n) -> a n", a=1).to_broadcast([P, DM])),
                    (w_r[:, :], A["w_r"])))

            def a_x(t, k):
                if not (isinstance(t, int) and t == 0):
                    for name, part in (("A_P", 3), ("V", 1)):
                        sp.wait_ge(t_full, filled(name, t - 1, part))
                        sp.sem_inc(sp_waits, 1)
                sp.dma_start(xT[:, :], A["x"][bass.ds(t, 1), :, :].rearrange("a n l -> (a n) l"))\
                    .then_inc(x_in, 16)
                if isinstance(t, int) and t == 0:
                    load_rest()

            def m_pv(m, k):
                sp.wait_ge(h2_ok, m * NC + NC)
                sp.sem_inc(sp_waits, 1)
                dst = out[bass.ds(m, 1), :, :].rearrange("a (c p) n -> p (a c) n", p=P)
                sp.dma_start(dst, h2[:, :, :]).then_inc(h2_out, 16)

            def load_later_parts():
                for dst, n in ((group, "group"), (before, "before"), (expert, "expert"),
                               (two_bits, "two_bits"), (tok_col, "tok_col"),
                               (tok_row, "tok_row")):
                    with nc.allow_non_contiguous_dma(reason="one column, once"):
                        sp.dma_start(dst[:, :], A[n]).then_inc(sel_in, 16)
                for e in range(2):
                    load_expert(sp, e, e)

            def m_lgt(m, k):
                if isinstance(m, int) and m == 0:
                    load_later_parts()
                sp.wait_ge(xn2_ok, m * NC + NC)
                sp.sem_inc(sp_waits, 1)
                sp.wait_ge(rowlg_ok, m + 1)
                sp.sem_inc(sp_waits, 1)
                dst = tab_d[bass.ds(m * L, L), :].rearrange("(c p) n -> p c n", p=P)
                sp.dma_start(dst, row[:, :, :]).then_inc(row_out, 16)
                sp.wait_ge(lgT_ok, m + 1)
                sp.sem_inc(sp_waits, 1)
                for j in range(NC):
                    sp.dma_start(lg_d[bass.ds(m, 1), :, j * P:(j + 1) * P]
                                 .rearrange("a e t -> (a e) t"), lgT[j * ROWS:j * ROWS + E, :])\
                        .then_inc(lgT_out, 16)

            run_all(sp, "sp", {"A_X": a_x, "M_PV": m_pv, "M_LGT": m_lgt})
            sp.wait_ge(lgT_out, 16 * NC * B)
            sp.dma_start(lgs[0:B * E, :], lg_d.rearrange("b e t -> (b e) t")).then_inc(sel_in, 16)

        @block.gpsimd
        def _(pool):
            nc.gpsimd.memset(half_m[:, :], -0.5).then_inc(pool_const, 1)
            nc.gpsimd.memset(nm_st[:, :, :], 0.0).then_inc(pool_const, 1)
            nc.gpsimd.memset(q_st[:, :, :], 0.0).then_inc(pool_const, 1)
            pool.wait_ge(pool_const, 3)
            nc.gpsimd.memset(kT[DA:P, :], 0.0).then_inc(pool_const, 1)
            nc.gpsimd.memset(qT[DA:P, :], 0.0).then_inc(pool_const, 1)

            def own_wait():
                pool.sem_inc(pool_waits, 1)

            def rsqrt(v, r, v_ok, r_ok, m):
                pool.wait_ge(v_ok, m + 1)
                own_wait()
                nc.gpsimd.tensor_scalar(r[:, :], v[:, :], EPS, 1.0, ALU.add, ALU.mult)\
                    .then_inc(r_ok, 1)
                pool.wait_ge(r_ok, m * 2 + 1)
                nc.gpsimd.tensor_tensor(r[:, :], r[:, :], half_m[:, :], ALU.pow).then_inc(r_ok, 1)

            def m_ln1(m, k):
                rsqrt(var, rstd, var_ok, rstd_ok, m)

            def m_hr(m, k):
                pool.wait_ge(comb_st, (m + 1) * 4)
                own_wait()
                if not (isinstance(m, int) and m == 0):
                    pool.wait_ge(h2_ok, m * NC)
                    own_wait()
                nc.gpsimd.tensor_copy(h_res[:, :, :], h_sb[:, :, :]).then_inc(hres_ok, 1)

            def m_row(m, k):
                rsqrt(var2, rstd2, var2_ok, rstd2_ok, m)

            run_all(pool, "pool", {"M_LN": m_ln1, "M_LN2": m_row, "M_HR": m_hr})

        @block.scalar
        def _(act):
            act.wait_ge(const_in, N_EARLY)
            act.wait_ge(pool_const, 5)

            def full(name, t, k):
                r = ring[name]
                act.wait_ge({"T": t_full, "S": s_full, "M": m_full}[r], filled(name, t, k))
                return {"T": t_ps, "S": s_ps, "M": m_ps}[r][bank_of[name, k]]

            def a_p(t, k):
                ps = full("A_P", t, k)
                if k < 2:
                    nc.scalar.copy(part1[:, k, :], ps[:, :]).then_inc(part1_ok, 1)
                else:
                    nc.scalar.activation(part1[:, k, :], ps[:, :], ACT.Identity,
                                         bias=coef[:, 4:5]).then_inc(part1_ok, 1)

            def scale_v_weights():
                act.wait_ge(const_in, N_CONST)
                for j in range(2):
                    w = w_v[:, (2 + j) * C:(3 + j) * C]
                    nc.scalar.mul(w, w, mixw[:, j:j + 1]).then_inc(act_const, 1)
                nc.scalar.copy(identb[:, :], ident[:, :]).then_inc(act_const, 1)

            def a_r(t, k):
                if k == 0 and isinstance(t, int) and t == 0:
                    scale_v_weights()
                act.wait_ge(rest_ok, t * 4 + k + 1)
                nc.scalar.copy(part2[:, k, :], rest[:, k, :]).then_inc(part2_ok, 1)

            def v(t, k):
                ps = full("V", t, k)
                src = ps[:, :].rearrange("p (c a n) -> p c a n", c=2, a=NA)
                for c in range(2):
                    nc.scalar.copy(v_sb[:, 2 * k + c, :, 0:C], src[:, c]).then_inc(v_ok, 1)

            def aug(t, pair):
                ps = full("AUG", t, pair)
                for h in range(2):
                    r = slice(64 * h + MAX_ROW, 64 * h + MAX_ROW + 3)
                    nc.scalar.copy(q_st[r, 2 * pair + h, :], ps[r, :]).then_inc(qmax_ok, 1)

            def ex(t, k):
                qc, pair = k // 2, k % 2
                ps = full("P1", t, k)
                if k == 0 and not (isinstance(t, int) and t == 0):
                    act.wait_ge(rden_ok, t)
                act.wait_ge(bias_ok, t * 2 * NC + k + 1)
                for h in range(2):
                    a = 2 * pair + h
                    if not (isinstance(t, int) and t == 0 and k < 2):
                        act.wait_ge(sum_ok, t * 4 * NC + 2 * k + h - 3)
                    nc.scalar.activation(
                        exps[:, 2 * (k % 2) + h, :], ps[:, h, :], ACT.Exp, scale=SC_T,
                        bias=nbias[:, NA * qc + a:NA * qc + a + 1],
                        accum_out=den[:, qc, a:a + 1]).then_inc(sum_ok, 1)

            def pv(t, k):
                if k == 0:
                    ps = full("PV", t, k)
                    nc.scalar.copy(oT[:, 0, :], ps[:, :]).then_inc(oT_act, 1)

            def p2(t, k):
                kc, pair = k // 2, k % 2
                ps = full("P2", t, k)
                nc.scalar.activation(pT[:, kc, 2 * pair:2 * pair + 2, :], ps[:, :, :], ACT.Exp,
                                     scale=SC_T).then_inc(p_ok, 1)

            def m_xnt(m, k):
                ps = full("M_XNT", m, k)
                nc.scalar.copy(xnT[:, :], ps[:, :]).then_inc(xnT_ok, 1)

            def m_hidk(m, k):
                if isinstance(m, int) and m == 0:
                    act.wait_ge(mlp_in, N_MLP)
                ps = full("M_HIDK", m, k)
                nc.scalar.activation(hid[:, 2 + k, :], ps[:, :], ACT.Relu,
                                     bias=b_in[:, 2 + k:3 + k]).then_inc(hidk_ok, 1)

            def m_ex(m, qc):
                ps = full("M_S1", m, qc)
                act.wait_ge(nmax2_ok, m * NC + qc + 1)
                nc.scalar.activation(probs2[:, qc, :], ps[:, :], ACT.Exp, bias=nmax2[:, qc:qc + 1],
                                     accum_out=den2[:, qc:qc + 1]).then_inc(p2_ok, 1)

            def m_tr(m, qc):
                if qc % 2 == 0:
                    ps = full("M_TR", m, qc)
                    nc.scalar.copy(p2T[:, :, qc * P:(qc + 1) * P],
                                   ps[:, :].rearrange("p (c n) -> p c n", c=NC))\
                        .then_inc(p2T_act, 1)

            def m_row(m, k):
                ps = full("M_ROW", m, k)
                nc.scalar.copy(rowT[:, :], ps[:, :]).then_inc(rowT_ok, 1)

            def m_lg(m, k):
                ps = full("M_LG", m, k)
                if not (isinstance(m, int) and m == 0):
                    act.wait_ge(lgT_out, m * NC * 16)
                nc.scalar.copy(lgT[:, :], ps[:, 0:P]).then_inc(lgT_ok, 1)

            run_all(act, "act", {
                "A_P": a_p, "A_R": a_r, "V": v, "EX": ex, "AUG": aug, "P2": p2, "PV": pv,
                "M_XNT": m_xnt,
                "M_HIDK": m_hidk, "M_EX": m_ex, "M_TR": m_tr, "M_ROW": m_row, "M_LG": m_lg})

        @block.vector
        def _(dve):
            dve.wait_ge(const_in, N_CONST)
            dve.wait_ge(pool_const, 5)

            def full(name, t, k):
                r = ring[name]
                dve.wait_ge({"T": t_full, "S": s_full, "M": m_full}[r], filled(name, t, k))
                return {"T": t_ps, "S": s_ps, "M": m_ps}[r][bank_of[name, k]]

            def a_p(t, k):
                co = 0 if k < 2 else 2
                dve.wait_ge(part1_ok, t * 4 + k + 1)
                nc.vector.scalar_tensor_tensor(
                    out=rest[:, k, :], in0=part1[:, k, :], scalar=coef[:, co:co + 1],
                    in1=t_ps[bank_of["A_P", k]][:, :], op0=ALU.mult, op1=ALU.add)\
                    .then_inc(rest_ok, 1)

            def a_r(t, k):
                co = 0 if k < 2 else 2
                dve.wait_ge(part2_ok, t * 4 + k + 1)
                if not (isinstance(t, int) and t == 0):
                    dve.wait_ge(s_full, filled("P2", t - 1, 2 * NC - 1))
                if k < 2:
                    for h in range(2):
                        r = slice(64 * h, 64 * h + 64)
                        nc.vector.scalar_tensor_tensor(
                            out=q_st[r, 2 * k + h, :], in0=part2[r, k, :],
                            scalar=coef[r, co + 1:co + 2], in1=rest[r, k, :], op0=ALU.mult,
                            op1=ALU.add).then_inc(stack_ok, 1)
                else:
                    nc.vector.scalar_tensor_tensor(
                        out=k_st[:, k - 2, :], in0=part2[:, k, :], scalar=coef[:, co + 1:co + 2],
                        in1=rest[:, k, :], op0=ALU.mult, op1=ALU.add).then_inc(stack_ok, 1)

            def p1(t, k):
                qc, pair = k // 2, k % 2
                ps = full("P1", t, k)
                at = NA * qc + 2 * pair
                nc.vector.tensor_reduce(nmax[:, at:at + 2], ps[:, :, :], AX.X, ALU.max,
                                        negate=True).then_inc(max_st, 1)
                dve.wait_ge(max_st, t * 2 * NC + k + 1)
                nc.vector.tensor_scalar(nbias[:, at:at + 2], nmax[:, at:at + 2], SC_T, None,
                                        ALU.mult).then_inc(bias_ok, 1)

            def rd(t, k):
                dve.wait_ge(sum_ok, (t + 1) * 4 * NC)
                nc.vector.reciprocal(rden[:, :, :], den[:, :, :]).then_inc(rden_ok, 1)

            def max_split(t, k):
                st = t * 3
                dve.wait_ge(max_st, (t + 1) * 2 * NC)
                nc.vector.tensor_copy(nm_st[:, :, MAX_ROW], nmax[:, :]).then_inc(tmax_ok, 1)
                dve.wait_ge(tmax_ok, st + 1)
                nc.vector.tensor_tensor(nrest[:, :], nmax[:, :], nm_st[:, :, MAX_ROW],
                                        ALU.subtract).then_inc(tmax_ok, 1)
                dve.wait_ge(tmax_ok, st + 2)
                nc.vector.tensor_copy(nm_st[:, :, MAX_ROW + 1], nrest[:, :]).then_inc(tmax_ok, 1)
                dve.wait_ge(tmax_ok, st + 3)
                nc.vector.tensor_tensor(nm_st[:, :, MAX_ROW + 2], nrest[:, :],
                                        nm_st[:, :, MAX_ROW + 1], ALU.subtract).then_inc(nm_ok, 1)

            def pv(t, k):
                if k == 1:
                    ps = full("PV", t, k)
                    nc.vector.tensor_copy(oT[:, 1, :], ps[:, :]).then_inc(oT_dve, 1)

            def ot(t, k):
                if k == 0:
                    dve.wait_ge(rden_ok, t + 1)
                    if not (isinstance(t, int) and t == 0):
                        dve.wait_ge(hres_ok, t)
                ps = full("OT", t, k)
                st = t * 4 + 2 * k
                nc.vector.tensor_tensor(
                    o_n[:, k, :, :, :], ps[:, :].rearrange("p (q a n) -> p q a n", q=2, a=NA),
                    rden[:, 2 * k:2 * k + 2, :].rearrange("p q (a n) -> p q a n", n=1)
                    .to_broadcast([P, 2, NA, C]), ALU.mult).then_inc(comb_st, 1)
                dve.wait_ge(comb_st, st + 1)
                on = o_n[:, k, :, :, :].rearrange("p q a n -> p q (a n)")
                nc.vector.tensor_tensor(h_sb[:, 2 * k:2 * k + 2, :], on[:, :, 0:DM],
                                        on[:, :, DM:2 * DM], ALU.add).then_inc(comb_st, 1)

            def statistics(m, src, st_t, mv_t, var_t, st, var_sem):
                for c in range(NC):
                    nc.vector.bn_stats(st_t[:, c, :], src[:, c, :]).then_inc(st, 1)
                for c in range(NC):
                    dve.wait_ge(st, m * 2 * NC + c + 1)
                    dve.sem_inc(dve_waits, 1)
                    nc.vector.bn_aggr(mv_t[:, c, :], st_t[:, c, :]).then_inc(st, 1)
                dve.wait_ge(st, m * 2 * NC + 2 * NC)
                nc.vector.tensor_copy(var_t[:, :], mv_t[:, :, 1]).then_inc(var_sem, 1)

            def normalise(m, src, mv_t, rstd_t, rstd_sem, outs, out_sem):
                dve.wait_ge(rstd_sem, m * 2 + 2)
                for c in range(NC):
                    nc.vector.tensor_scalar(outs[:, c, 0:DM], src[:, c, :], mv_t[:, c, 0:1],
                                            rstd_t[:, c:c + 1], ALU.subtract, ALU.mult)\
                        .then_inc(out_sem, 1)

            def m_ln(m, k):
                dve.wait_ge(comb_st, (m + 1) * 4)
                statistics(m, h_sb, stats, mv, var, ln_st, var_ok)

            def m_xn(m, k):
                normalise(m, h_sb, mv, rstd, rstd_ok, xn, xn_ok)

            def m_hide(m, k):
                if isinstance(m, int) and m == 0:
                    dve.wait_ge(mlp_in, N_MLP)
                ps = full("M_HIDE", m, k)
                nc.vector.tensor_scalar(hid[:, k, :], ps[:, :], b_in[:, k:k + 1], 0.0,
                                        ALU.add, ALU.max).then_inc(hide_ok, 1)

            def m_kq(m, k):
                ps = full("M_KQ", m, k)
                for dst, r in ((kT, slice(0, DA)), (qT, slice(DA, 2 * DA))):
                    nc.vector.tensor_scalar(dst[0:DA, :], ps[r, :], b_kq[r, :], None,
                                            ALU.add).then_inc(kq_ok, 1)

            def m_e(m, k):
                ps = full("M_E", m, k)
                nc.vector.tensor_tensor(
                    e_sb[:, 2 * k:2 * k + 2, 0:DM],
                    ps[:, 0:2 * DM].rearrange("p (c n) -> p c n", n=DM),
                    b_e2[:, :].rearrange("p (a n) -> p a n", a=1).to_broadcast([P, 2, DM]),
                    ALU.add).then_inc(e_ok, 1)

            def m_s1(m, qc):
                ps = full("M_S1", m, qc)
                nc.vector.tensor_reduce(nmax2[:, qc:qc + 1], ps[:, :], AX.X, ALU.max,
                                        negate=True).then_inc(nmax2_ok, 1)

            def m_tr(m, qc):
                if qc % 2 == 1:
                    ps = full("M_TR", m, qc)
                    nc.vector.tensor_copy(p2T[:, :, qc * P:(qc + 1) * P],
                                          ps[:, :].rearrange("p (c n) -> p c n", c=NC))\
                        .then_inc(p2T_dve, 1)

            def m_pv(m, k):
                dve.wait_ge(p2_ok, (m + 1) * NC)
                nc.vector.reciprocal(rden2[:, :], den2[:, :]).then_inc(out2_st, 1)
                ps = full("M_PV", m, k)
                dve.wait_ge(out2_st, m + 1)
                dve.wait_ge(hres_ok, m + 1)
                if not (isinstance(m, int) and m == 0):
                    dve.wait_ge(h2_out, m * 16)
                for c in range(NC):
                    nc.vector.scalar_tensor_tensor(
                        out=h2[:, c, :], in0=ps[:, c * DM:(c + 1) * DM],
                        scalar=rden2[:, c:c + 1], in1=h_res[:, c, :], op0=ALU.mult,
                        op1=ALU.add).then_inc(h2_ok, 1)

            def m_ln2(m, k):
                dve.wait_ge(h2_ok, m * NC + NC)
                statistics(m, h2, stats2, mv2, var2, ln2_st, var2_ok)

            def m_xn2(m, k):
                if not (isinstance(m, int) and m == 0):
                    dve.wait_ge(row_out, m * 16)
                normalise(m, h2, mv2, rstd2, rstd2_ok, row, xn2_ok)

            def m_lgt(m, k):
                ps = full("M_LGT", m, k)
                nc.vector.tensor_copy(row[:, :, DM:TW], ps[:, 0:P]
                                      .rearrange("p (c r) -> p c r", r=ROWS)[:, :, 0:E])\
                    .then_inc(rowlg_ok, 1)

            run_all(dve, "dve", {
                "A_P": a_p, "A_R": a_r, "P1": p1, "MAX": max_split, "RD": rd, "PV": pv,
                "OT": ot, "M_LN": m_ln,
                "M_XN": m_xn, "M_HIDE": m_hide, "M_KQ": m_kq, "M_E": m_e, "M_S1": m_s1,
                "M_TR": m_tr, "M_PV": m_pv, "M_LN2": m_ln2, "M_XN2": m_xn2, "M_LGT": m_lgt})

        @block.tensor
        def _(pe):
            pe.wait_ge(const_in, N_EARLY)
            pe.wait_ge(pool_const, 5)

            def transposes(ps, parts, n=P):
                for j, src in enumerate(parts):
                    last = nc.tensor.transpose(ps[:, j * n:(j + 1) * n], src, ident[:, :])
                return last

            def slot(name, t, k, known=None):
                last = use_before(name, t, k)
                if last is not None and last[0] != known:
                    of, n, b = last
                    reader = {
                        "A_P": (rest_ok, b * 4 + n + 1),
                        "V": (v_ok, b * 4 + 2 * n + 2), "AUG": (qmax_ok, b * 4 + 2 * n + 2),
                        "PV": (oT_dve if n else oT_act, b + 1),
                        "OT": (comb_st, b * 4 + 2 * n + 1),
                        "P1": (sum_ok, b * 4 * NC + 2 * n + 2), "P2": (p_ok, b * 2 * NC + n + 1),
                        "M_XNT": (xnT_ok, b + 1), "M_HIDK": (hidk_ok, b * 2 + n + 1),
                        "M_HIDE": (hide_ok, b * 2 + n + 1), "M_KQ": (kq_ok, b * 2 + 2),
                        "M_E": (e_ok, b * 2 + n + 1), "M_S1": (p2_ok, b * NC + n + 1),
                        "M_TR": ((p2T_dve if n % 2 else p2T_act), b * 2 + n // 2 + 1),
                        "M_PV": (h2_ok, (b + 1) * NC), "M_ROW": (rowT_ok, b + 1),
                        "M_LG": (lgT_ok, b + 1), "M_LGT": (rowlg_ok, b + 1)}[of]
                    pe.wait_ge(*reader)
                return {"T": t_ps, "S": s_ps, "M": m_ps}[ring[name]][bank_of[name, k]]

            def a_p(t, k):
                if k == 0:
                    pe.wait_ge(x_in, (t + 1) * 16)
                ps = slot("A_P", t, k)
                nc.tensor.matmul(ps[:, :], w_stack[:, k, :], xT[:, :], start=True, stop=True)\
                    .then_inc(t_full, 1)

            def v(t, k):
                if isinstance(t, int) and t == 0:
                    pe.wait_ge(act_const, 3)
                ps = slot("V", t, k)
                for c in range(2):
                    at = (2 * k + c) * P
                    last = nc.tensor.matmul(ps[:, c * 256:(c + 1) * 256], xT[:, at:at + P],
                                            w_v[:, :], start=True, stop=True)
                last.then_inc(t_full, 1)

            def p1(t, k):
                if k == 0:
                    pe.wait_ge(stack_ok, t * 6 + 6)
                qc, pair = k // 2, k % 2
                ps = slot("P1", t, k)
                for h in range(2):
                    last = nc.tensor.matmul(
                        ps[:, h, :], q_st[:, 2 * pair + h, qc * P:(qc + 1) * P],
                        k_st[:, pair, :], start=True, stop=True)
                last.then_inc(s_full, 1)

            def aug(t, pair):
                if pair == 0:
                    pe.wait_ge(nm_ok, t + 1)
                ps = slot("AUG", t, pair)
                for qc in range(NC):
                    at = NA * qc + 2 * pair
                    last = nc.tensor.matmul(
                        ps[:, qc * P:(qc + 1) * P],
                        nm_st[:, at:at + 2, :].rearrange("p a n -> p (a n)"), identb[:, :],
                        start=True, stop=True)
                last.then_inc(t_full, 1)

            def p2(t, k):
                kc, pair = k // 2, k % 2
                if kc == 0:
                    pe.wait_ge(qmax_ok, t * 4 + 2 * pair + 2)
                ps = slot("P2", t, k)
                for h in range(2):
                    last = nc.tensor.matmul(
                        ps[:, h, :], k_st[:, pair, kc * P:(kc + 1) * P],
                        q_st[:, 2 * pair + h, :], start=True, stop=True)
                last.then_inc(s_full, 1)

            def pv(t, pair):
                if pair == 0:
                    pe.wait_ge(p_ok, t * 8 + 8)
                    pe.wait_ge(v_ok, t * 4 + 4)
                ps = slot("PV", t, pair)
                for kc in range(NC):
                    for h in range(2):
                        a = 2 * pair + h
                        last = nc.tensor.matmul(
                            ps[h * C:(h + 1) * C, :], v_sb[:, kc, a, :], pT[:, kc, a, :],
                            start=kc == 0, stop=kc == NC - 1)
                last.then_inc(t_full, 1)

            def ot(t, k):
                if k == 0:
                    pe.wait_ge(oT_act, t + 1)
                    pe.wait_ge(oT_dve, t + 1)
                ps = slot("OT", t, k, known="PV")
                transposes(ps, [oT[:, pair, (2 * k + q) * P:(2 * k + q + 1) * P]
                                for q in range(2) for pair in range(2)]).then_inc(t_full, 1)

            def m_xnt(m, k):
                pe.wait_ge(xn_ok, m * NC + NC)
                ps = slot("M_XNT", m, 0)
                transposes(ps, [xn[:, c, :] for c in range(NC)]).then_inc(m_full, 1)

            def hidden(name, m, k, j):
                if isinstance(m, int) and m == 0:
                    pe.wait_ge(mlp_in, N_MLP)
                if k == 0:
                    pe.wait_ge(xnT_ok, m + 1)
                ps = slot(name, m, k)
                nc.tensor.matmul(ps[:, :], w_in[:, j * P:(j + 1) * P], xnT[:, :],
                                 start=True, stop=True).then_inc(m_full, 1)

            def m_hidk(m, k):
                hidden("M_HIDK", m, k, 2 + k)

            def m_hide(m, k):
                hidden("M_HIDE", m, k, k)

            def m_kq(m, k):
                pe.wait_ge(hidk_ok, m * 2 + 2)
                ps = slot("M_KQ", m, 0)
                for i in range(2):
                    last = nc.tensor.matmul(ps[:, :], w_kq[:, i, :], hid[:, 2 + i, :],
                                            start=i == 0, stop=i == 1)
                last.then_inc(m_full, 1)

            def m_e(m, k):
                if k == 0:
                    pe.wait_ge(hide_ok, m * 2 + 2)
                ps = slot("M_E", m, k)
                for j in range(2):
                    c = 2 * k + j
                    for i in range(2):
                        last = nc.tensor.matmul(ps[:, j * P:(j + 1) * P],
                                                hid[:, i, c * P:(c + 1) * P], w_e2[:, i, :],
                                                start=i == 0, stop=i == 1)
                last.then_inc(m_full, 1)

            def m_s1(m, qc):
                if qc == 0:
                    pe.wait_ge(kq_ok, m * 2 + 2)
                ps = slot("M_S1", m, qc)
                nc.tensor.matmul(ps[:, :], qT[:, qc * P:(qc + 1) * P], kT[:, :],
                                 start=True, stop=True).then_inc(m_full, 1)

            def m_tr(m, qc):
                of, n, _ = use_before("M_TR", m, qc)
                pe.wait_ge(p2_ok, m * NC + (max(n, qc) if of == "M_S1" else qc) + 1)
                ps = slot("M_TR", m, qc, known="M_S1")
                transposes(ps, [probs2[:, qc, c * P:(c + 1) * P] for c in range(NC)])\
                    .then_inc(m_full, 1)

            def m_pv(m, k):
                pe.wait_ge(e_ok, m * 2 + 2)
                of, n, _ = use_before("M_PV", m, k)
                pe.wait_ge(p2T_act, m * 2 + 2)
                if of == "M_TR" and n % 2 == 1:
                    pe.wait_ge(p2T_dve, m * 2 + 2)
                ps = slot("M_PV", m, k, known="M_TR")
                for qc in range(NC):
                    if qc % 2 == 1 and not (of == "M_TR" and n % 2 == 1):
                        pe.wait_ge(p2T_dve, m * 2 + qc // 2 + 1)
                    for kc in range(NC):
                        last = nc.tensor.matmul(ps[:, qc * DM:(qc + 1) * DM],
                                                p2T[:, kc, qc * P:(qc + 1) * P], e_sb[:, kc, :],
                                                start=kc == 0, stop=kc == NC - 1)
                last.then_inc(m_full, 1)

            def m_row(m, k):
                pe.wait_ge(xn2_ok, m * NC + NC)
                ps = slot("M_ROW", m, 0)
                transposes(ps, [row[:, c, 0:DM] for c in range(NC)]).then_inc(m_full, 1)

            def m_lg(m, k):
                pe.wait_ge(rowT_ok, m + 1)
                ps = slot("M_LG", m, 0)
                for j in range(NC):
                    last = nc.tensor.matmul(ps[j * ROWS:(j + 1) * ROWS, 0:P], w_r[:, :],
                                            rowT[:, j * P:(j + 1) * P], start=True, stop=True)
                last.then_inc(m_full, 1)

            def m_lgt(m, k):
                pe.wait_ge(lgT_ok, m + 1)
                ps = slot("M_LGT", m, 0)
                nc.tensor.transpose(ps[:, 0:P], lgT[:, :], ident[:, :]).then_inc(m_full, 1)

            run_all(pe, "pe", {
                "A_P": a_p, "V": v, "P1": p1, "AUG": aug, "P2": p2, "PV": pv,
                "OT": ot, "M_XNT": m_xnt, "M_HIDK": m_hidk, "M_HIDE": m_hide, "M_KQ": m_kq, "M_E": m_e,
                "M_S1": m_s1, "M_TR": m_tr, "M_PV": m_pv, "M_ROW": m_row,
                "M_LG": m_lg, "M_LGT": m_lgt})
        first_block.close()
        own.pop().close()
        own.append(ctx.enter_context(ExitStack()))

        ones = sb("ones", [P, L])
        prob = sb("prob", [P, L])
        prob_top = sb("prob_top", [P, L], BF16)
        rmax = sb("rmax", [P, 1])
        gmax = sb("gmax", [1, E])
        nrow = sb("nrow", [1, P])
        nmx = sb("nmx", [P, 1])
        zpart = sb("zpart", [P, 1])
        zrow = sb("zrow", [P, E])
        cur = sb("cur", [P, 1], I32)
        base = sb("base", [P, 3], I32)
        cand = sb("cand", [P, 3], I32)
        count = sb("count", [P, 3])
        passed = sb("passed", [P, 3])
        digit = sb("digit", [P, 1])
        digit_i = sb("digit_i", [P, 1], I32)
        need = sb("need", [P, 1])
        above = sb("above", [P, L])
        flags_b = sb("flags_b", [P, 3, L], BF16)
        flags = sb("flags", [P, 3, L])
        ties = sb("ties", [P, L])
        scan = sb("scan", [P, L])
        chosen = sb("chosen", [P, L])
        place = sb("place", [P, L])
        placeT = sb("placeT", [P, L], I32)
        hi_i = sb("hi_i", [P, L], I32)
        lo_i = sb("lo_i", [P, L], I32)
        hi_b = sb("hi_b", [P, L], BF16)
        lo_b = sb("lo_b", [P, L], BF16)
        col_b = sb("col_b", [P, L], BF16)
        CB = NC * B
        hot_hi = sb("hot_hi", [P, E, HI, CB], BF16)
        hot_lo = sb("hot_lo", [P, E, LO, CB], BF16)
        hot_tok = sb("hot_tok", [P, E, 2, LO, CB], BF16)
        idx_low = sb("idx_low", [P, E // 2, LO])

        sel_st = sem("sel_st")
        sel_pe = sem("sel_pe")
        sel_act = sem("sel_act")
        cand_ok = sem("cand_ok")
        sums_ok = sem("sums_ok")
        ones_ok = sem("ones_ok")
        col_ok = sem("col_ok")
        placeT_ps = sem("placeT_ps")
        hot_ok = sem("hot_ok")
        hot_p_ok = sem("hot_p_ok")
        idx_ps = sem("idx_ps")
        idx_ok = sem("idx_ok")

        STEP_TIES = 8 + 1 + 5 * (SEARCH_BITS // 2) - 2 + 2
        STEP_RANK = STEP_TIES + 5

        second_block = ExitStack()
        block = second_block.enter_context(nc.Block())

        @block.sync
        def _(sp):
            sp.wait_ge(h2_out, 16 * B)
            sp.wait_ge(row_out, 16 * B)

        @block.gpsimd
        def _(pool):
            nc.gpsimd.memset(ones[:, :], 1.0).then_inc(ones_ok, 1)
            nc.gpsimd.memset(cur[:, :], 0).then_inc(ones_ok, 1)

        @block.scalar
        def _(act):
            act.wait_ge(sel_in, N_SEL + 16)
            nc.scalar.copy(col_b[:, :], tok_col[:, :]).then_inc(col_ok, 1)
            act.wait_ge(sel_st, 5)
            nc.scalar.activation(prob[:, :], lgs[:, :], ACT.Exp, bias=nmx[:, :],
                                 accum_out=zpart[:, :]).then_inc(sel_act, 1)
            act.wait_ge(hot_ok, LO)
            for h in range(2):
                es = slice(h * E // 2, (h + 1) * E // 2)
                nc.scalar.mul(hot_tok[:, es, 0, :, :].rearrange("p e l n -> p e (l n)"),
                              hot_lo[:, es, :, :].rearrange("p e l n -> p e (l n)"),
                              tok_row[:, 0:1]).then_inc(hot_p_ok, 1)

        @block.vector
        def _(dve):
            steps = [0]

            def step(instruction):
                instruction.then_inc(sel_st, 1)
                steps[0] += 1
                dve.wait_ge(sel_st, steps[0])

            dve.wait_ge(sel_in, N_SEL + 16)
            step(nc.vector.tensor_reduce(rmax[:, :], lgs[:, :], AX.X, ALU.max))
            dve.wait_ge(sel_pe, 1)
            step(nc.vector.tensor_reduce(
                gmax[:, :], m_ps[0][0:1, 0:P].rearrange("p (b e) -> p e b", e=E), AX.X, ALU.max))
            step(nc.vector.tensor_scalar(
                nrow[:, :].rearrange("p (b e) -> p b e", e=E),
                gmax[:, :].rearrange("p (a e) -> p a e", a=1).to_broadcast([1, B, E]), -1.0, None,
                ALU.mult))
            dve.wait_ge(sel_pe, 2)
            nc.vector.tensor_copy(nmx8[:, :], m_ps[1][:, 8:8 + E]).then_inc(sel_st, 1)
            steps[0] += 1
            step(nc.vector.tensor_copy(nmx[:, :], m_ps[1][:, 0:1]))
            dve.wait_ge(sel_act, 1)
            step(nc.vector.tensor_scalar(zrow[:, :], expert[:, :], zpart[:, 0:1], None, ALU.mult))
            step(nc.vector.tensor_copy(prob_top[:, :], prob[:, :].bitcast(BF16)
                                       .rearrange("p (n h) -> p n h", h=2)[:, :, 1]))
            dve.wait_ge(sel_pe, 3)
            step(nc.vector.reciprocal(rz8[:, :], m_ps[0][:, 16:16 + E]))

            dve.wait_ge(ones_ok, 2)
            n_steps = SEARCH_BITS // 2
            step(nc.vector.tensor_copy(cand[:, :], two_bits[:, 0:3]))
            for i in range(n_steps):
                shift = SEARCH_BITS - 2 * i - 2
                x, each = (prob_top, flags_b) if shift >= 16 else (prob, flags)
                for k in range(3):
                    nc.vector.tensor_scalar(each[:, k, :], x[:, :], cand[:, k:k + 1].bitcast(F32),
                                            None, ALU.is_ge, ALU.add,
                                            accum_out=count[:, k:k + 1]).then_inc(cand_ok, 1)
                if i + 1 < n_steps:
                    nc.vector.tensor_tensor(
                        base[:, :], two_bits[:, 3 * i + 3:3 * i + 6],
                        cur[:, :].to_broadcast([P, 3]), ALU.bitwise_or).then_inc(sel_st, 1)
                    steps[0] += 1
                dve.wait_ge(sums_ok, i + 1)
                step(nc.vector.tensor_scalar(passed[:, :], m_ps[0][:, 0:3], float(CAP), None,
                                             ALU.is_ge, ALU.add, accum_out=digit[:, :]))
                step(nc.vector.tensor_scalar(digit_i[:, :], digit[:, :], float(1 << shift), None,
                                             ALU.mult))
                if i + 1 < n_steps:
                    nc.vector.tensor_tensor(
                        cand[:, :], base[:, :], digit_i[:, :].to_broadcast([P, 3]),
                        ALU.bitwise_or).then_inc(sel_st, 1)
                    steps[0] += 1
                step(nc.vector.tensor_tensor(cur[:, :], cur[:, :], digit_i[:, :],
                                             ALU.bitwise_or))
            thr = cur[:, :].bitcast(F32)
            nc.vector.tensor_scalar(above[:, :], prob[:, :], thr, None, ALU.is_gt, ALU.add,
                                    accum_out=count[:, 0:1]).then_inc(cand_ok, 1)
            step(nc.vector.tensor_scalar(ties[:, :], prob[:, :], thr, None, ALU.is_equal))
            step(nc.vector.tensor_tensor_scan(scan[:, :], ones[:, :], ties[:, :], 0.0, ALU.mult,
                                              ALU.add))
            assert steps[0] == STEP_TIES
            dve.wait_ge(sel_pe, 4)
            step(nc.vector.tensor_scalar(need[:, :], m_ps[1][:, 32:33], -1.0, float(CAP), ALU.mult,
                                         ALU.add))
            step(nc.vector.tensor_tensor(need[:, :], need[:, :], m_ps[1][:, 33:34], ALU.subtract))
            step(nc.vector.scalar_tensor_tensor(out=chosen[:, :], in0=scan[:, :],
                                                scalar=need[:, :], in1=ties[:, :], op0=ALU.is_le,
                                                op1=ALU.mult))
            step(nc.vector.tensor_tensor(chosen[:, :], chosen[:, :], above[:, :], ALU.add))
            step(nc.vector.tensor_tensor_scan(scan[:, :], ones[:, :], chosen[:, :], 0.0, ALU.mult,
                                              ALU.add))
            assert steps[0] == STEP_RANK
            dve.wait_ge(sel_pe, 5)
            step(nc.vector.tensor_copy(need[:, :], m_ps[0][:, 34:35]))
            step(nc.vector.scalar_tensor_tensor(out=place[:, :], in0=scan[:, :], scalar=need[:, :],
                                                in1=chosen[:, :], op0=ALU.add, op1=ALU.mult))
            dve.wait_ge(placeT_ps, 1)
            step(nc.vector.tensor_scalar(placeT[:, :], m_ps[1][:, :], -1.0, None, ALU.add))
            nc.vector.tensor_scalar(lo_i[:, :], placeT[:, :], LO - 1, None, ALU.bitwise_and)\
                .then_inc(sel_st, 1)
            steps[0] += 1
            step(nc.vector.tensor_scalar(hi_i[:, :], placeT[:, :], LO.bit_length() - 1, None,
                                         ALU.arith_shift_right))
            for dst, src in ((lo_b, lo_i), (hi_b, hi_i)):
                nc.vector.tensor_copy(dst[:, :].rearrange("p (e n) -> p e n", e=E),
                                      src[:, :].rearrange("p (n e) -> p e n", e=E))\
                    .then_inc(sel_st, 1)
                steps[0] += 1
            dve.wait_ge(sel_st, steps[0])
            lo_e = lo_b[:, :].rearrange("p (e n) -> p e n", e=E)
            hi_e = hi_b[:, :].rearrange("p (e n) -> p e n", e=E)
            for n in range(LO):
                nc.vector.tensor_scalar(hot_lo[:, :, n, :], lo_e, float(n), None,
                                        ALU.is_equal).then_inc(hot_ok, 1)
            dve.wait_ge(col_ok, 1)
            dve.wait_ge(hot_ok, LO)
            for e in range(E):
                nc.vector.tensor_tensor(
                    hot_tok[:, e, 1, :, :], hot_lo[:, e, :, :],
                    col_b[:, e * CB:(e + 1) * CB].rearrange("p (a n) -> p a n", a=1)
                    .to_broadcast([P, LO, CB]), ALU.mult).then_inc(hot_ok, 1)
            for n in range(HI):
                nc.vector.tensor_scalar(hot_hi[:, :, n, :], hi_e, float(n), None,
                                        ALU.is_equal).then_inc(hot_ok, 1)
            dve.wait_ge(idx_ps, 1)
            ps = s_ps[0][:, 0, 0:E // 2 * 4 * LO].rearrange("p (g h t l) -> p g h t l", h=2, t=2,
                                                            l=LO)
            tok = idx[:, :, :, :].rearrange("p (g h) u j -> p g h (u j)", h=2)
            for h in range(2):
                r = slice(h * HI, (h + 1) * HI)
                nc.vector.tensor_copy(idx_low[r, :, :], ps[r, :, h, 0, :]).then_inc(idx_ok, 1)
            dve.wait_ge(idx_ok, 2)
            for h in range(2):
                r = slice(h * HI, (h + 1) * HI)
                for half in range(2):
                    ls = slice(half * LO // 2, (half + 1) * LO // 2)
                    nc.vector.scalar_tensor_tensor(
                        out=tok[half * HI:(half + 1) * HI, :, h, :], in0=ps[r, :, h, 1, ls],
                        scalar=float(P), in1=idx_low[r, :, ls], op0=ALU.mult, op1=ALU.add)\
                        .then_inc(idx_ok, 1)

        @block.tensor
        def _(pe):
            pe.wait_ge(sel_in, N_SEL + 16)
            pe.wait_ge(ones_ok, 2)
            pe.wait_ge(sel_st, 1)
            nc.tensor.matmul(m_ps[0][0:1, 0:P], rmax[:, :], ident[:, :], start=True, stop=True)\
                .then_inc(sel_pe, 1)
            pe.wait_ge(sel_st, 3)
            nc.tensor.matmul(m_ps[1][:, 0:1], nrow[:, :], ones[0:1, 0:1], start=True, stop=True)
            nc.tensor.matmul(m_ps[1][:, 8:8 + E], ones[0:1, 0:P], nrow[:, 0:E],
                             start=True, stop=True).then_inc(sel_pe, 1)
            pe.wait_ge(sel_st, 6)
            nc.tensor.matmul(m_ps[0][:, 16:16 + E], ones[:, 0:P], zrow[:, :],
                             start=True, stop=True).then_inc(sel_pe, 1)
            for i in range(SEARCH_BITS // 2):
                pe.wait_ge(cand_ok, 3 * i + 3)
                nc.tensor.matmul(m_ps[0][:, 0:3], group[:, :], count[:, :], start=True, stop=True)\
                    .then_inc(sums_ok, 1)
            pe.wait_ge(cand_ok, 3 * (SEARCH_BITS // 2) + 1)
            pe.wait_ge(sel_st, STEP_TIES)
            nc.tensor.matmul(m_ps[1][:, 32:33], group[:, :], count[:, 0:1], start=True, stop=True)
            nc.tensor.matmul(m_ps[1][:, 33:34], before[:, :], scan[:, L - 1:L],
                             start=True, stop=True).then_inc(sel_pe, 1)
            pe.wait_ge(sel_st, STEP_RANK)
            nc.tensor.matmul(m_ps[0][:, 34:35], before[:, :], scan[:, L - 1:L],
                             start=True, stop=True).then_inc(sel_pe, 1)
            pe.wait_ge(sel_st, STEP_RANK + 2)
            for c in range(NC):
                last = nc.tensor.transpose(m_ps[1][:, c * P:(c + 1) * P],
                                           place[:, c * P:(c + 1) * P], ident[:, :])
            last.then_inc(placeT_ps, 1)
            pe.wait_ge(hot_ok, LO + E + HI)
            pe.wait_ge(hot_p_ok, 2)
            for g in range(E // 2):
                for at in range(CB):
                    last = nc.tensor.matmul(
                        s_ps[0][:, 0, g * 4 * LO:(g + 1) * 4 * LO],
                        hot_hi[:, 2 * g:2 * g + 2, :, at].rearrange("p e n -> p (e n)"),
                        hot_tok[:, 2 * g:2 * g + 2, :, :, at].rearrange("p e t l -> p (e t l)"),
                        start=at == 0, stop=at == CB - 1)
            last.then_inc(idx_ps, 1)

        second_block.close()

        own.pop().close()
        own.append(ctx)
        TILES = E * NT
        g_idx = sb("g_idx", [P, NT, NC], I32)
        s_idx = [sb(f"s_idx{u}", [P, NC], I32) for u in range(NT)]
        g_sb = sb("g_sb", [P, NT, NC, TW])
        gT = [sb(f"gT{u}", [P, L]) for u in range(NT)]
        hT = [sb(f"hT{u}", [P, NF, L]) for u in range(NT)]
        wt = [sb(f"wt{s}", [P, NT, NC]) for s in range(2)]
        y = [sb(f"y{u}", [P, NC, DM]) for u in range(NT)]

        g_idx_ok = sem("g_idx_ok")
        s_idx_ok = sem("s_idx_ok")
        g_in = [sem(f"g_in{u}") for u in range(NT)]
        gT_ps = sem("gT_ps")
        gT_ok = sem("gT_ok")
        f_full = sem("f_full")
        hT_ok = sem("hT_ok")
        o_full = sem("o_full")
        we_ok = sem("we_ok")
        wz_ok = sem("wz_ok")
        y_st = sem("y_st")
        y_ok = sem("y_ok")
        y_out = [sem(f"y_out{u}") for u in range(NT)]
        y_done = sem("y_done")
        Y_ST, Y_DONE = 1, 1

        third_block = ExitStack()
        block = third_block.enter_context(nc.Block())

        out_rows = out.rearrange("b l n -> (b l) n")

        def run_experts(eng, body):
            body(0, 0)
            with eng.Fori(0, E // 2 - 2) as i:
                body(i * 2 + 1, 1)
                body(i * 2 + 2, 0)
            body(E - 3, 1)
            body(E - 2, 0)
            body(E - 1, 1)

        @block.sync
        def _(sp):
            def load(e, s):
                sp.wait_ge(y_st, (e - 1) * NT + Y_ST)
                sp.sem_inc(sp_waits, 1)
                load_expert(sp, e, s)

            with sp.Fori(1, E // 2) as i:
                load(i * 2, 0)
                load(i * 2 + 1, 1)
            for u in range(NT):
                sp.wait_ge(y_out[u], E * NC * 16)

        @block.gpsimd
        def _(pool):
            pool.sem_inc(y_done, Y_DONE)

            def gather(u):
                for j in range(NC):
                    nc.gpsimd.indirect_dma_start(
                        out=g_sb[:, u, j, :], out_offset=None, in_=tab_d[:, :],
                        in_offset=bass.IndirectOffsetOnAxis(
                            ap=g_idx[:, u, j:j + 1], axis=0)).then_inc(g_in[u], 16)

            def scatter(u):
                for j in range(NC):
                    nc.gpsimd.indirect_dma_start(
                        out=out_rows, out_offset=bass.IndirectOffsetOnAxis(
                            ap=s_idx[u][:, j:j + 1], axis=0),
                        in_=y[u][:, j, :], in_offset=None, compute_op=ALU.add)\
                        .then_inc(y_out[u], 16)

            def own_wait():
                pool.sem_inc(pool_waits, 1)

            def body(e, s):
                first = isinstance(e, int) and e == 0
                last = isinstance(e, int) and e == E - 1
                if not last:
                    pool.wait_ge(gT_ps, (e + 1) * NT)
                    pool.wait_ge(we_ok, e + 1)
                    own_wait()
                    gather(1)
                if not first:
                    pool.wait_ge(y_ok, e * NT)
                    pool.wait_ge(s_idx_ok, e * NT)
                    own_wait()
                    scatter(1)
                if not (last or isinstance(e, int) and e == E - 2):
                    pool.wait_ge(gT_ps, (e + 1) * NT + 1)
                    pool.wait_ge(we_ok, e + 2)
                    pool.wait_ge(g_idx_ok, e + 3)
                    own_wait()
                    gather(0)
                if not first:
                    for u in range(NT):
                        pool.wait_ge(y_out[u], e * NC * 16)
                    pool.sem_inc(y_done, 1)
                pool.wait_ge(y_ok, e * NT + 1)
                pool.wait_ge(s_idx_ok, e * NT + 1)
                own_wait()
                scatter(0)

            pool.wait_ge(g_idx_ok, 1)
            gather(0)
            gather(1)
            pool.wait_ge(gT_ps, 1)
            pool.wait_ge(we_ok, 1)
            pool.wait_ge(g_idx_ok, 2)
            gather(0)
            run_experts(pool, body)
            pool.wait_ge(y_ok, TILES)
            pool.wait_ge(s_idx_ok, TILES)
            scatter(1)

        @block.scalar
        def _(act):
            def weights(e, s):
                if not (isinstance(e, int) and e < 2):
                    act.wait_ge(y_ok, (e - 1) * NT)
                for u in range(NT):
                    act.wait_ge(g_in[u], (e + 1) * NC * 16)
                nc.scalar.activation(
                    wt[s][:, :, :], g_sb[:, :, :, bass.ds(e + DM, 1)]
                    .rearrange("p u c a -> p u (c a)"), ACT.Exp, bias=nmx8[:, bass.ds(e, 1)])\
                    .then_inc(we_ok, 1)

            def indices(e):
                if isinstance(e, int) and e == 0:
                    act.wait_ge(idx_ok, 6)
                nc.scalar.copy(g_idx[:, :, :], idx[:, bass.ds(e, 1), :, :]
                               .rearrange("p e u j -> p (e u) j")).then_inc(g_idx_ok, 1)

            def body(e, s):
                for u in range(NT):
                    for f in range(NF):
                        act.wait_ge(f_full, (e * NT + u) * NF + f + 1)
                        nc.scalar.activation(hT[u][:, f, :], s_ps[f // 2][:, f % 2, :],
                                             ACT.Gelu, bias=b1[s][:, f:f + 1])\
                            .then_inc(hT_ok, 1)
                if not (isinstance(e, int) and e == E - 1):
                    weights(e + 1, 1 - s)
                if not (isinstance(e, int) and e >= E - 2):
                    indices(e + 2)

            indices(0)
            weights(0, 0)
            indices(1)
            run_experts(act, body)

        @block.vector
        def _(dve):
            dve.sem_inc(y_st, Y_ST)

            def copy_gT(n, u):
                dve.wait_ge(gT_ps, n + 1)
                nc.vector.tensor_copy(gT[u][:, :], m_ps[u][:, :]).then_inc(gT_ok, 1)

            def result(n, e, u, s):
                nc.vector.tensor_copy(s_idx[u][:, :], idx[:, bass.ds(e, 1), u, :]
                                      .rearrange("p e j -> p (e j)")).then_inc(s_idx_ok, 1)
                dve.wait_ge(o_full, n + 1)
                nc.vector.tensor_tensor(
                    y[u][:, :, :],
                    t_ps[u][:, :].rearrange("p (c n) -> p c n", n=DM),
                    b2[s][:, :].rearrange("p (a n) -> p a n", a=1)
                    .to_broadcast([P, NC, DM]), ALU.add).then_inc(y_st, 1)
                dve.wait_ge(y_st, n + 1 + Y_ST)
                nc.vector.tensor_tensor(
                    y[u][:, :, :], y[u][:, :, :],
                    wt[s][:, u, :].rearrange("p (c a) -> p c a", a=1)
                    .to_broadcast([P, NC, DM]), ALU.mult).then_inc(y_ok, 1)

            def body(e, s):
                first = isinstance(e, int) and e == 0
                last = isinstance(e, int) and e == E - 1
                copy_gT(e * NT + 1, 1)
                if not first:
                    dve.wait_ge(y_done, e - 1 + Y_DONE)
                    result(e * NT - 1, e - 1, 1, 1 - s)
                dve.wait_ge(we_ok, e + 1)
                nc.vector.tensor_scalar(wt[s][:, :, :], wt[s][:, :, :], rz8[:, bass.ds(e, 1)],
                                        None, ALU.mult).then_inc(wz_ok, 1)
                if not last:
                    copy_gT(e * NT + 2, 0)
                if not first:
                    dve.wait_ge(y_out[0], e * NC * 16)
                dve.wait_ge(wz_ok, e + 1)
                result(e * NT, e, 0, s)

            copy_gT(0, 0)
            run_experts(dve, body)
            dve.wait_ge(y_out[1], (E - 1) * NC * 16)
            result(TILES - 1, E - 1, 1, 1)

        @block.tensor
        def _(pe):
            def turn(e, u):
                pe.wait_ge(g_in[u], (e + 1) * NC * 16)
                for j in range(NC):
                    last = nc.tensor.transpose(m_ps[u][:, j * P:(j + 1) * P],
                                               g_sb[:, u, j, 0:DM], ident[:, :])
                last.then_inc(gT_ps, 1)

            def hidden(e, s, u):
                n = e * NT + u
                pe.wait_ge(gT_ok, n + 1)
                for f in range(NF):
                    if not (isinstance(n, int) and n == 0):
                        pe.wait_ge(hT_ok, (n - 1) * NF + f + 1)
                    nc.tensor.matmul(s_ps[f // 2][:, f % 2, :], w1[s][:, f * P:(f + 1) * P],
                                     gT[u][:, :], start=True, stop=True).then_inc(f_full, 1)

            def output(n, s, u):
                pe.wait_ge(hT_ok, n * NF + NF)
                if not (isinstance(n, int) and n < 2):
                    pe.wait_ge(y_st, n - 1 + Y_ST)
                for j in range(NC):
                    for f in range(NF):
                        last = nc.tensor.matmul(
                            t_ps[u][:, j * P:(j + 1) * P],
                            hT[u][:, f, j * P:(j + 1) * P], w2[s][:, f, :],
                            start=f == 0, stop=f == NF - 1)
                last.then_inc(o_full, 1)

            def body(e, s):
                first = isinstance(e, int) and e == 0
                last = isinstance(e, int) and e == E - 1
                if isinstance(e, int):
                    pe.wait_ge(w_in_s[s], (e // 2 + 1) * 4 * 16)
                else:
                    pe.wait_ge(w_in_s[s], (e - s + 2) * 2 * 16)
                hidden(e, s, 0)
                turn(e, 1)
                if not first:
                    output(e * NT - 1, 1 - s, 1)
                hidden(e, s, 1)
                if not last:
                    turn(e + 1, 0)
                output(e * NT, s, 0)

            turn(0, 0)
            run_experts(pe, body)
            output(TILES - 1, 1, 1)

        third_block.close()


def layout(i):
    g = {k: np.ascontiguousarray(np.asarray(v)) for k, v in i.items()}
    w = {n: g[f"L0_tok_w{n}"] for n in range(1, 13)}
    ecg, pcg = 0, 1
    q = [(4, ecg), (10, pcg), (1, ecg), (7, pcg)]
    k = [(5, pcg), (11, ecg), (2, ecg), (8, pcg)]
    v = [(6, pcg), (12, ecg), (3, ecg), (9, pcg)]
    w_stack = np.zeros((4, DM, P), np.float32)
    w_v = np.zeros((DM, NA * C), np.float32)
    for a in range(NA):
        for r in SLOT_ROW:
            at = 64 * (a % 2) + r
            w_stack[a // 2, q[a][1]::2, at:at + D] = w[q[a][0]]
            w_stack[2 + a // 2, k[a][1]::2, at:at + D] = w[k[a][0]]
        w_v[v[a][1]::2, a * C:(a + 1) * C] = w[v[a][0]]
    w_r = np.zeros((DM, ROWS), np.float32)
    w_r[:, :E] = g["L0_ffn_Wr"]
    d = {"x": g["x"].reshape(B, L, DM).transpose(0, 2, 1), "w_stack": w_stack, "w_v": w_v,
         "alpha": g["L0_tok_alpha"], "gamma": g["L0_tok_gamma"],
         "w_in": np.concatenate([g["L0_attn_We1"], g["L0_attn_Wk1"]], 1),
         "b_in": np.concatenate([g["L0_attn_be1"], g["L0_attn_bk1"]]),
         "w_kq": g["L0_attn_Wk2"], "b_kq": g["L0_attn_bk2"],
         "w_e2": g["L0_attn_We2"], "b_e2": g["L0_attn_be2"], "w_r": w_r,
         "w1": g["L0_ffn_W1"], "b1": g["L0_ffn_b1"], "w2": g["L0_ffn_W2"], "b2": g["L0_ffn_b2"]}
    d.update(constants())
    return {n: np.ascontiguousarray(a) for n, a in d.items()}


def kernel(**inputs):
    import concourse.bacc as bacc
    from concourse.bass_utils import run_bass_kernel_spmd

    arrays = layout(inputs)
    nc = bacc.Bacc("TRN2", target_bir_lowering=False, num_devices=1)
    aps = {n: nc.dram_tensor("in_" + n, a.shape, mybir.dt.from_np(a.dtype), kind="ExternalInput").ap()
           for n, a in arrays.items()}
    out = nc.dram_tensor("out", (B, L, DM), F32, kind="ExternalOutput").ap()
    build(nc, aps, out)
    r = run_bass_kernel_spmd(nc, [{"in_" + n: a for n, a in arrays.items()}], core_ids=[0])
    return r.results[0]["out"]
```
